# Optimizing a Trainium2 kernel written in Bass

```python
import numpy as np
import jax
import jax.numpy as jnp

def _softmax(x, axis=-1):
    return jax.nn.softmax(x, axis=axis)

def _gelu(x):
    return jax.nn.gelu(x, approximate=True)

def _silu(x):
    return jax.nn.silu(x)

def _sigmoid(x):
    return jax.nn.sigmoid(x)

def _layernorm(x, axis=-1, eps=1e-05):
    m = jnp.mean(x, axis=axis, keepdims=True)
    v = jnp.var(x, axis=axis, keepdims=True)
    return (x - m) / jnp.sqrt(v + eps)

def _scatter_add(tgt, idx, src, axis=0):
    return tgt.at[idx].add(src)

def _segment_sum(src, seg, n):
    return jax.ops.segment_sum(src, seg, n)
kernel_name = 'mk_cond_seq_d2_seqx_r4_0ddc69'

def setup_inputs(seed: int=0):
    np.random.seed(seed)
    _w = jnp.asarray

    def _rec_inputs():
        import jax
        import jax.numpy as jnp
        _rk = jax.random.key(seed)
        x = -0.0002928 + 1 * jax.random.normal(jax.random.fold_in(_rk, 1), (4, 512, 256), jnp.float32)
        _lenS = 512 - jax.random.randint(jax.random.fold_in(_rk, 7), (4,), 0, max(1, 512 // 4) + 1, jnp.int32)
        _lenS2 = 512 - jax.random.randint(jax.random.fold_in(_rk, 8), (4,), 0, max(1, 512 // 4) + 1, jnp.int32)
        cond_1024 = 0.000887014 + 1.03683 * jax.random.normal(jax.random.fold_in(_rk, 11), (4, 256), jnp.float32)
        return (x, cond_1024)
    x, cond_1024 = _rec_inputs()

    def _L0_cond_setup():
        import math
        import jax, jax.numpy as jnp
        import numpy as np
        D_MODEL = 256
        N_HEADS = 16
        FFN_DIM = 1024
        EPS = 1e-05

        def _layernorm(x, w, b):
            mu = jnp.mean(x, axis=-1, keepdims=True)
            var = jnp.var(x, axis=-1, keepdims=True)
            return (x - mu) * jax.lax.rsqrt(var + EPS) * w + b

        def _modulate(x, shift, scale):
            return x * (1.0 + scale[:, None, :]) + shift[:, None, :]
        key = jax.random.key(seed)
        ks = jax.random.split(key, 16)
        B, S, D, F = (2, 512, D_MODEL, FFN_DIM)
        s = 0.02
        return {'x': jax.random.normal(ks[0], (B, S, D), jnp.float32), 't_emb': jax.random.normal(ks[1], (B, D), jnp.float32), 'ln1_w': jnp.ones((D,), jnp.float32), 'ln1_b': jnp.zeros((D,), jnp.float32), 'ln2_w': jnp.ones((D,), jnp.float32), 'ln2_b': jnp.zeros((D,), jnp.float32), 'wq': jax.random.normal(ks[2], (D, D), jnp.float32) * s, 'bq': jnp.zeros((D,), jnp.float32), 'wk': jax.random.normal(ks[3], (D, D), jnp.float32) * s, 'bk': jnp.zeros((D,), jnp.float32), 'wv': jax.random.normal(ks[4], (D, D), jnp.float32) * s, 'bv': jnp.zeros((D,), jnp.float32), 'wo': jax.random.normal(ks[5], (D, D), jnp.float32) * s, 'bo': jnp.zeros((D,), jnp.float32), 'wt_attn': jax.random.normal(ks[6], (D, 2 * D), jnp.float32) * s, 'bt_attn': jnp.zeros((2 * D,), jnp.float32), 'wt_ffn': jax.random.normal(ks[7], (D, 2 * D), jnp.float32) * s, 'bt_ffn': jnp.zeros((2 * D,), jnp.float32), 'w1': jax.random.normal(ks[8], (D, F), jnp.float32) * s, 'b1': jnp.zeros((F,), jnp.float32), 'w2': jax.random.normal(ks[9], (F, D), jnp.float32) * s, 'b2': jnp.zeros((D,), jnp.float32)}
    _L0_cond_all = _L0_cond_setup()
    _L0_cond_in = {k: v for k, v in _L0_cond_all.items() if k in ('ln1_w', 'ln1_b', 'ln2_w', 'ln2_b', 'wq', 'bq', 'wk', 'bk', 'wv', 'bv', 'wo', 'bo', 'wt_attn', 'bt_attn', 'wt_ffn', 'bt_ffn', 'w1', 'b1', 'w2', 'b2')}
    del _L0_cond_all

    def _L1_cond_setup():
        import jax, jax.numpy as jnp
        import numpy as np
        B, L, D, P = (8, 512, 256, 64)

        def _ln(x):
            m = x.mean(-1, keepdims=True)
            v = x.var(-1, keepdims=True)
            return (x - m) * jax.lax.rsqrt(v + 1e-05)

        def _s5(u, Lam_re, Lam_im, B_re, B_im, C_re, C_im, D_diag, log_step):
            Lam = Lam_re + 1j * Lam_im
            dt = jnp.exp(log_step)
            Lam_bar = jnp.exp(Lam * dt)
            Bc = B_re + 1j * B_im
            B_bar = ((Lam_bar - 1.0) / Lam)[:, None] * Bc
            Bu = jnp.einsum('bld,pd->blp', u.astype(B_bar.dtype), B_bar)
            A = jnp.broadcast_to(Lam_bar, Bu.shape)

            def binop(e1, e2):
                a1, b1 = e1
                a2, b2 = e2
                return (a1 * a2, a2 * b1 + b2)
            _, xs = jax.lax.associative_scan(binop, (A, Bu), axis=1)
            Cc = C_re + 1j * C_im
            return 2.0 * jnp.einsum('blp,dp->bld', xs, Cc).real + D_diag * u
        key = jax.random.key(seed)
        ks = jax.random.split(key, 16)
        inp = {'y': jax.random.normal(ks[0], (B, L, D), jnp.float32), 't': jax.random.normal(ks[1], (B, D), jnp.float32), 'Wm': jax.random.normal(ks[2], (D, 6 * D), jnp.float32) * 0.02, 'bm': jax.random.normal(ks[3], (6 * D,), jnp.float32) * 0.02, 'Lam_re': -0.5 * jnp.ones((P,), jnp.float32), 'Lam_im': jnp.pi * jnp.arange(P, dtype=jnp.float32), 'B_re': jax.random.normal(ks[4], (P, D), jnp.float32) / np.sqrt(D), 'B_im': jax.random.normal(ks[5], (P, D), jnp.float32) / np.sqrt(D), 'C_re': jax.random.normal(ks[6], (D, P), jnp.float32) / np.sqrt(P), 'C_im': jax.random.normal(ks[7], (D, P), jnp.float32) / np.sqrt(P), 'D_diag': jax.random.normal(ks[8], (D,), jnp.float32), 'log_step': jax.random.uniform(ks[9], (P,), jnp.float32, np.log(0.001), np.log(0.1)), 'Wc': jax.random.normal(ks[10], (D, 2 * D), jnp.float32) * 0.02, 'bc': jax.random.normal(ks[11], (2 * D,), jnp.float32) * 0.02, 'W1': jax.random.normal(ks[12], (D, 4 * D), jnp.float32) / np.sqrt(D), 'b1': jnp.zeros((4 * D,), jnp.float32), 'W2': jax.random.normal(ks[13], (4 * D, D), jnp.float32) / np.sqrt(4 * D) * 0.1, 'b2': jnp.zeros((D,), jnp.float32)}
        return inp
    _L1_cond_all = _L1_cond_setup()
    _L1_cond_in = {k: v for k, v in _L1_cond_all.items() if k in ('Wm', 'bm', 'Lam_re', 'Lam_im', 'B_re', 'B_im', 'C_re', 'C_im', 'D_diag', 'log_step', 'Wc', 'bc', 'W1', 'b1', 'W2', 'b2')}
    del _L1_cond_all
    return {'x': x, 'cond_1024': cond_1024, 'L0_cond_ln1_w': _L0_cond_in['ln1_w'], 'L0_cond_ln1_b': _L0_cond_in['ln1_b'], 'L0_cond_ln2_w': _L0_cond_in['ln2_w'], 'L0_cond_ln2_b': _L0_cond_in['ln2_b'], 'L0_cond_wq': _L0_cond_in['wq'], 'L0_cond_bq': _L0_cond_in['bq'], 'L0_cond_wk': _L0_cond_in['wk'], 'L0_cond_bk': _L0_cond_in['bk'], 'L0_cond_wv': _L0_cond_in['wv'], 'L0_cond_bv': _L0_cond_in['bv'], 'L0_cond_wo': _L0_cond_in['wo'], 'L0_cond_bo': _L0_cond_in['bo'], 'L0_cond_wt_attn': _L0_cond_in['wt_attn'], 'L0_cond_bt_attn': _L0_cond_in['bt_attn'], 'L0_cond_wt_ffn': _L0_cond_in['wt_ffn'], 'L0_cond_bt_ffn': _L0_cond_in['bt_ffn'], 'L0_cond_w1': _L0_cond_in['w1'], 'L0_cond_b1': _L0_cond_in['b1'], 'L0_cond_w2': _L0_cond_in['w2'], 'L0_cond_b2': _L0_cond_in['b2'], 'L1_cond_Wm': _L1_cond_in['Wm'], 'L1_cond_bm': _L1_cond_in['bm'], 'L1_cond_Lam_re': _L1_cond_in['Lam_re'], 'L1_cond_Lam_im': _L1_cond_in['Lam_im'], 'L1_cond_B_re': _L1_cond_in['B_re'], 'L1_cond_B_im': _L1_cond_in['B_im'], 'L1_cond_C_re': _L1_cond_in['C_re'], 'L1_cond_C_im': _L1_cond_in['C_im'], 'L1_cond_D_diag': _L1_cond_in['D_diag'], 'L1_cond_log_step': _L1_cond_in['log_step'], 'L1_cond_Wc': _L1_cond_in['Wc'], 'L1_cond_bc': _L1_cond_in['bc'], 'L1_cond_W1': _L1_cond_in['W1'], 'L1_cond_b1': _L1_cond_in['b1'], 'L1_cond_W2': _L1_cond_in['W2'], 'L1_cond_b2': _L1_cond_in['b2']}

def reference(x, cond_1024, L0_cond_ln1_w, L0_cond_ln1_b, L0_cond_ln2_w, L0_cond_ln2_b, L0_cond_wq, L0_cond_bq, L0_cond_wk, L0_cond_bk, L0_cond_wv, L0_cond_bv, L0_cond_wo, L0_cond_bo, L0_cond_wt_attn, L0_cond_bt_attn, L0_cond_wt_ffn, L0_cond_bt_ffn, L0_cond_w1, L0_cond_b1, L0_cond_w2, L0_cond_b2, L1_cond_Wm, L1_cond_bm, L1_cond_Lam_re, L1_cond_Lam_im, L1_cond_B_re, L1_cond_B_im, L1_cond_C_re, L1_cond_C_im, L1_cond_D_diag, L1_cond_log_step, L1_cond_Wc, L1_cond_bc, L1_cond_W1, L1_cond_b1, L1_cond_W2, L1_cond_b2):
    import jax
    import jax.numpy as jnp

    def _L0_cond_ref(x, t_emb, ln1_w, ln1_b, ln2_w, ln2_b, wq, bq, wk, bk, wv, bv, wo, bo, wt_attn, bt_attn, wt_ffn, bt_ffn, w1, b1, w2, b2):
        import math
        import jax, jax.numpy as jnp
        import numpy as np
        D_MODEL = 256
        N_HEADS = 16
        FFN_DIM = 1024
        EPS = 1e-05

        def _layernorm(x, w, b):
            mu = jnp.mean(x, axis=-1, keepdims=True)
            var = jnp.var(x, axis=-1, keepdims=True)
            return (x - mu) * jax.lax.rsqrt(var + EPS) * w + b

        def _modulate(x, shift, scale):
            return x * (1.0 + scale[:, None, :]) + shift[:, None, :]
        B, S, D = x.shape
        H = N_HEADS
        hd = D // H
        residual = x
        xn = _layernorm(x, ln1_w, ln1_b)
        t_attn = t_emb @ wt_attn + bt_attn
        shift_a, scale_a = jnp.split(t_attn, 2, axis=-1)
        xn = _modulate(xn, shift_a, scale_a)
        q = (xn @ wq + bq).reshape(B, S, H, hd).transpose(0, 2, 1, 3)
        k = (xn @ wk + bk).reshape(B, S, H, hd).transpose(0, 2, 1, 3)
        v = (xn @ wv + bv).reshape(B, S, H, hd).transpose(0, 2, 1, 3)
        scores = jnp.einsum('bhqd,bhkd->bhqk', q, k) / math.sqrt(hd)
        attn = jax.nn.softmax(scores, axis=-1)
        out = jnp.einsum('bhqk,bhkd->bhqd', attn, v)
        out = out.transpose(0, 2, 1, 3).reshape(B, S, D)
        x = residual + (out @ wo + bo)
        residual = x
        xn = _layernorm(x, ln2_w, ln2_b)
        t_ffn = t_emb @ wt_ffn + bt_ffn
        shift_f, scale_f = jnp.split(t_ffn, 2, axis=-1)
        xn = _modulate(xn, shift_f, scale_f)
        h = jax.nn.gelu(xn @ w1 + b1, approximate=False)
        x = residual + (h @ w2 + b2)
        return x

    def _L1_cond_ref(y, t, Wm, bm, Lam_re, Lam_im, B_re, B_im, C_re, C_im, D_diag, log_step, Wc, bc, W1, b1, W2, b2):
        import jax, jax.numpy as jnp
        import numpy as np
        B, L, D, P = (8, 512, 256, 64)

        def _ln(x):
            m = x.mean(-1, keepdims=True)
            v = x.var(-1, keepdims=True)
            return (x - m) * jax.lax.rsqrt(v + 1e-05)

        def _s5(u, Lam_re, Lam_im, B_re, B_im, C_re, C_im, D_diag, log_step):
            Lam = Lam_re + 1j * Lam_im
            dt = jnp.exp(log_step)
            Lam_bar = jnp.exp(Lam * dt)
            Bc = B_re + 1j * B_im
            B_bar = ((Lam_bar - 1.0) / Lam)[:, None] * Bc
            Bu = jnp.einsum('bld,pd->blp', u.astype(B_bar.dtype), B_bar)
            A = jnp.broadcast_to(Lam_bar, Bu.shape)

            def binop(e1, e2):
                a1, b1 = e1
                a2, b2 = e2
                return (a1 * a2, a2 * b1 + b2)
            _, xs = jax.lax.associative_scan(binop, (A, Bu), axis=1)
            Cc = C_re + 1j * C_im
            return 2.0 * jnp.einsum('blp,dp->bld', xs, Cc).real + D_diag * u
        mod = t @ Wm + bm
        shift_a, scale_a, gate_a, shift_ff, scale_ff, gate_ff = jnp.split(mod, 6, axis=-1)
        y_mod = _ln(y) * (1 + scale_a[:, None]) + shift_a[:, None]
        a_y = _s5(y_mod, Lam_re, Lam_im, B_re, B_im, C_re, C_im, D_diag, log_step)
        y = y + gate_a[:, None] * a_y
        cond = t @ Wc + bc
        scale_c, shift_c = jnp.split(cond, 2, axis=-1)
        y_norm = _ln(y) * (1 + scale_c[:, None]) + shift_c[:, None]
        y_mod = y_norm * (1 + scale_ff[:, None]) + shift_ff[:, None]
        h = jax.nn.gelu(y_mod @ W1 + b1)
        ff_y = h @ W2 + b2
        return y + gate_ff[:, None] * ff_y
    x = _L0_cond_ref(x, cond_1024, L0_cond_ln1_w, L0_cond_ln1_b, L0_cond_ln2_w, L0_cond_ln2_b, L0_cond_wq, L0_cond_bq, L0_cond_wk, L0_cond_bk, L0_cond_wv, L0_cond_bv, L0_cond_wo, L0_cond_bo, L0_cond_wt_attn, L0_cond_bt_attn, L0_cond_wt_ffn, L0_cond_bt_ffn, L0_cond_w1, L0_cond_b1, L0_cond_w2, L0_cond_b2)
    x = _L1_cond_ref(x, cond_1024, L1_cond_Wm, L1_cond_bm, L1_cond_Lam_re, L1_cond_Lam_im, L1_cond_B_re, L1_cond_B_im, L1_cond_C_re, L1_cond_C_im, L1_cond_D_diag, L1_cond_log_step, L1_cond_Wc, L1_cond_bc, L1_cond_W1, L1_cond_b1, L1_cond_W2, L1_cond_b2)
    return x

_drawn_inputs = setup_inputs


def setup_inputs(seed=0):
    import zlib

    import numpy as np

    out = dict(_drawn_inputs(seed))
    spreads = {'L0_cond_ln1_w': (1.0, 0.6),
     'L0_cond_ln1_b': (0.0, 0.695),
     'L0_cond_ln2_w': (1.0, 0.6),
     'L0_cond_ln2_b': (0.0, 0.731),
     'L0_cond_bq': (0.0, 0.8),
     'L0_cond_bk': (0.0, 2.0),
     'L0_cond_bv': (0.0, 0.273),
     'L0_cond_bo': (0.0, 0.1),
     'L0_cond_bt_attn': (0.0, 0.751),
     'L0_cond_bt_ffn': (0.0, 0.49),
     'L0_cond_b1': (0.0, 0.1),
     'L0_cond_b2': (0.0, 0.1),
     'L1_cond_Lam_re': (-0.5, 0.6),
     'L1_cond_b1': (0.0, 2.0),
     'L1_cond_b2': (0.0, 0.268)}
    factors = {'L0_cond_wq': 8.0,
     'L0_cond_wk': 8.0,
     'L1_cond_Wc': 5.582,
     'L1_cond_bc': 34.051,
     'L1_cond_W1': 2.696}
    for name, (base, spread) in spreads.items():
        noise = np.random.default_rng([zlib.crc32(name.encode()), seed]).standard_normal(out[name].shape)
        drawn = base * np.exp(spread * noise) if base else spread * noise
        out[name] = jnp.asarray(drawn.astype(out[name].dtype))
    for name, factor in factors.items():
        out[name] = (out[name] * factor).astype(out[name].dtype)
    return out
```

```python
import math
from contextlib import ExitStack

import concourse.bass as bass
from concourse import mybir

F32 = mybir.dt.float32
F32R = mybir.dt.float32r
I32 = mybir.dt.int32
ALU = mybir.AluOpType
ACT = mybir.ActivationFunctionType
AX_X = mybir.AxisListType.X

P = 128
B, S, D = 4, 512, 256
H, HD = 16, 16
F = 1024
NS = 64
KT = D // P
TT = S // P
FT = F // P
EPS = 1e-5
QUADS = H // 4
SCALE = 1.0 / math.sqrt(HD)
ZERO_ROW, MAX_HI, MAX_LO = 64, 65, 66
P1_ROWS, P2_ROWS = 65, 67
LAG = 6
NMOD = 24

M_SHIFT0, M_SCALE0, M_SHIFT1, M_SCALE1 = 0, 2, 4, 6
M_SHIFT2, M_SCALE2, M_GATE_A, M_SHIFTF, M_SCALEF, M_GATE_F = 8, 10, 12, 14, 16, 18
M_SCALEC, M_SHIFTC = 20, 22

VEC_SIZES = [("ln1_w", 2), ("ln1_b", 2), ("ln2_w", 2), ("ln2_b", 2), ("bq", 2), ("bk", 2), ("bmod", NMOD),
             ("b1_0", FT), ("b1_1", FT), ("d_diag", 2), ("lam_re", 1), ("lam_im", 1), ("log_step", 1)]
VEC = {}
for _name, _n in VEC_SIZES:
    VEC[_name] = sum(VEC[k][1] for k in VEC), _n
NVEC = sum(n for _, n in VEC_SIZES)


MAG_COL = 31


def turns_of(kind):
    first, last, tail = kind == "first", kind == "last", kind == "tail"
    steps = {s: [] for s in range(16)}
    if first:
        steps[0] += [("V", 0, 0)]
        steps[1] += [("V", 0, 1), ("Q", 0, 1)]
        steps[2] += [("K", 0, 1)]
    else:
        steps[0] += [("MX", -1, 3)]
    if not (last or tail):
        steps[2] += [("LT", 1, 0)]
        steps[3] += [("LT", 1, 1)]
    if not first:
        steps[3] += [("OT", -1, 2)]
    if not tail:
        steps[4] += [("MX", 0, 0)]
    if not (last or tail):
        steps[5] += [("Q", 1, 0)]
        steps[6] += [("K", 1, 0)]
    if not first:
        steps[7] += [("OT", -1, 3)]
        steps[8] += [("OB", -1, 0)]
        steps[9] += [("OB", -1, 1)]
        steps[10] += [("WO", -1, 0)]
        steps[11] += [("WO", -1, 1)]
    if not tail:
        steps[8] += [("MX", 0, 1)]
        steps[11] += [("OT", 0, 0)]
        steps[12] += [("MX", 0, 2)]
        steps[15] += [("OT", 0, 1)]
    if not (last or tail):
        steps[9] += [("V", 1, 0)]
        steps[10] += [("V", 1, 1)]
        steps[13] += [("Q", 1, 1)]
        steps[14] += [("K", 1, 1)]
    return steps


def n_turns(kind):
    return sum(len(v) for v in turns_of(kind).values())


PRO_TURNS = 4
FIRST_TURNS, MID_TURNS, LAST_TURNS, TAIL_TURNS = (n_turns(k) for k in ("first", "middle", "last", "tail"))


def turn_base(b):
    if isinstance(b, int) and b == 0:
        return PRO_TURNS
    if isinstance(b, int) and b == B:
        return PRO_TURNS + FIRST_TURNS + (B - 2) * MID_TURNS + LAST_TURNS
    return b * MID_TURNS + (PRO_TURNS + FIRST_TURNS - MID_TURNS)


ALL_TURNS = turn_base(B) + TAIL_TURNS


def numbered(b, kind):
    out, n = {}, turn_base(b)
    for s, turns in turns_of(kind).items():
        out[s] = []
        for what, off, i in turns:
            out[s].append((n, what, b + off, i))
            n = n + 1
    return out


def positive(b):
    return not (isinstance(b, int) and b <= 0)


def cond_seq_kernel(nc, x, vecs, cond, wmod, bgate, wqkv, bv, wo, bo, w1_0, w2_0, b2_0,
                    b_st, b_sw, c_st, c_sw, w1_1, w2_1, b2_1, out):
    ctx = ExitStack()
    with ctx:
        def sb(name, shape, dt=F32):
            return ctx.enter_context(nc.sbuf_tensor(name, shape, dt))

        def sem(name):
            return ctx.enter_context(nc.semaphore(name))

        X = sb("X", [P, B * TT, D])
        STK = sb("STK", [P, 2 * H * S], F32R)
        PT = sb("PT", [P, TT * 4 * S])
        SRCQ = sb("SRCQ", [P, 2, 2, S], F32R)
        SRCK = sb("SRCK", [P, 2, 3, S], F32R)
        WQ = sb("WQ", [P, 3072], F32R)
        WRAW = sb("WRAW", [P, 2048])
        XNF = sb("XNF", [P, KT, S])
        XN = sb("XN", [P, 2, KT, S], F32R)
        XH = sb("XH", [P, TT, D])
        AO = sb("AO", [P, 6144])
        WO = sb("WO", [P, KT, D])
        VEC_SB = sb("VEC_SB", [P, NVEC])
        COND = sb("COND", [P, KT, B])
        IDENT = sb("IDENT", [P, P])
        BV = sb("BV", [P, D])
        BO = sb("BO", [P, D])
        GATE_A = sb("GATE_A", [P, B, D])
        GATE_F = sb("GATE_F", [P, B, D])
        MT = sb("MT", [P, NMOD, B])
        ONE_S = sb("ONE_S", [P, KT, B])
        AB = sb("AB", [P, 4, 2, KT, B])
        DG = sb("DG", [P, KT, B])
        STAT = sb("STAT", [P, TT, 6])
        MV = sb("MV", [P, TT, 2])
        VE = sb("VE", [P, TT])
        RSTD = sb("RSTD", [P, TT])
        MINUS_HALF = sb("MINUS_HALF", [P, TT])
        MX = sb("MX", [P, 2, 4, TT])
        NEGMX = sb("NEGMX", [16, QUADS, 2, P], F32R)
        RC = sb("RC", [P, 16])
        SC = sb("SC", [P, 32])

        QS = STK[0:P2_ROWS, 0:H * S].rearrange("p (h t) -> p h t", h=H)
        KS = STK[0:P2_ROWS, H * S:2 * H * S].rearrange("p (h t) -> p h t", h=H)
        PTV = PT[:, :].rearrange("p (k j t) -> p k j t", k=TT, j=4)
        WMOD = PT[:, 0:2 * NMOD * P].rearrange("p (k n) -> p k n", k=KT)
        WQV = WQ[:, :].rearrange("p (s k n) -> p s k n", s=2, k=KT)
        VS = AO[:, 0:1024].rearrange("p (t n) -> p t n", t=TT)
        VA = AO[:, 1024:3072].rearrange("p (o t h d) -> p o t h d", o=2, t=TT, h=8)
        OR = AO[:, 3072:4096].rearrange("p (s t) -> p s t", s=2)
        OTK = AO[:, 4096:5120].rearrange("p (t n) -> p t n", t=TT)
        OF = AO[:, 5120:6144].rearrange("p (k t) -> p k t", k=KT)
        MROW = AO[:, 4096:4864].rearrange("p (h n) -> p h n", h=2)
        BG = AO[:, 3072:3584].rearrange("p (g n) -> p g n", g=2)
        W1P = STK[:, 0:4096].rearrange("p (s k n) -> p s k n", s=2, k=KT)
        W2P = STK[:, 4096:8192].rearrange("p (s f n) -> p s f n", s=2, f=FT)
        HH = STK[:, 8192:12288].rearrange("p (f t) -> p f t", f=FT)
        HL = STK[:, 12288:16384].rearrange("p (f t) -> p f t", f=FT)
        CYP = STK[:, 8192:12288].rearrange("p (m s t) -> p m s t", m=4, s=2)
        W2RAW = PT[:, 0:2048]
        HF = PT[:, 2048:3072].rearrange("p (s t) -> p s t", s=2)
        TMP = PT[:, 3072:4096].rearrange("p (t n) -> p t n", t=TT)
        RAW1 = PT[:, 4096:6144]
        RAW2 = PT[:, 6144:8192]
        S5T = PT[:, 0:4096].rearrange("p (m t) -> p m t", m=8)
        TAB_C, TAB_S = AO[:, 0:512], AO[:, 512:1024]
        B_ST, B_SW, C_ST, C_SW = (AO[:, 1024 + 256 * i:1280 + 256 * i] for i in range(4))
        BB = AO[:, 2048:2560].rearrange("p (m n) -> p m n", m=2)
        WC = AO[:, 2560:3072].rearrange("p (m n) -> p m n", m=2)
        WGF = AO[:, 3072:3584].rearrange("p (m n) -> p m n", m=2)
        DGF = AO[:, 3584:3840].rearrange("p (k n) -> p k n", k=KT)
        B2_0, B2_1 = AO[:, 4096:4352], AO[:, 4352:4608]
        GB2 = AO[:, 4608:4864]
        BBT = AO[:, 5120:5632].rearrange("p (m n) -> p m n", m=4)
        WB = WQ[:, 0:1024].rearrange("p (s m n) -> p s m n", s=2, m=4)
        WG = WQ[:, 1024:2048].rearrange("p (s m n) -> p s m n", s=2, m=2)
        DGP = WQ[:, 2048:2560].rearrange("p (s k n) -> p s k n", s=2, k=KT)

        PS = [ctx.enter_context(nc.psum_tensor(f"bank{i}", [P, 512], F32)) for i in range(4, 8)]
        PS1 = ctx.enter_context(nc.psum_tensor("banks0_3", [P, 4, 512], F32))
        bank = [PS1[:, i, :] for i in range(4)] + [p[:, :] for p in PS]
        PV, MISC = bank[6], bank[7]

        def vec(name, i):
            at = VEC[name][0] + i
            return VEC_SB[:, at:at + 1]

        def vecs_of(name):
            at, n = VEC[name]
            return VEC_SB[:, at:at + n]

        def x_tile(b, tt):
            return X[:, bass.ds(b * TT + tt, 1), :].rearrange("p a n -> p (a n)")

        def x_pair(b, p):
            return X[:, bass.ds(b * TT + 2 * p, 2), :]

        def x_batch(b):
            return X[:, bass.ds(b * TT, TT), :]

        def ab(ln, which, k, b):
            return AB[:, ln, which, k, bass.ds(b, 1)]

        s_x = [sem(f"x_loaded{b}") for b in range(B)]
        s_small = sem("small_loaded")
        s_wq = sem("wqkv_loaded")
        s_wmod_a = sem("wmod_attn_loaded")
        s_wmod_b = sem("wmod_rest_loaded")
        s_rows = sem("rows_loaded")
        s_w1raw = sem("w1_raw_loaded")
        s_w2raw = sem("w2_raw_loaded")
        s_raw1 = sem("block1_raw_loaded")
        s_s5raw = sem("s5_raw_loaded")
        s_out = sem("out_stored")
        ident_ready = sem("ident_ready")
        const_ready = sem("const_ready")
        wq_hi, wq_lo = sem("wq_hi"), sem("wq_lo")
        mrow_mm, mrow_out, mt_mm, mt_ready = sem("mrow_mm"), sem("mrow_out"), sem("mt_mm"), sem("mt_ready")
        gate_mm, gate_ready = sem("gate_mm"), sem("gate_ready")
        ab_ready = sem("ab_ready")
        pool_chain = sem("pool_chain")
        ln_stats, ln_mv, ln_ve, ln_rstd, ln_xhat = (sem(n) for n in ("ln_stats", "ln_mv", "ln_ve", "ln_rstd", "ln_xhat"))
        xn_hi, xn_ready = sem("xn_hi"), sem("xn_ready")
        misc_full, misc_free = sem("misc_full"), sem("misc_free")
        src_hi, src_dup = sem("src_hi"), sem("src_dup")
        mx_hi = sem("mx_hi")
        stack_ready = [sem(f"stack_ready{h}") for h in range(H)]
        negmax_ready = [sem(f"negmax_ready{q}") for q in range(QUADS)]
        s1_full, s1_free = sem("s1_full"), sem("s1_free")
        s2_full, exp_done = sem("s2_full"), sem("exp_done")
        pv_done, pv_evac = sem("pv_done"), sem("pv_evac")
        va_ready = sem("va_ready")
        rc_ready = sem("rc_ready")
        x_bias = sem("x_bias")
        ffn = {}
        for ph in (1, 3):
            ffn[ph] = {n: sem(f"{n}_ffn{ph}") for n in
                       ("t_full", "xnf", "up_full", "h_hi", "h_lo", "down_ft", "down_full", "down_free",
                        "w1_hi", "w1_lo", "w2_hi", "w2_lo", "gated")}
        gb2_ready = sem("gb2_ready")
        waits_carried = sem("waits_carried")
        s5c = sem("s5_consts")
        s5 = {n: sem(f"{n}_s5") for n in
              ("t_full", "xnf", "bu_full", "t1", "t2", "rot", "scan", "cyf", "cy_hi", "cy_lo", "wgf", "wg_hi",
               "wg_lo", "out_full", "out_free", "bb_t", "bbt", "wb_hi", "wb_lo")}
        block = ctx.enter_context(nc.Block())

        LN_ATT, LN_FFN0, LN_S5, LN_FFN1 = 0, B, 2 * B, 3 * B

        def ln_stats_dve(dve, n, b):
            for tt in range(TT):
                op = nc.vector.bn_stats(STAT[:, tt, :], x_tile(b, tt))
            op.then_inc(ln_stats, 1)
            alone(dve, ln_stats, n + 1)
            for tt in range(TT):
                op = nc.vector.bn_aggr(MV[:, tt, :], STAT[:, tt, :])
            op.then_inc(ln_mv, 1)

        def ln_rstd_pool(pool, n):
            alone(pool, ln_mv, n + 1)
            nc.gpsimd.tensor_scalar(VE[:, :], MV[:, :, 1], EPS, None, ALU.add).then_inc(ln_ve, 1)
            pool.wait_ge(ln_ve, n + 1)
            nc.gpsimd.tensor_tensor(RSTD[:, :], VE[:, :], MINUS_HALF[:, :], ALU.pow).then_inc(ln_rstd, 1)

        def ln_xhat_dve(dve, n, b):
            dve.wait_ge(ln_rstd, n + 1)
            for tt in range(TT):
                op = nc.vector.tensor_scalar(XH[:, tt, :], x_tile(b, tt), MV[:, tt, 0:1], RSTD[:, tt:tt + 1],
                                             ALU.subtract, ALU.mult)
            op.then_inc(ln_xhat, 1)

        def ln_transpose_pe(pe, n, k, into):
            pe.wait_ge(ln_xhat, n + 1)
            for tt in range(TT):
                op = nc.tensor.transpose(into[:, tt * P:(tt + 1) * P], XH[:, tt, k * P:(k + 1) * P], IDENT[:, :])
            return op

        def xn_split_dve(dve, n, k):
            nc.vector.tensor_copy(XN[:, 0, k, :], XNF[:, k, :]).then_inc(xn_hi, 1)
            dve.wait_ge(xn_hi, 2 * n + (k + 1))
            nc.vector.tensor_tensor(XN[:, 1, k, :], XNF[:, k, :], XN[:, 0, k, :].bitcast(F32),
                                    ALU.subtract).then_inc(xn_ready, 1)

        def alone(engine, semaphore, value):
            engine.wait_ge(semaphore, value)
            if not isinstance(value, int):
                engine.sem_inc(waits_carried, 1)

        @block.sync
        def _(sp):
            xv = x.rearrange("b (t p) d -> p (b t) d", p=P)
            sp.dma_start(X[:, 0:TT, :], xv[:, 0:TT, :]).then_inc(s_x[0], 16)
            sp.dma_start(VEC_SB[:, :], vecs).then_inc(s_small, 16)
            sp.dma_start(COND[:, :, :], cond).then_inc(s_small, 16)
            sp.dma_start(WMOD[:, :, 0:768], wmod[:, :, 0:768]).then_inc(s_wmod_a, 16)
            sp.dma_start(WRAW[:, 0:1536], wqkv).then_inc(s_wq, 16)
            sp.dma_start(WMOD[:, :, 768:NMOD * P], wmod[:, :, 768:NMOD * P]).then_inc(s_wmod_b, 16)
            sp.dma_start(BV[:, :], bv.partition_broadcast(P)).then_inc(s_rows, 16)
            sp.dma_start(BO[:, :], bo.partition_broadcast(P)).then_inc(s_rows, 16)
            sp.dma_start(BG[:, 0, :], bgate[0, :].partition_broadcast(P)).then_inc(s_rows, 16)
            sp.dma_start(BG[:, 1, :], bgate[1, :].partition_broadcast(P)).then_inc(s_rows, 16)
            sp.dma_start(WO[:, :, :], wo).then_inc(s_rows, 16)
            for b in range(1, B):
                sp.dma_start(X[:, b * TT:(b + 1) * TT, :], xv[:, b * TT:(b + 1) * TT, :]).then_inc(s_x[b], 16)
            sp.wait_ge(wq_hi, 1)
            sp.wait_ge(wq_lo, 1)
            sp.dma_start(WRAW[:, :], w1_0).then_inc(s_w1raw, 16)

            def stack(b, h):
                o, r = h // 8, HD * (h % 8)
                alone(sp, src_dup, b * 2 + (o + 1))
                if positive(b):
                    alone(sp, exp_done, b * 64 + (16 * (h // 4 + 1) - 64))
                nc.sync.dma_start(QS[0:32, h, :].bitcast(F32), SRCQ[r:r + HD, o, :, :].bitcast(F32))\
                    .then_inc(stack_ready[h], 16)
                nc.sync.dma_start(QS[32:64, h, :].bitcast(F32), SRCQ[r:r + HD, o, :, :].bitcast(F32))\
                    .then_inc(stack_ready[h], 16)
                nc.sync.dma_start(KS[0:32, h, :].bitcast(F32), SRCK[r:r + HD, o, 0:2, :].bitcast(F32))\
                    .then_inc(stack_ready[h], 16)
                nc.sync.dma_start(KS[32:64, h, :].bitcast(F32), SRCK[r:r + HD, o, 1:3, :].bitcast(F32))\
                    .then_inc(stack_ready[h], 16)

            def negmax(q, turn):
                alone(sp, misc_free, turn + 1)
                for part, row in ((0, MAX_HI), (1, MAX_LO)):
                    nc.sync.dma_start(QS[row:row + 1, 4 * q:4 * q + 4, :].bitcast(F32),
                                      NEGMX[:, q, part, :].bitcast(F32)).then_inc(negmax_ready[q], 16)

            def frame(b, kind):
                turns = numbered(b, kind)
                for s in range(16):
                    for t, what, _, i in turns[s]:
                        if what == "MX":
                            negmax(i, t)
                    if kind != "tail" and s < 10:
                        stack(b, 6 + s)
                    if kind in ("first", "middle") and s >= 10:
                        stack(b + 1, s - 10)

            for h in range(6):
                stack(0, h)
            frame(0, "first")
            with sp.Fori(1, B - 1) as b:
                frame(b, "middle")
            frame(B - 1, "last")
            frame(B, "tail")

            sp.wait_ge(pv_done, 16 * B)
            sp.dma_start(W2RAW, w2_0).then_inc(s_w2raw, 16)
            sp.dma_start(RAW1, w1_1).then_inc(s_raw1, 16)
            sp.dma_start(RAW2, w2_1).then_inc(s_raw1, 16)
            sp.wait_ge(misc_free, ALL_TURNS)
            sp.dma_start(B2_0, b2_0.partition_broadcast(P)).then_inc(s_s5raw, 16)
            sp.dma_start(B2_1, b2_1.partition_broadcast(P)).then_inc(s_s5raw, 16)
            for dst, src in ((B_ST, b_st), (B_SW, b_sw), (C_ST, c_st), (C_SW, c_sw)):
                sp.dma_start(dst, src).then_inc(s_s5raw, 16)
            ov = out.rearrange("b (t p) d -> p (b t) d", p=P)
            for b in range(B):
                sp.wait_ge(ffn[3]["down_free"], TT * (b + 1))
                sp.dma_start(ov[:, b * TT:(b + 1) * TT, :], X[:, b * TT:(b + 1) * TT, :]).then_inc(s_out, 16)
            sp.wait_ge(s_out, 16 * B)

        @block.gpsimd
        def _(pool):
            g = nc.gpsimd
            g.memset(IDENT[:, :], 0.0).then_inc(pool_chain, 1)
            g.memset(MINUS_HALF[:, :], -0.5)
            pool.wait_ge(pool_chain, 1)
            g.affine_select(out=IDENT[:, :], in_=IDENT[:, :], compare_op=ALU.not_equal, fill=1.0, base=0,
                            pattern=[[-1, P]], channel_multiplier=1).then_inc(ident_ready, 1)
            pool.wait_ge(ident_ready, 1)
            g.memset(KS[ZERO_ROW:P2_ROWS, :, :].bitcast(F32), 1.0).then_inc(const_ready, 1)
            pool.wait_ge(const_ready, 1)
            g.memset(QS[ZERO_ROW:ZERO_ROW + 1, :, :].bitcast(F32), 0.0).then_inc(const_ready, 1)
            pool.wait_ge(const_ready, 2)
            g.memset(KS[ZERO_ROW:ZERO_ROW + 1, :, :].bitcast(F32), 0.0).then_inc(const_ready, 1)
            pool.wait_ge(const_ready, 3)
            g.memset(VA[:, :, :, :, HD:2 * HD].rearrange("p o t h d -> p (o t h) d"), 1.0).then_inc(const_ready, 1)

            chain = [1]

            def link(op):
                chain[0] += 1
                op.then_inc(pool_chain, 1)
                pool.wait_ge(pool_chain, chain[0])

            def over_b(name):
                return vecs_of(name).unsqueeze(2).to_broadcast([P, KT, B])

            def mt(t):
                return MT[:, t:t + KT, :]

            ln_rstd_pool(pool, LN_ATT)
            pool.wait_ge(mt_ready, 1)
            pool.wait_ge(s_small, 32)

            def affine(ln, scale, shift, w, bias):
                link(g.tensor_scalar(ONE_S[:, :, :], mt(scale), 1.0, None, ALU.add))
                link(g.tensor_tensor(AB[:, ln, 0, :, :], ONE_S[:, :, :], over_b(w), ALU.mult))
                link(g.tensor_tensor(AB[:, ln, 1, :, :], ONE_S[:, :, :], over_b(bias), ALU.mult))
                return g.tensor_tensor(AB[:, ln, 1, :, :], AB[:, ln, 1, :, :], mt(shift), ALU.add)

            affine(0, M_SCALE0, M_SHIFT0, "ln1_w", "ln1_b").then_inc(ab_ready, 1)

            def dup_turn(t, o):
                alone(pool, misc_free, t + 1)
                g.tensor_copy(SRCK[:, o, 2, :], SRCK[:, o, 0, :].bitcast(F32)).then_inc(src_dup, 1)

            def va_fill(o):
                for tt in range(TT):
                    op = g.tensor_copy(VA[:, o, tt, :, 0:HD],
                                       VS[:, tt, o * P:(o + 1) * P].rearrange("p (h d) -> p h d", h=8))
                op.then_inc(va_ready, 1)

            def frame(b, kind):
                turns = numbered(b, kind)
                for s in range(16):
                    if kind in ("first", "middle") and s == 0:
                        ln_rstd_pool(pool, LN_ATT + 1 + b)
                    for t, what, bb, i in turns[s]:
                        if what == "K":
                            dup_turn(t, i)
                        if what == "V" and i == 1 and kind == "first" and s == 1:
                            alone(pool, misc_free, t + 1)
                            pool.wait_ge(const_ready, 4)
                            va_fill(0)
                            va_fill(1)
                    if kind != "first" and kind != "tail" and s == 1:
                        alone(pool, pv_done, b * 16 - 8)
                        va_fill(0)
                    if kind != "first" and kind != "tail" and s == 7:
                        alone(pool, pv_done, b * 16)
                        va_fill(1)
                    if kind == "middle" or kind == "last" or kind == "first":
                        if s == 3:
                            alone(pool, ln_xhat, b + 1)
                            g.tensor_tensor(x_batch(b), x_batch(b), BO[:, :].unsqueeze(1).to_broadcast([P, TT, D]),
                                            ALU.add).then_inc(x_bias, 1)

            dup_turn(3, 0)
            pool.wait_ge(s_rows, 80)
            pool.wait_ge(mt_ready, 4)
            link(affine(1, M_SCALE1, M_SHIFT1, "ln2_w", "ln2_b"))
            g.tensor_scalar(AB[:, 2, 0, :, :], mt(M_SCALE2), 1.0, None, ALU.add)
            g.tensor_copy(AB[:, 2, 1, :, :], mt(M_SHIFT2))
            g.tensor_tensor(DG[:, :, :], mt(M_GATE_A), over_b("d_diag"), ALU.mult)
            link(g.tensor_scalar(ONE_S[:, :, :], mt(M_SCALEF), 1.0, None, ALU.add))
            link(g.tensor_scalar(AB[:, 3, 0, :, :], mt(M_SCALEC), 1.0, None, ALU.add))
            link(g.tensor_tensor(AB[:, 3, 0, :, :], AB[:, 3, 0, :, :], ONE_S[:, :, :], ALU.mult))
            link(g.tensor_tensor(AB[:, 3, 1, :, :], mt(M_SHIFTC), ONE_S[:, :, :], ALU.mult))
            g.tensor_tensor(AB[:, 3, 1, :, :], AB[:, 3, 1, :, :], mt(M_SHIFTF), ALU.add).then_inc(ab_ready, 1)

            frame(0, "first")
            with pool.Fori(1, B - 1) as b:
                frame(b, "middle")
            frame(B - 1, "last")

            ln_rstd_pool(pool, LN_FFN0)
            pool.wait_ge(s_s5raw, 16 * 6)

            def ffn0_pool(b, last):
                alone(pool, ln_xhat, b + (LN_FFN0 + 1))
                g.tensor_tensor(x_batch(b), x_batch(b), B2_0.unsqueeze(1).to_broadcast([P, TT, D]),
                                ALU.add).then_inc(x_bias, 1)
                if not last:
                    ln_rstd_pool(pool, b + (LN_FFN0 + 1))

            with pool.Fori(0, B - 1) as b:
                ffn0_pool(b, False)
            ffn0_pool(B - 1, True)

            cols = {}

            def col(name):
                cols.setdefault(name, len(cols))
                assert len(cols) <= MAG_COL
                return SC[:, cols[name]:cols[name] + 1]

            def ts(dst, src, s1, op0, s2=None, op1=ALU.bypass):
                link(g.tensor_scalar(dst, src, s1, s2, op0, op1) if s2 is not None
                     else g.tensor_scalar(dst, src, s1, None, op0))

            def tt_(dst, a, b_, op):
                link(g.tensor_tensor(dst, a, b_, op))

            ROUND = 1.5 * 2.0 ** 23

            def nearest(dst, src, factor, offset=0.0):
                ts(dst, src, factor, ALU.mult, offset, ALU.add)
                ts(dst, dst, ROUND, ALU.add)
                ts(dst, dst, ROUND, ALU.subtract)

            def horner(dst, r, coefficients):
                ts(dst, r, coefficients[0], ALU.mult, coefficients[1], ALU.add)
                for c in coefficients[2:]:
                    ts(dst, dst, r, ALU.mult, c, ALU.add)

            def exp_(dst, src):
                n, r, t = col("n"), col("r"), col("t")
                nearest(n, src, 1.0 / math.log(2.0))
                ts(n, n, -126.0, ALU.max, 127.0, ALU.min)
                ts(t, n, -0.693359375, ALU.mult)
                tt_(r, src, t, ALU.add)
                ts(t, n, 2.12194440e-4, ALU.mult)
                tt_(r, r, t, ALU.add)
                horner(t, r, [1.0 / math.factorial(k) for k in range(8, -1, -1)])
                ts(col("bits").bitcast(I32), n, 127.0, ALU.add, 2.0 ** 23, ALU.mult)
                tt_(dst, t, col("bits"), ALU.mult)

            lre, lim = vec("lam_re", 0), vec("lam_im", 0)
            dt, mag, th = col("dt"), col("mag"), col("th")
            exp_(dt, vec("log_step", 0))
            tt_(th, lre, dt, ALU.mult)
            exp_(mag, th)
            tt_(th, lim, dt, ALU.mult)
            n, r, t, r2, si, co = col("n"), col("r"), col("t"), col("r2"), col("si"), col("co")
            nearest(n, th, 2.0 / math.pi)
            ts(t, n, -1.5703125, ALU.mult)
            tt_(r, th, t, ALU.add)
            ts(t, n, -4.837512969970703125e-4, ALU.mult)
            tt_(r, r, t, ALU.add)
            ts(t, n, -7.54978995489188216e-8, ALU.mult)
            tt_(r, r, t, ALU.add)
            tt_(r2, r, r, ALU.mult)
            horner(si, r2, [(-1.0) ** k / math.factorial(2 * k + 1) for k in range(5, -1, -1)])
            tt_(si, si, r, ALU.mult)
            horner(co, r2, [(-1.0) ** k / math.factorial(2 * k) for k in range(6, -1, -1)])
            m, is1, is3, odd = col("m"), col("is1"), col("is3"), col("odd")
            nearest(m, n, 0.25, -0.375)
            ts(m, m, -4.0, ALU.mult)
            tt_(m, m, n, ALU.add)
            ts(is1, m, 1.0, ALU.is_equal)
            ts(is3, m, 3.0, ALU.is_equal)
            tt_(odd, is1, is3, ALU.add)
            even, sg_s, sg_c = col("even"), col("sg_s"), col("sg_c")
            ts(even, odd, -1.0, ALU.mult, 1.0, ALU.add)
            ts(sg_s, m, 2.0, ALU.is_ge, -2.0, ALU.mult)
            ts(sg_s, sg_s, 1.0, ALU.add)
            ts(sg_c, m, 2.0, ALU.is_equal)
            tt_(sg_c, sg_c, is1, ALU.add)
            ts(sg_c, sg_c, -2.0, ALU.mult, 1.0, ALU.add)
            sin, cos = col("sin"), col("cos")
            tt_(sin, si, even, ALU.mult)
            tt_(t, co, odd, ALU.mult)
            tt_(sin, sin, t, ALU.add)
            tt_(sin, sin, sg_s, ALU.mult)
            tt_(cos, co, even, ALU.mult)
            tt_(t, si, odd, ALU.mult)
            tt_(cos, cos, t, ALU.add)
            tt_(cos, cos, sg_c, ALU.mult)
            lb_re, lb_im, cr, ci = col("lb_re"), col("lb_im"), col("cr"), col("ci")
            tt_(lb_re, mag, cos, ALU.mult)
            ts(lb_re, lb_re, 1.0, ALU.subtract)
            tt_(lb_im, mag, sin, ALU.mult)
            tt_(cr, lb_re, lre, ALU.mult)
            tt_(t, lb_im, lim, ALU.mult)
            tt_(cr, cr, t, ALU.add)
            tt_(ci, lb_im, lre, ALU.mult)
            tt_(t, lb_re, lim, ALU.mult)
            tt_(ci, ci, t, ALU.subtract)
            tt_(r2, lre, lre, ALU.mult)
            tt_(t, lim, lim, ALU.mult)
            tt_(r2, r2, t, ALU.add)
            link(g.memset(t, -1.0))
            tt_(r2, r2, t, ALU.pow)
            tt_(cr, cr, r2, ALU.mult)
            tt_(ci, ci, r2, ALU.mult)
            sgn, nci, scr, s2 = col("sgn"), col("nci"), col("scr"), col("s2")
            link(g.memset(sgn[0:NS, :], 1.0))
            link(g.memset(sgn[NS:P, :], -1.0))
            tt_(nci, sgn, ci, ALU.mult)
            ts(nci, nci, -1.0, ALU.mult)
            tt_(scr, sgn, cr, ALU.mult)
            ts(s2, sgn, 2.0, ALU.mult)
            part = WGF[:, 0, :]
            ts(BB[:, 0, :], B_ST, cr, ALU.mult)
            ts(part, B_SW, nci, ALU.mult)
            tt_(BB[:, 0, :], BB[:, 0, :], part, ALU.add)
            ts(BB[:, 1, :], B_ST, ci, ALU.mult)
            ts(part, B_SW, scr, ALU.mult)
            g.tensor_tensor(BB[:, 1, :], BB[:, 1, :], part, ALU.add).then_inc(s5c, 1)
            ts(WC[:, 0, :], C_ST, s2, ALU.mult)
            ts(WC[:, 1, :], C_SW, -2.0, ALU.mult)
            link(g.memset(TAB_C[:, 0:1], 1.0))
            link(g.memset(TAB_S[:, 0:1], 0.0))
            wc, ws = col("wc"), col("ws")
            link(g.tensor_copy(wc, cos))
            link(g.tensor_copy(ws, sin))
            n_ = 1
            while n_ < S:
                lo, hi = slice(0, n_), slice(n_, 2 * n_)
                ts(TAB_C[:, hi], TAB_C[:, lo], wc, ALU.mult)
                ts(part[:, lo], TAB_S[:, lo], ws, ALU.mult)
                tt_(TAB_C[:, hi], TAB_C[:, hi], part[:, lo], ALU.subtract)
                ts(TAB_S[:, hi], TAB_S[:, lo], wc, ALU.mult)
                ts(part[:, lo], TAB_C[:, lo], ws, ALU.mult)
                tt_(TAB_S[:, hi], TAB_S[:, hi], part[:, lo], ALU.add)
                if 2 * n_ < S:
                    tt_(t, ws, ws, ALU.mult)
                    tt_(r2, wc, ws, ALU.mult)
                    tt_(wc, wc, wc, ALU.mult)
                    tt_(wc, wc, t, ALU.subtract)
                    ts(ws, r2, 2.0, ALU.mult)
                n_ *= 2
            g.tensor_copy(SC[:, MAG_COL:MAG_COL + 1], mag).then_inc(s5c, 1)

            def s5_pool(b):
                if positive(b):
                    alone(pool, s5["wg_lo"], 2 * b)
                for i in range(2):
                    g.tensor_tensor(WGF[:, i, :], WC[:, i, :],
                                    GATE_A[:, bass.ds(b, 1), :].rearrange("p a n -> p (a n)"),
                                    ALU.mult).then_inc(s5["wgf"], 1)
                for k in range(KT):
                    g.tensor_tensor(DGF[:, k, :], IDENT[:, :], DG[:, k, bass.ds(b, 1)].to_broadcast([P, P]),
                                    ALU.mult).then_inc(s5["wgf"], 1)
                ln_rstd_pool(pool, b + LN_S5)
                pool.wait_ge(s5["t2"], b + 1)
                g.tensor_tensor(S5T[:, 2, :], S5T[:, 0, :], S5T[:, 1, :], ALU.add).then_inc(s5["rot"], 1)

            s5_pool(0)
            with pool.Fori(1, B) as b:
                s5_pool(b)

            ln_rstd_pool(pool, LN_FFN1)

            def ffn1_pool(b, last):
                alone(pool, ln_xhat, b + (LN_FFN1 + 1))
                g.tensor_tensor(GB2, GATE_F[:, bass.ds(b, 1), :].rearrange("p a n -> p (a n)"), B2_1,
                                ALU.mult).then_inc(gb2_ready, 1)
                pool.wait_ge(gb2_ready, b + 1)
                g.tensor_tensor(x_batch(b), x_batch(b), GB2.unsqueeze(1).to_broadcast([P, TT, D]),
                                ALU.add).then_inc(x_bias, 1)
                if not last:
                    ln_rstd_pool(pool, b + (LN_FFN1 + 1))

            with pool.Fori(0, B - 1) as b:
                ffn1_pool(b, False)
            ffn1_pool(B - 1, True)

        @block.scalar
        def _(act):
            a = nc.scalar
            act.wait_ge(s_wq, 16)
            a.activation(WQ[:, 0:1536], WRAW[:, 0:1536], ACT.Copy).then_inc(wq_hi, 1)

            def mrow_out_copies(chunks):
                for c in chunks:
                    j = c // 2
                    op = a.activation(MROW[32 * j:32 * j + B, c % 2, :], bank[c % 2][32 * j:32 * j + B, 0:384], ACT.Copy)
                op.then_inc(mrow_out, 1)

            act.wait_ge(mrow_mm, 1)
            mrow_out_copies((0, 1))

            def turn(t, what, b, i):
                if what == "LT":
                    act.wait_ge(misc_full, t + 1)
                    if positive(b):
                        act.wait_ge(xn_ready, 2 * b + (i - 1))
                    a.activation(XNF[:, i, :], MISC, ACT.Identity, bias=ab(0, 1, i, b), scale=ab(0, 0, i, b))\
                        .then_inc(misc_free, 1)
                if what in ("Q", "K"):
                    act.wait_ge(misc_full, t + 1)
                    if positive(b) and what == "Q":
                        act.wait_ge(s1_full, 32 * b + (16 * i + 10 - 32))
                        for h in range(8 * i + 5, 8 * i + 8):
                            act.wait_ge(stack_ready[h], 64 * b)
                    src, bias = (SRCQ, "bq") if what == "Q" else (SRCK, "bk")
                    a.activation(src[:, i, 0, :], MISC, ACT.Identity, bias=vec(bias, i)).then_inc(src_hi, 1)
                if what == "MX":
                    act.wait_ge(misc_full, t + 1)
                    if positive(b):
                        act.wait_ge(negmax_ready[i], 32 * b)
                    a.activation(NEGMX[:, i, 0, :], MISC[0:16, 0:P], ACT.Copy, scale=-1.0).then_inc(mx_hi, 1)
                if what == "OB":
                    act.wait_ge(misc_full, t + 1)
                    a.activation(OF[:, i, :], MISC, ACT.Copy).then_inc(misc_free, 1)

            act.wait_ge(ab_ready, 1)
            turn(0, "LT", 0, 0)
            turn(1, "LT", 0, 1)
            turn(2, "Q", 0, 0)
            turn(3, "K", 0, 0)
            act.wait_ge(mrow_mm, 2)
            mrow_out_copies(range(2, 8))

            def exps(b, s, js):
                g = 16 * b + (s - LAG)
                kt = (s - LAG) % 4
                for j in js:
                    act.wait_ge(s2_full, 4 * g + (j + 1))
                    if j == 0 and not (isinstance(g, int) and g < 4):
                        act.wait_ge(pv_done, g - 3)
                    a.activation(PTV[:, kt, j, :], bank[4 + j % 2], ACT.Exp, scale=SCALE).then_inc(exp_done, 1)

            def frame(b, kind):
                turns = numbered(b, kind)
                for s in range(16 if kind != "tail" else 12):
                    has_p2 = (kind != "first" or s >= LAG) and (kind != "tail" or s < LAG)
                    if has_p2:
                        exps(b, s, (0, 1))
                    for one in turns[s][0:1]:
                        turn(*one)
                    if has_p2:
                        exps(b, s, (2, 3))
                    for one in turns[s][1:]:
                        turn(*one)
                    done = s - LAG - 1
                    if (kind != "first" or done >= 0) and (kind != "tail" or done < 0) and done % 4 == 3:
                        q = (done // 4) % 4
                        act.wait_ge(pv_done, 16 * b + (done + 1))
                        a.activation(OR[:, q % 2, :], PV, ACT.Copy).then_inc(pv_evac, 1)

            frame(0, "first")
            with act.Fori(1, B - 1) as b:
                frame(b, "middle")
            frame(B - 1, "last")
            frame(B, "tail")

            def split_hi(ph, raw1, raw2):
                a.activation(W1P[:, 0, :, :], raw1.rearrange("p (k n) -> p k n", k=KT), ACT.Copy)\
                    .then_inc(ffn[ph]["w1_hi"], 1)
                a.activation(W2P[:, 0, :, :], raw2.rearrange("p (f n) -> p f n", f=FT), ACT.Copy)\
                    .then_inc(ffn[ph]["w2_hi"], 1)

            def xnf_out(ph, ln, n0, b, done, full):
                for k in range(KT):
                    act.wait_ge(full, 2 * b + (k + 1))
                    act.wait_ge(xn_ready, 2 * b + (2 * n0 + k - 1))
                    a.activation(XNF[:, k, :], bank[k], ACT.Identity, bias=ab(ln, 1, k, b), scale=ab(ln, 0, k, b))\
                        .then_inc(done, 1)

            def ffn_act(ph, ln, n0, b, last, func, b1):
                f = ffn[ph]
                for ft in range(FT):
                    act.wait_ge(f["up_full"], FT * b + (ft + 1))
                    if positive(b) or ft >= 2:
                        act.wait_ge(f["h_lo"], FT * b + (ft - 1))
                    a.activation(HF[:, ft % 2, :], bank[2 + ft % 2], func, bias=vec(b1, ft))
                    if positive(b):
                        if ft < FT - 1:
                            act.wait_ge(f["down_ft"], (FT - 1) * b + (ft + 2 - FT))
                        else:
                            act.wait_ge(f["down_full"], TT * b)
                    a.activation(HH[:, ft, :], bank[2 + ft % 2], func, bias=vec(b1, ft)).then_inc(f["h_hi"], 1)
                if not last:
                    xnf_out(ph, ln, n0, b + 1, f["xnf"], f["t_full"])

            def ffn_act_all(ph, ln, n0, func, b1):
                ffn_act(ph, ln, n0, 0, False, func, b1)
                with act.Fori(1, B - 1) as b:
                    ffn_act(ph, ln, n0, b, False, func, b1)
                ffn_act(ph, ln, n0, B - 1, True, func, b1)

            act.wait_ge(s_w1raw, 16)
            act.wait_ge(s_w2raw, 16)
            split_hi(1, WRAW[:, :], W2RAW)
            xnf_out(1, 1, LN_FFN0, 0, ffn[1]["xnf"], ffn[1]["t_full"])
            ffn_act_all(1, 1, LN_FFN0, ACT.Gelu, "b1_0")

            act.wait_ge(s5["bb_t"], 1)
            a.activation(BBT[:, :, :], bank[0].rearrange("p (m n) -> p m n", m=4), ACT.Copy).then_inc(s5["bbt"], 1)
            act.wait_ge(s5["bbt"], 1)
            a.activation(WB[:, 0, :, :], BBT[:, :, :], ACT.Copy).then_inc(s5["wb_hi"], 1)

            def s5_act(b):
                act.wait_ge(s5["wgf"], 4 * b + 4)
                if positive(b):
                    act.wait_ge(s5["out_full"], TT * b)
                a.activation(WG[:, 0, :, :], WGF[:, :, :], ACT.Copy).then_inc(s5["wg_hi"], 1)
                a.activation(DGP[:, 0, :, :], DGF[:, :, :], ACT.Copy).then_inc(s5["wg_hi"], 1)
                xnf_out(2, 2, LN_S5, b, s5["xnf"], s5["t_full"])
                for m in range(2):
                    act.wait_ge(s5["cyf"], 2 * b + (m + 1))
                    a.activation(CYP[:, m, 0, :], S5T[:, 4 + m, :], ACT.Copy).then_inc(s5["cy_hi"], 1)

            s5_act(0)
            act.wait_ge(s_raw1, 32)
            split_hi(3, RAW1, RAW2)
            with act.Fori(1, B) as b:
                s5_act(b)

            xnf_out(3, 3, LN_FFN1, 0, ffn[3]["xnf"], ffn[3]["t_full"])
            ffn_act_all(3, 3, LN_FFN1, ACT.Gelu_apprx_tanh, "b1_1")

        @block.vector
        def _(dve):
            v = nc.vector
            dve.wait_ge(s_x[0], 16)
            ln_stats_dve(dve, LN_ATT, 0)
            dve.wait_ge(wq_hi, 1)
            v.tensor_tensor(WQ[:, 1536:3072], WRAW[:, 0:1536], WQ[:, 0:1536].bitcast(F32), ALU.subtract)\
                .then_inc(wq_lo, 1)
            ln_xhat_dve(dve, LN_ATT, 0)

            def mt_out(j):
                t0, t1 = 6 * j, 6 * j + 6
                dve.wait_ge(mt_mm, j + 1)
                v.tensor_tensor(MT[:, t0:t1, :], bank[2 + j][:, t0 * B:t1 * B].rearrange("p (t b) -> p t b", b=B),
                                VEC_SB[:, VEC["bmod"][0] + t0:VEC["bmod"][0] + t1].unsqueeze(2)
                                .to_broadcast([P, t1 - t0, B]), ALU.add).then_inc(mt_ready, 1)

            dve.wait_ge(s_small, 32)
            mt_out(0)

            def turn(t, what, b, i):
                if what == "LT":
                    dve.wait_ge(misc_free, t + 1)
                    xn_split_dve(dve, b + LN_ATT, i)
                    return
                dve.wait_ge(misc_full, t + 1)
                if what in ("Q", "K"):
                    src, bias, second = (SRCQ, "bq", 0) if what == "Q" else (SRCK, "bk", 1)
                    dve.wait_ge(src_hi, 4 * b + (2 * i + second + 1))
                    v.scalar_tensor_tensor(src[:, i, 1, :], MISC, vec(bias, i), src[:, i, 0, :].bitcast(F32),
                                           ALU.add, ALU.subtract).then_inc(misc_free, 1)
                if what == "V":
                    if positive(b):
                        dve.wait_ge(va_ready, 2 * b)
                    v.tensor_tensor(VS[:, 2 * i:2 * i + 2, :], MISC.rearrange("p (a n) -> p a n", a=2),
                                    BV[:, :].unsqueeze(1).to_broadcast([P, 2, D]), ALU.add).then_inc(misc_free, 1)
                if what == "MX":
                    dve.wait_ge(mx_hi, QUADS * b + (i + 1))
                    v.scalar_tensor_tensor(NEGMX[:, i, 1, :], MISC[0:16, 0:P], -1.0,
                                           NEGMX[:, i, 0, :].bitcast(F32), ALU.mult, ALU.subtract)\
                        .then_inc(misc_free, 1)
                if what == "OT":
                    o = MISC.rearrange("p (t j c) -> p t j c", t=TT, j=4)
                    v.reciprocal(RC[:, :].rearrange("p (t j) -> p t j", t=TT), o[:, :, :, HD]).then_inc(rc_ready, 1)
                    dve.wait_ge(rc_ready, QUADS * b + (i + 1))
                    v.tensor_tensor(OTK[:, :, 64 * i:64 * i + 64].rearrange("p t (j d) -> p t j d", j=4),
                                    o[:, :, :, 0:HD],
                                    RC[:, :].rearrange("p (t j) -> p t j", t=TT).unsqueeze(3)
                                    .to_broadcast([P, TT, 4, HD]), ALU.mult).then_inc(misc_free, 1)
                if what == "WO":
                    dve.wait_ge(x_bias, b + 1)
                    v.tensor_tensor(x_pair(b, i), x_pair(b, i), MISC.rearrange("p (a n) -> p a n", a=2), ALU.add)\
                        .then_inc(misc_free, 1)

            turn(0, "LT", 0, 0)
            turn(1, "LT", 0, 1)
            turn(2, "Q", 0, 0)
            turn(3, "K", 0, 0)
            for j in range(1, 4):
                mt_out(j)
            dve.wait_ge(s_rows, 80)
            for gi, gate in enumerate((GATE_A, GATE_F)):
                for bp in range(2):
                    dve.wait_ge(gate_mm, 2 * gi + bp + 1)
                    v.tensor_tensor(gate[:, 2 * bp:2 * bp + 2, :],
                                    bank[(2 * gi + bp)].rearrange("p (a n) -> p a n", a=2),
                                    BG[:, gi, :].unsqueeze(1).to_broadcast([P, 2, D]), ALU.add).then_inc(gate_ready, 1)

            def row_max(b, s, half):
                n = 32 * b + (2 * s + half)
                dve.wait_ge(s1_full, n + 1)
                v.reduce_max(MX[:, (s // 4) % 2, s % 4, 2 * half:2 * half + 2], PS1[:, 2 * half:2 * half + 2, :],
                             AX_X).then_inc(s1_free, 1)

            def frame(b, kind):
                turns = numbered(b, kind)
                for s in range(16 if kind != "tail" else 12):
                    if kind != "tail":
                        row_max(b, s, 0)
                    for one in turns[s][0:1]:
                        turn(*one)
                    if kind != "tail":
                        row_max(b, s, 1)
                    for one in turns[s][1:]:
                        turn(*one)
                    if kind in ("first", "middle") and s == 0:
                        if kind == "first":
                            dve.wait_ge(s_x[1], 16)
                            dve.wait_ge(s_x[2], 16)
                            dve.wait_ge(s_x[3], 16)
                        ln_stats_dve(dve, b + (LN_ATT + 1), b + 1)
                    if kind in ("first", "middle") and s == 1:
                        ln_xhat_dve(dve, b + (LN_ATT + 1), b + 1)

            frame(0, "first")
            with dve.Fori(1, B - 1) as b:
                frame(b, "middle")
            frame(B - 1, "last")
            frame(B, "tail")

            def split_lo(ph, raw1, raw2):
                f = ffn[ph]
                dve.wait_ge(f["w1_hi"], 1)
                v.tensor_tensor(W1P[:, 1, :, :], raw1.rearrange("p (k n) -> p k n", k=KT),
                                W1P[:, 0, :, :].bitcast(F32), ALU.subtract).then_inc(f["w1_lo"], 1)
                dve.wait_ge(f["w2_hi"], 1)
                v.tensor_tensor(W2P[:, 1, :, :], raw2.rearrange("p (f n) -> p f n", f=FT),
                                W2P[:, 0, :, :].bitcast(F32), ALU.subtract).then_inc(f["w2_lo"], 1)

            def xn_split(n, b, xnf):
                for k in range(KT):
                    dve.wait_ge(xnf, 2 * b + (k + 1))
                    xn_split_dve(dve, n, k)

            def ffn_dve(ph, n0, b, last, biases):
                f = ffn[ph]
                for ft in range(FT):
                    dve.wait_ge(f["h_hi"], FT * b + (ft + 1))
                    v.tensor_tensor(HL[:, ft, :], HF[:, ft % 2, :], HH[:, ft, :].bitcast(F32), ALU.subtract)\
                        .then_inc(f["h_lo"], 1)
                    if not last and ft == 1:
                        ln_stats_dve(dve, b + (n0 + 1), b + 1)
                    if not last and ft == 4:
                        dve.wait_ge(f["t_full"], 2 * b + 2)
                        ln_xhat_dve(dve, b + (n0 + 1), b + 1)
                if not last:
                    xn_split(b + (n0 + 1), b + 1, f["xnf"])
                dve.wait_ge(x_bias, b + (biases + 1))
                for tt in range(TT):
                    dve.wait_ge(f["down_full"], TT * b + (tt + 1))
                    if ph == 1:
                        v.tensor_tensor(x_tile(b, tt), x_tile(b, tt), bank[4 + tt][:, 0:D], ALU.add)\
                            .then_inc(f["down_free"], 1)
                    else:
                        v.tensor_tensor(TMP[:, tt, :], bank[4 + tt][:, 0:D],
                                        GATE_F[:, bass.ds(b, 1), :].rearrange("p a n -> p (a n)"), ALU.mult)\
                            .then_inc(f["gated"], 1)
                        dve.wait_ge(f["gated"], TT * b + (tt + 1))
                        v.tensor_tensor(x_tile(b, tt), x_tile(b, tt), TMP[:, tt, :], ALU.add)\
                            .then_inc(f["down_free"], 1)

            def ffn_dve_all(ph, n0, biases):
                with dve.Fori(0, B - 1) as b:
                    ffn_dve(ph, n0, b, False, biases)
                ffn_dve(ph, n0, B - 1, True, biases)

            dve.wait_ge(misc_free, ALL_TURNS)
            ln_stats_dve(dve, LN_FFN0, 0)
            ln_xhat_dve(dve, LN_FFN0, 0)
            split_lo(1, WRAW[:, :], W2RAW)
            xn_split(LN_FFN0, 0, ffn[1]["xnf"])
            ffn_dve_all(1, LN_FFN0, B)

            dve.wait_ge(s5["wb_hi"], 1)
            v.tensor_tensor(WB[:, 1, :, :], BBT[:, :, :], WB[:, 0, :, :].bitcast(F32), ALU.subtract)\
                .then_inc(s5["wb_lo"], 1)
            dve.wait_ge(ffn[1]["down_free"], TT * B)
            dve.wait_ge(s5c, 2)
            mag = SC[:, MAG_COL:MAG_COL + 1]

            def s5_dve(b):
                n = b + LN_S5
                ln_stats_dve(dve, n, b)
                dve.wait_ge(s5["wg_hi"], 2 * b + 1)
                v.tensor_tensor(WG[:, 1, :, :], WGF[:, :, :], WG[:, 0, :, :].bitcast(F32), ALU.subtract)\
                    .then_inc(s5["wg_lo"], 1)
                dve.wait_ge(s5["wg_hi"], 2 * b + 2)
                v.tensor_tensor(DGP[:, 1, :, :], DGF[:, :, :], DGP[:, 0, :, :].bitcast(F32), ALU.subtract)\
                    .then_inc(s5["wg_lo"], 1)
                if positive(b):
                    dve.wait_ge(s5["t_full"], 2 * b)
                ln_xhat_dve(dve, n, b)
                if positive(b):
                    dve.wait_ge(s5["out_full"], TT * b)
                xn_split(n, b, s5["xnf"])
                dve.wait_ge(s5["bu_full"], 2 * b + 1)
                v.tensor_tensor(S5T[:, 0, :], bank[2], TAB_C, ALU.mult).then_inc(s5["t1"], 1)
                dve.wait_ge(s5["bu_full"], 2 * b + 2)
                v.tensor_tensor(S5T[:, 1, :], bank[3], TAB_S, ALU.mult).then_inc(s5["t2"], 1)
                dve.wait_ge(s5["rot"], b + 1)
                v.tensor_tensor_scan(S5T[:, 3, :], mag.to_broadcast([P, S]), S5T[:, 2, :], 0.0, ALU.mult, ALU.add)\
                    .then_inc(s5["scan"], 1)
                dve.wait_ge(s5["scan"], b + 1)
                v.tensor_tensor(S5T[:, 4, :], S5T[:, 3, :], TAB_C, ALU.mult).then_inc(s5["cyf"], 1)
                v.tensor_tensor(S5T[:, 5, :], S5T[:, 3, :], TAB_S, ALU.mult).then_inc(s5["cyf"], 1)
                for m in range(2):
                    dve.wait_ge(s5["cy_hi"], 2 * b + (m + 1))
                    v.tensor_tensor(CYP[:, m, 1, :], S5T[:, 4 + m, :], CYP[:, m, 0, :].bitcast(F32), ALU.subtract)\
                        .then_inc(s5["cy_lo"], 1)
                for tt in range(TT):
                    dve.wait_ge(s5["out_full"], TT * b + (tt + 1))
                    v.tensor_tensor(x_tile(b, tt), x_tile(b, tt), bank[4 + tt][:, 0:D], ALU.add)\
                        .then_inc(s5["out_free"], 1)

            dve.wait_ge(ffn[1]["t_full"], 2 * B)
            s5_dve(0)
            split_lo(3, RAW1, RAW2)
            with dve.Fori(1, B) as b:
                s5_dve(b)

            dve.wait_ge(s5["out_free"], TT * B)
            ln_stats_dve(dve, LN_FFN1, 0)
            ln_xhat_dve(dve, LN_FFN1, 0)
            xn_split(LN_FFN1, 0, ffn[3]["xnf"])
            ffn_dve_all(3, LN_FFN1, 2 * B)

        @block.tensor
        def _(pe):
            def mm(out_, lhsT, rhs, start, stop):
                return nc.tensor.matmul(out_, lhsT, rhs, start=start, stop=stop, skip_group_check=True)

            PARTS = ((0, 0), (0, 1), (1, 0))

            def parts(out_, pairs, start=True, stop=True):
                n = 0
                for left, right in pairs:
                    for p, q in PARTS:
                        op = mm(out_, left(p), right(q), start and n == 0, stop and n == 3 * len(pairs) - 1)
                        n += 1
                return op

            pe.wait_ge(ident_ready, 1)

            def mrow(chunks):
                for k in range(KT):
                    for c in chunks:
                        j = c // 2
                        op = mm(bank[c % 2][32 * j:32 * j + B, 0:384], COND[:, k, :], WMOD[:, k, 384 * c:384 * (c + 1)],
                                k == 0, k == KT - 1)
                op.then_inc(mrow_mm, 1)

            def mt_transpose(j):
                for t in range(6 * j, 6 * j + 6):
                    c = t // 3
                    rows = slice(32 * j, 32 * j + B)
                    op = nc.tensor.transpose(bank[2 + j][:, t * B:(t + 1) * B],
                                             MROW[rows, c % 2, P * (t % 3):P * (t % 3 + 1)], IDENT[rows, rows])
                op.then_inc(mt_mm, 1)

            pe.wait_ge(s_small, 32)
            pe.wait_ge(s_wmod_a, 16)
            mrow((0, 1))
            pe.wait_ge(mrow_out, 1)
            mt_transpose(0)

            def turn(t, what, b, i):
                if not (isinstance(t, int) and t == 0):
                    pe.wait_ge(misc_free, t)
                if what == "LT":
                    op = ln_transpose_pe(pe, b + LN_ATT, i, MISC)
                if what in ("Q", "K"):
                    pe.wait_ge(xn_ready, 2 * b + 2)
                    c0 = (0 if what == "Q" else D) + P * i
                    op = parts(MISC, [(lambda p, k=k: WQV[:, p, k, c0:c0 + P], lambda q, k=k: XN[:, q, k, :])
                                      for k in range(KT)])
                if what == "V":
                    for one in range(2):
                        at = (2 * i + one) * P
                        op = parts(MISC[:, D * one:D * (one + 1)],
                                   [(lambda p, k=k, at=at: XN[:, p, k, at:at + P], lambda q, k=k: WQV[:, q, k, 2 * D:3 * D])
                                    for k in range(KT)])
                if what == "MX":
                    pe.wait_ge(s1_free, 32 * b + 8 * (i + 1))
                    op = nc.tensor.transpose(MISC[0:16, 0:P], MX[:, i % 2, :, :].rearrange("p j t -> p (j t)"),
                                             IDENT[:, :])
                if what == "OT":
                    pe.wait_ge(pv_evac, QUADS * b + (i + 1))
                    for qt in range(TT):
                        op = nc.tensor.transpose(MISC[:, qt * P:(qt + 1) * P], OR[:, i % 2, qt * P:(qt + 1) * P],
                                                 IDENT[:, :])
                if what == "OB":
                    for qt in range(TT):
                        op = nc.tensor.transpose(MISC[:, qt * P:(qt + 1) * P], OTK[:, qt, i * P:(i + 1) * P],
                                                 IDENT[:, :])
                if what == "WO":
                    for one in range(2):
                        at = (2 * i + one) * P
                        for k in range(KT):
                            op = mm(MISC[:, D * one:D * (one + 1)], OF[:, k, at:at + P], WO[:, k, :],
                                    k == 0, k == KT - 1)
                op.then_inc(misc_full, 1)

            turn(0, "LT", 0, 0)
            turn(1, "LT", 0, 1)
            pe.wait_ge(wq_lo, 1)
            turn(2, "Q", 0, 0)
            turn(3, "K", 0, 0)
            pe.wait_ge(s_wmod_b, 16)
            mrow(range(2, 8))
            pe.wait_ge(mrow_out, 2)
            for j in range(1, 4):
                mt_transpose(j)
            pe.wait_ge(mt_ready, 4)
            for gi, tile in enumerate((M_GATE_A, M_GATE_F)):
                for bp in range(2):
                    for one in range(2):
                        for k in range(KT):
                            op = mm(bank[2 * gi + bp][:, D * one:D * (one + 1)],
                                    COND[:, k, 2 * bp + one:2 * bp + one + 1].to_broadcast([P, P]),
                                    WMOD[:, k, tile * P:tile * P + D], k == 0, k == KT - 1)
                    op.then_inc(gate_mm, 1)
            pe.wait_ge(gate_ready, 4)
            pe.wait_ge(const_ready, 4)
            pe.wait_ge(s_rows, 80)

            def scores_for_max(b, s, half):
                n = 32 * b + (2 * s + half)
                if half == 0:
                    pe.wait_ge(stack_ready[s], 64 * b + 64)
                if positive(b) or 2 * s + half >= 2:
                    pe.wait_ge(s1_free, n - 1)
                for one in range(2):
                    qt = 2 * half + one
                    op = mm(bank[qt], QS[0:P1_ROWS, s, qt * P:(qt + 1) * P], KS[0:P1_ROWS, s, :], True, True)
                op.then_inc(s1_full, 1)

            def scores_less_max(b, s, j):
                g = 16 * b + (s - LAG)
                q, kt = ((s - LAG) // 4) % 4, (s - LAG) % 4
                h = 4 * q + j
                if kt == 0 and j == 0:
                    pe.wait_ge(negmax_ready[q], 32 * b + (32 if s >= LAG else 0))
                if not (isinstance(g, int) and g == 0 and j < 2):
                    pe.wait_ge(exp_done, 4 * g + (j - 1))
                mm(bank[4 + j % 2], KS[0:P2_ROWS, h, kt * P:(kt + 1) * P], QS[0:P2_ROWS, h, :], True, True)\
                    .then_inc(s2_full, 1)

            def values(b, s):
                g = 16 * b + (s - LAG - 1)
                q, kt = ((s - LAG - 1) // 4) % 4, (s - LAG - 1) % 4
                o = q // 2
                if kt == 0:
                    if not (isinstance(g, int) and g == 0):
                        pe.wait_ge(pv_evac, QUADS * b + ((s - LAG - 1) // 4))
                    pe.wait_ge(va_ready, 2 * b + (o + 1 if s > LAG else o - 1))
                pe.wait_ge(exp_done, 4 * g + 4)
                for j in range(4):
                    op = mm(PV[32 * j:32 * (j + 1), :], VA[:, o, kt, 4 * (q % 2) + j, :], PTV[:, kt, j, :],
                            kt == 0, kt == TT - 1)
                op.then_inc(pv_done, 1)

            def frame(b, kind):
                turns = numbered(b, kind)
                for s in range(16 if kind != "tail" else 12):
                    has_p1 = kind != "tail"
                    has_p2 = (kind != "first" or s >= LAG) and (kind != "tail" or s < LAG)
                    has_pv = (kind != "first" or s > LAG) and (kind != "tail" or s <= LAG)
                    if has_p2:
                        scores_less_max(b, s, 0)
                    if has_p1:
                        scores_for_max(b, s, 0)
                    if has_p2:
                        scores_less_max(b, s, 1)
                    for one in turns[s][0:1]:
                        turn(*one)
                    if has_p2:
                        scores_less_max(b, s, 2)
                    if has_p1:
                        scores_for_max(b, s, 1)
                    if has_p2:
                        scores_less_max(b, s, 3)
                    if has_pv:
                        values(b, s)
                    for one in turns[s][1:]:
                        turn(*one)

            frame(0, "first")
            with pe.Fori(1, B - 1) as b:
                frame(b, "middle")
            frame(B - 1, "last")
            frame(B, "tail")

            def transpose_norm(n, b, full):
                for k in range(KT):
                    ln_transpose_pe(pe, n, k, bank[k]).then_inc(full, 1)

            def ffn_pe(ph, n0, b, last):
                f = ffn[ph]

                def down(ft):
                    pe.wait_ge(f["h_lo"], FT * b + (ft + 1))
                    for tt in range(TT):
                        if ft == 0 and positive(b):
                            pe.wait_ge(f["down_free"], TT * b + (tt + 1 - TT))
                        op = parts(bank[4 + tt][:, 0:D],
                                   [(lambda p: (HH, HL)[p][:, ft, tt * P:(tt + 1) * P], lambda q: W2P[:, q, ft, :])],
                                   start=ft == 0, stop=ft == FT - 1)
                        if ft == FT - 1:
                            op.then_inc(f["down_full"], 1)
                    if ft < FT - 1:
                        op.then_inc(f["down_ft"], 1)

                pe.wait_ge(xn_ready, 2 * b + (2 * n0 + 2))
                for ft in range(FT):
                    if positive(b) or ft >= 2:
                        pe.wait_ge(f["h_hi"], FT * b + (ft - 1))
                    parts(bank[2 + ft % 2], [(lambda p, k=k: W1P[:, p, k, ft * P:(ft + 1) * P],
                                              lambda q, k=k: XN[:, q, k, :]) for k in range(KT)])\
                        .then_inc(f["up_full"], 1)
                    if ft == 2 and not positive(b):
                        pe.wait_ge(f["w2_lo"], 1)
                    if 2 <= ft:
                        down(ft - 2)
                if not last:
                    transpose_norm(b + (n0 + 1), b + 1, f["t_full"])
                down(FT - 2)
                down(FT - 1)

            def ffn_pe_all(ph, n0):
                ffn_pe(ph, n0, 0, False)
                with pe.Fori(1, B - 1) as b:
                    ffn_pe(ph, n0, b, False)
                ffn_pe(ph, n0, B - 1, True)

            pe.wait_ge(s1_free, 2 * H * B)
            transpose_norm(LN_FFN0, 0, ffn[1]["t_full"])
            pe.wait_ge(exp_done, 64 * B)
            pe.wait_ge(pv_evac, QUADS * B)
            pe.wait_ge(misc_free, ALL_TURNS)
            pe.wait_ge(ffn[1]["w1_lo"], 1)
            ffn_pe_all(1, LN_FFN0)

            pe.wait_ge(s5c, 1)
            pe.wait_ge(ffn[1]["xnf"], KT * B)
            for m in range(2):
                for k in range(KT):
                    op = nc.tensor.transpose(bank[0][:, (2 * m + k) * P:(2 * m + k + 1) * P],
                                             BB[:, m, k * P:(k + 1) * P], IDENT[:, :])
            op.then_inc(s5["bb_t"], 1)
            pe.wait_ge(s5["bbt"], 1)
            pe.wait_ge(ffn[1]["h_hi"], FT * B)
            pe.wait_ge(s5["wb_lo"], 1)

            def s5_pe(b):
                if positive(b):
                    pe.wait_ge(s5["xnf"], KT * b)
                transpose_norm(b + LN_S5, b, s5["t_full"])
                pe.wait_ge(xn_ready, 2 * b + (2 * LN_S5 + 2))
                for m in range(2):
                    if positive(b):
                        pe.wait_ge((s5["t1"], s5["t2"])[m], b)
                    parts(bank[2 + m], [(lambda p, k=k: WB[:, p, 2 * m + k, :], lambda q, k=k: XN[:, q, k, :])
                                        for k in range(KT)]).then_inc(s5["bu_full"], 1)
                pe.wait_ge(s5["wg_lo"], 2 * b + 2)
                pe.wait_ge(s5["cy_lo"], 2 * b + 2)
                for tt in range(TT):
                    at = slice(tt * P, (tt + 1) * P)
                    if positive(b):
                        pe.wait_ge(s5["out_free"], TT * b + (tt + 1 - TT))
                    parts(bank[4 + tt][:, 0:D], [(lambda p, m=m: CYP[:, m, p, at], lambda q, m=m: WG[:, q, m, :])
                                                 for m in range(2)], stop=False)
                    for k in range(KT):
                        op = parts(bank[4 + tt][:, k * P:(k + 1) * P],
                                   [(lambda p: XN[:, p, k, at], lambda q: DGP[:, q, k, :])],
                                   start=False, stop=k == KT - 1)
                    op.then_inc(s5["out_full"], 1)

            pe.wait_ge(ffn[1]["down_free"], TT * B)
            s5_pe(0)
            with pe.Fori(1, B) as b:
                s5_pe(b)

            pe.wait_ge(s5["xnf"], KT * B)
            transpose_norm(LN_FFN1, 0, ffn[3]["t_full"])
            pe.wait_ge(s5["t2"], B)
            pe.wait_ge(s5["out_free"], TT * B)
            pe.wait_ge(ffn[3]["w1_lo"], 1)
            ffn_pe_all(3, LN_FFN1)


_ORDER = ["x", "vecs", "cond", "wmod", "bgate", "wqkv", "bv", "wo", "bo", "w1_0", "w2_0", "b2_0",
          "b_st", "b_sw", "c_st", "c_sw", "w1_1", "w2_1", "b2_1"]


def kernel(**inputs):
    import numpy as np
    import concourse.bacc as bacc
    from concourse.bass_utils import run_bass_kernel_spmd

    a = {k: np.asarray(v) for k, v in inputs.items()}
    L0, L1 = "L0_cond_", "L1_cond_"

    def feature_tiles(m):
        return np.ascontiguousarray(m.reshape(m.shape[0] // P, P, m.shape[1]).transpose(1, 0, 2))

    def columns(v):
        return v.reshape(-1, P).T

    def twice(v):
        return np.concatenate([v, v])

    bmod = np.concatenate([a[L0 + "bt_attn"], a[L0 + "bt_ffn"], a[L1 + "bm"], a[L1 + "bc"]])
    vectors = {"ln1_w": a[L0 + "ln1_w"], "ln1_b": a[L0 + "ln1_b"], "ln2_w": a[L0 + "ln2_w"], "ln2_b": a[L0 + "ln2_b"],
               "bq": a[L0 + "bq"], "bk": a[L0 + "bk"], "bmod": bmod, "b1_0": a[L0 + "b1"], "b1_1": a[L1 + "b1"],
               "d_diag": a[L1 + "D_diag"], "lam_re": twice(a[L1 + "Lam_re"]), "lam_im": twice(a[L1 + "Lam_im"]),
               "log_step": twice(a[L1 + "log_step"])}
    laid = {
        "x": a["x"],
        "vecs": np.concatenate([columns(vectors[name]) for name, _ in VEC_SIZES], axis=1),
        "cond": feature_tiles(a["cond_1024"].T),
        "wmod": feature_tiles(np.concatenate([a[L0 + "wt_attn"], a[L0 + "wt_ffn"], a[L1 + "Wm"], a[L1 + "Wc"]], axis=1)),
        "bgate": np.stack([a[L1 + "bm"][2 * D:3 * D], a[L1 + "bm"][5 * D:6 * D]]),
        "wqkv": feature_tiles(np.concatenate([a[L0 + "wq"], a[L0 + "wk"], a[L0 + "wv"]], axis=1)).reshape(P, -1),
        "bv": a[L0 + "bv"],
        "wo": feature_tiles(a[L0 + "wo"]),
        "bo": a[L0 + "bo"],
        "w1_0": feature_tiles(a[L0 + "w1"]).reshape(P, -1),
        "w2_0": feature_tiles(a[L0 + "w2"]).reshape(P, -1),
        "b2_0": a[L0 + "b2"],
        "b_st": np.concatenate([a[L1 + "B_re"], a[L1 + "B_im"]]),
        "b_sw": np.concatenate([a[L1 + "B_im"], a[L1 + "B_re"]]),
        "c_st": np.concatenate([a[L1 + "C_re"].T, a[L1 + "C_im"].T]),
        "c_sw": np.concatenate([a[L1 + "C_im"].T, a[L1 + "C_re"].T]),
        "w1_1": feature_tiles(a[L1 + "W1"]).reshape(P, -1),
        "w2_1": feature_tiles(a[L1 + "W2"]).reshape(P, -1),
        "b2_1": a[L1 + "b2"],
    }
    nc = bacc.Bacc("TRN2", target_bir_lowering=False, num_devices=1, dynamic_dma_scratch_size=4096)
    arrays, args = {}, []
    for name in _ORDER:
        arrays["in_" + name] = np.ascontiguousarray(laid[name])
        args.append(nc.dram_tensor("in_" + name, laid[name].shape, F32, kind="ExternalInput").ap())
    out = nc.dram_tensor("out_y", (B, S, D), F32, kind="ExternalOutput").ap()
    cond_seq_kernel(nc, *args, out)
    r = run_bass_kernel_spmd(nc, [arrays], core_ids=[0])
    return r.results[0]["out_y"]
```

```python
import math
from contextlib import ExitStack

import concourse.bass as bass
from concourse import mybir

F32 = mybir.dt.float32
F32R = mybir.dt.float32r
I32 = mybir.dt.int32
ALU = mybir.AluOpType
ACT = mybir.ActivationFunctionType
AX_X = mybir.AxisListType.X

P = 128
B, S, D = 4, 512, 256
H, HD = 16, 16
F = 1024
NS = 64
KT = D // P
TT = S // P
FT = F // P
EPS = 1e-5
QUADS = H // 4
SCALE = 1.0 / math.sqrt(HD)
ZERO_ROW, MAX_HI, MAX_LO = 64, 65, 66
P1_ROWS, P2_ROWS = 65, 67
LAG = 6
NMOD = 24

M_SHIFT0, M_SCALE0, M_SHIFT1, M_SCALE1 = 0, 2, 4, 6
M_SHIFT2, M_SCALE2, M_GATE_A, M_SHIFTF, M_SCALEF, M_GATE_F = 8, 10, 12, 14, 16, 18
M_SCALEC, M_SHIFTC = 20, 22

VEC_SIZES = [("ln1_w", 2), ("ln1_b", 2), ("ln2_w", 2), ("ln2_b", 2), ("bq", 2), ("bk", 2), ("bmod", NMOD),
             ("b1_0", FT), ("b1_1", FT), ("d_diag", 2), ("lam_re", 1), ("lam_im", 1), ("log_step", 1)]
VEC = {}
for _name, _n in VEC_SIZES:
    VEC[_name] = sum(VEC[k][1] for k in VEC), _n
NVEC = sum(n for _, n in VEC_SIZES)


MAG_COL = 31


def turns_of(kind):
    first, last, tail = kind == "first", kind == "last", kind == "tail"
    steps = {s: [] for s in range(16)}
    if first:
        steps[0] += [("V", 0, 0)]
        steps[1] += [("V", 0, 1), ("Q", 0, 1)]
        steps[2] += [("K", 0, 1)]
    else:
        steps[0] += [("MX", -1, 3)]
    if not (last or tail):
        steps[2] += [("LT", 1, 0)]
        steps[3] += [("LT", 1, 1)]
    if not first:
        steps[3] += [("OT", -1, 2)]
    if not tail:
        steps[4] += [("MX", 0, 0)]
    if not (last or tail):
        steps[5] += [("Q", 1, 0)]
        steps[6] += [("K", 1, 0)]
    if not first:
        steps[7] += [("OT", -1, 3)]
        steps[8] += [("OB", -1, 0)]
        steps[9] += [("OB", -1, 1)]
        steps[10] += [("WO", -1, 0)]
        steps[11] += [("WO", -1, 1)]
    if not tail:
        steps[8] += [("MX", 0, 1)]
        steps[11] += [("OT", 0, 0)]
        steps[12] += [("MX", 0, 2)]
        steps[15] += [("OT", 0, 1)]
    if not (last or tail):
        steps[9] += [("V", 1, 0)]
        steps[10] += [("V", 1, 1)]
        steps[13] += [("Q", 1, 1)]
        steps[14] += [("K", 1, 1)]
    return steps


def n_turns(kind):
    return sum(len(v) for v in turns_of(kind).values())


PRO_TURNS = 4
FIRST_TURNS, MID_TURNS, LAST_TURNS, TAIL_TURNS = (n_turns(k) for k in ("first", "middle", "last", "tail"))


def turn_base(b):
    if isinstance(b, int) and b == 0:
        return PRO_TURNS
    if isinstance(b, int) and b == B:
        return PRO_TURNS + FIRST_TURNS + (B - 2) * MID_TURNS + LAST_TURNS
    return b * MID_TURNS + (PRO_TURNS + FIRST_TURNS - MID_TURNS)


ALL_TURNS = turn_base(B) + TAIL_TURNS


def numbered(b, kind):
    out, n = {}, turn_base(b)
    for s, turns in turns_of(kind).items():
        out[s] = []
        for what, off, i in turns:
            out[s].append((n, what, b + off, i))
            n = n + 1
    return out


def positive(b):
    return not (isinstance(b, int) and b <= 0)


def cond_seq_kernel(nc, x, vecs, cond, wmod, bgate, wqkv, bv, wo, bo, w1_0, w2_0, b2_0,
                    b_st, b_sw, c_st, c_sw, w1_1, w2_1, b2_1, out):
    ctx = ExitStack()
    with ctx:
        def sb(name, shape, dt=F32):
            return ctx.enter_context(nc.sbuf_tensor(name, shape, dt))

        def sem(name):
            return ctx.enter_context(nc.semaphore(name))

        X = sb("X", [P, B * TT, D])
        STK = sb("STK", [P, 2 * H * S], F32R)
        PT = sb("PT", [P, TT * 4 * S])
        SRCQ = sb("SRCQ", [P, 2, 2, S], F32R)
        SRCK = sb("SRCK", [P, 2, 3, S], F32R)
        WQ = sb("WQ", [P, 3072], F32R)
        WRAW = sb("WRAW", [P, 2048])
        XNF = sb("XNF", [P, KT, S])
        XNF2 = sb("XNF2", [P, KT, S])
        XN = sb("XN", [P, 2, KT, S], F32R)
        XH = sb("XH", [P, TT, D])
        AO = sb("AO", [P, 6144])
        WO = sb("WO", [P, KT, D])
        VEC_SB = sb("VEC_SB", [P, NVEC])
        COND = sb("COND", [P, KT, B])
        IDENT = sb("IDENT", [P, P])
        BV = sb("BV", [P, D])
        BO = sb("BO", [P, D])
        GATE_A = sb("GATE_A", [P, B, D])
        GATE_F = sb("GATE_F", [P, B, D])
        MT = sb("MT", [P, NMOD, B])
        ONE_S = sb("ONE_S", [P, KT, B])
        AB = sb("AB", [P, 4, 2, KT, B])
        DG = sb("DG", [P, KT, B])
        STAT = sb("STAT", [P, TT, 6])
        MV = sb("MV", [P, TT, 2])
        VE = sb("VE", [P, TT])
        RSTD = sb("RSTD", [P, TT])
        MINUS_HALF = sb("MINUS_HALF", [P, TT])
        MX = sb("MX", [P, 2, 4, TT])
        NEGMX = sb("NEGMX", [16, QUADS, 2, P], F32R)
        RC = sb("RC", [P, 16])
        PART = sb("PART", [P, D])
        SC = sb("SC", [P, 32])

        QS = STK[0:P2_ROWS, 0:H * S].rearrange("p (h t) -> p h t", h=H)
        KS = STK[0:P2_ROWS, H * S:2 * H * S].rearrange("p (h t) -> p h t", h=H)
        PTV = PT[:, :].rearrange("p (k j t) -> p k j t", k=TT, j=4)
        WMOD = PT[:, 0:2 * NMOD * P].rearrange("p (k n) -> p k n", k=KT)
        WQV = WQ[:, :].rearrange("p (s k n) -> p s k n", s=2, k=KT)
        VS = AO[:, 0:1024].rearrange("p (t n) -> p t n", t=TT)
        VA = AO[:, 1024:3072].rearrange("p (o t h d) -> p o t h d", o=2, t=TT, h=8)
        OR = AO[:, 3072:4096].rearrange("p (s t) -> p s t", s=2)
        OTK = AO[:, 4096:5120].rearrange("p (t n) -> p t n", t=TT)
        OF = AO[:, 5120:6144].rearrange("p (k t) -> p k t", k=KT)
        MROW = AO[:, 4096:4864].rearrange("p (h n) -> p h n", h=2)
        BG = AO[:, 3072:3584].rearrange("p (g n) -> p g n", g=2)
        ROWS = AO[:, 3584:4096]
        W1P = STK[:, 0:4096].rearrange("p (s k n) -> p s k n", s=2, k=KT)
        HH = STK[:, 4096:8192].rearrange("p (f t) -> p f t", f=FT)
        W2P = STK[:, 8192:12288].rearrange("p (s f n) -> p s f n", s=2, f=FT)
        HL = STK[:, 12288:16384].rearrange("p (f t) -> p f t", f=FT)
        T1, T2, ROT, STATE = (PT[:, S * i:S * (i + 1)] for i in range(4))
        HF = PT[:, 2048:3072].rearrange("p (s t) -> p s t", s=2)
        CYF = PT[:, 3072:4096].rearrange("p (m t) -> p m t", m=2)
        TMP = PT[:, 3072:4096].rearrange("p (a t n) -> p a t n", a=2, t=2)
        RAW1 = PT[:, 4096:6144]
        RAW2 = PT[:, 6144:8192]
        CYP, XN2 = SRCK, SRCQ
        TAB_C, TAB_S = AO[:, 0:512], AO[:, 512:1024]
        B_ST, B_SW, C_ST, C_SW = (AO[:, 1024 + 256 * i:1280 + 256 * i] for i in range(4))
        B2_0, B2_1, GB2 = (AO[:, 2048 + 256 * i:2304 + 256 * i] for i in range(3))
        BB = AO[:, 3072:3584].rearrange("p (m n) -> p m n", m=2)
        WC = AO[:, 3584:4096].rearrange("p (m n) -> p m n", m=2)
        WGF = AO[:, 4096:4608].rearrange("p (m n) -> p m n", m=2)
        DGF = AO[:, 4608:4864].rearrange("p (k n) -> p k n", k=KT)
        BBT = AO[:, 5120:5632].rearrange("p (m n) -> p m n", m=4)
        WB = WQ[:, 0:1024].rearrange("p (s m n) -> p s m n", s=2, m=4)
        WG = WQ[:, 1024:2048].rearrange("p (s m n) -> p s m n", s=2, m=2)
        DGP = WQ[:, 2048:2560].rearrange("p (s k n) -> p s k n", s=2, k=KT)

        PS = [ctx.enter_context(nc.psum_tensor(f"bank{i}", [P, 512], F32)) for i in range(4, 8)]
        PS1 = ctx.enter_context(nc.psum_tensor("banks0_3", [P, 4, 512], F32))
        bank = [PS1[:, i, :] for i in range(4)] + [p[:, :] for p in PS]
        PV, MISC = bank[6], bank[7]
        T_BANK, UP_BANK, DOWN_BANK, S5_BANK = 0, 2, 4, 6

        def vec(name, i):
            at = VEC[name][0] + i
            return VEC_SB[:, at:at + 1]

        def vecs_of(name):
            at, n = VEC[name]
            return VEC_SB[:, at:at + n]

        def x_tile(b, tt):
            return X[:, bass.ds(b * TT + tt, 1), :].rearrange("p a n -> p (a n)")

        def x_pair(b, p):
            return X[:, bass.ds(b * TT + 2 * p, 2), :]

        def x_batch(b):
            return X[:, bass.ds(b * TT, TT), :]

        def ab(ln, which, k, b):
            return AB[:, ln, which, k, bass.ds(b, 1)]

        s_x = [sem(f"x_loaded{b}") for b in range(B)]
        s_small = sem("small_loaded")
        s_wq = sem("wqkv_loaded")
        s_wmod_a = sem("wmod_attn_loaded")
        s_wmod_b = sem("wmod_rest_loaded")
        s_rows = sem("rows_loaded")
        s_const_rows = sem("constant_rows_placed")
        s_w1raw = sem("w1_raw_loaded")
        s_w2raw = sem("w2_raw_loaded")
        s_raw1 = sem("block1_raw_loaded")
        s_s5raw = sem("s5_raw_loaded")
        s_out = sem("out_stored")
        ident_ready = sem("ident_ready")
        const_ready = sem("const_ready")
        wq_hi, wq_lo = sem("wq_hi"), sem("wq_lo")
        mrow_mm, mrow_out, mt_mm, mt_ready = sem("mrow_mm"), sem("mrow_out"), sem("mt_mm"), sem("mt_ready")
        gate_mm, gate_ready = sem("gate_mm"), sem("gate_ready")
        ab_ready = sem("ab_ready")
        pool_chain = sem("pool_chain")
        ln_stats, ln_mv, ln_ve, ln_rstd, ln_xhat = (sem(n) for n in ("ln_stats", "ln_mv", "ln_ve", "ln_rstd", "ln_xhat"))
        xn_hi, xn_ready = sem("xn_hi"), sem("xn_ready")
        misc_full, misc_free = sem("misc_full"), sem("misc_free")
        src_hi, src_dup = sem("src_hi"), sem("src_dup")
        mx_hi = sem("mx_hi")
        stack_ready = [sem(f"stack_ready{h}") for h in range(H)]
        negmax_ready = [sem(f"negmax_ready{q}") for q in range(QUADS)]
        s1_full, s1_free = sem("s1_full"), sem("s1_free")
        s2_full, exp_done = sem("s2_full"), sem("exp_done")
        pv_done, pv_evac = sem("pv_done"), sem("pv_evac")
        va_ready = sem("va_ready")
        rc_ready = sem("rc_ready")
        x_bias = sem("x_bias")
        ffn = {n: sem(f"{n}_ffn") for n in
               ("t_full", "xnf", "up_full", "h_hi", "h_lo", "down_ft", "down_full", "down_free",
                "w1_hi", "w1_lo", "w2_hi", "w2_lo", "gated")}
        gb2_ready = sem("gb2_ready")
        waits_carried = sem("waits_carried")
        s5_tables, s5_inputs = sem("s5_tables"), sem("s5_inputs")
        s5 = {n: sem(f"{n}_s5") for n in
              ("t_full", "xnf", "xn_hi", "xn_ready", "bu_full", "t1", "t2", "rot", "scan", "cyf", "cy_hi", "cy_lo",
               "wgf", "wg_hi", "wg_lo", "out_full", "out_free", "bb_t", "bbt", "wb_hi", "wb_lo")}
        block = ctx.enter_context(nc.Block())

        LN_ATT, LN_FFN = 0, B
        LAYERS = 2
        FRAMES = LAYERS * B
        W_CHUNKS = 2
        WN = FT // W_CHUNKS

        def ffn_batch(f, layer):
            return f - B * layer

        def norm_next(f, with_s5):
            if isinstance(f, int) and f == 0:
                return LN_FFN + 1
            return 2 * f + (LN_FFN + 1) if with_s5 else f + (LN_FFN + B + 1)

        def norm_s5(f):
            return 2 * f + LN_FFN

        def ffn_frames(engine, frame):
            frame(0, 0, False, True, True)
            with engine.Fori(1, B - 1) as f:
                frame(f, 0, True, True, True)
            frame(B - 1, 0, True, True, True)
            frame(B, 1, True, True, False)
            with engine.Fori(B + 1, FRAMES - 1) as f:
                frame(f, 1, False, True, False)
            frame(FRAMES - 1, 1, False, False, False)

        def ln_stats_dve(dve, n, b):
            for tt in range(TT):
                op = nc.vector.bn_stats(STAT[:, tt, :], x_tile(b, tt))
            op.then_inc(ln_stats, 1)
            alone(dve, ln_stats, n + 1)
            for tt in range(TT):
                op = nc.vector.bn_aggr(MV[:, tt, :], STAT[:, tt, :])
            op.then_inc(ln_mv, 1)

        def ln_rstd_pool(pool, n):
            alone(pool, ln_mv, n + 1)
            nc.gpsimd.tensor_scalar(VE[:, :], MV[:, :, 1], EPS, None, ALU.add).then_inc(ln_ve, 1)
            pool.wait_ge(ln_ve, n + 1)
            nc.gpsimd.tensor_tensor(RSTD[:, :], VE[:, :], MINUS_HALF[:, :], ALU.pow).then_inc(ln_rstd, 1)

        def ln_xhat_dve(dve, n, b):
            dve.wait_ge(ln_rstd, n + 1)
            for tt in range(TT):
                op = nc.vector.tensor_scalar(XH[:, tt, :], x_tile(b, tt), MV[:, tt, 0:1], RSTD[:, tt:tt + 1],
                                             ALU.subtract, ALU.mult)
            op.then_inc(ln_xhat, 1)

        def ln_transpose_pe(pe, n, k, into):
            pe.wait_ge(ln_xhat, n + 1)
            for tt in range(TT):
                op = nc.tensor.transpose(into[:, tt * P:(tt + 1) * P], XH[:, tt, k * P:(k + 1) * P], IDENT[:, :])
            return op

        def xn_split_dve(dve, m, k, full, parts_, hi, ready):
            nc.vector.tensor_copy(parts_(0, k), full[:, k, :]).then_inc(hi, 1)
            dve.wait_ge(hi, 2 * m + (k + 1))
            nc.vector.tensor_tensor(parts_(1, k), full[:, k, :], parts_(0, k).bitcast(F32),
                                    ALU.subtract).then_inc(ready, 1)

        def xn_part(p, k):
            return XN[:, p, k, :]

        def xn2_part(p, k):
            return XN2[:, k, p, :]

        def alone(engine, semaphore, value):
            engine.wait_ge(semaphore, value)
            if not isinstance(value, int):
                engine.sem_inc(waits_carried, 1)

        @block.sync
        def _(sp):
            xv = x.rearrange("b (t p) d -> p (b t) d", p=P)
            sp.dma_start(X[:, 0:TT, :], xv[:, 0:TT, :]).then_inc(s_x[0], 16)
            sp.dma_start(VEC_SB[:, :], vecs).then_inc(s_small, 16)
            sp.dma_start(COND[:, :, :], cond).then_inc(s_small, 16)
            sp.dma_start(WMOD[:, :, 0:768], wmod[:, :, 0:768]).then_inc(s_wmod_a, 16)
            sp.dma_start(WRAW[:, 0:1536], wqkv).then_inc(s_wq, 16)
            sp.dma_start(WMOD[:, :, 768:NMOD * P], wmod[:, :, 768:NMOD * P]).then_inc(s_wmod_b, 16)
            sp.wait_ge(const_ready, 2)
            for stacks, row, constant in ((QS, ZERO_ROW, 0), (KS, ZERO_ROW, 0), (KS, MAX_HI, 32), (KS, MAX_LO, 32)):
                sp.dma_start(stacks[row:row + 1, :, :].bitcast(F32),
                             ROWS[constant:constant + 1, :].unsqueeze(1).to_broadcast([1, H, S]))\
                    .then_inc(s_const_rows, 16)
            sp.dma_start(BV[:, :], bv.partition_broadcast(P)).then_inc(s_rows, 16)
            sp.dma_start(BO[:, :], bo.partition_broadcast(P)).then_inc(s_rows, 16)
            sp.dma_start(BG[:, 0, :], bgate[0, :].partition_broadcast(P)).then_inc(s_rows, 16)
            sp.dma_start(BG[:, 1, :], bgate[1, :].partition_broadcast(P)).then_inc(s_rows, 16)
            sp.dma_start(WO[:, :, :], wo).then_inc(s_rows, 16)
            for b in range(1, B):
                sp.dma_start(X[:, b * TT:(b + 1) * TT, :], xv[:, b * TT:(b + 1) * TT, :]).then_inc(s_x[b], 16)
            sp.wait_ge(wq_hi, 1)
            sp.wait_ge(wq_lo, 1)
            sp.dma_start(WRAW[:, :], w1_0).then_inc(s_w1raw, 16)

            def stack(b, h):
                o, r = h // 8, HD * (h % 8)
                alone(sp, src_dup, b * 2 + (o + 1))
                if positive(b):
                    alone(sp, exp_done, b * 64 + (16 * (h // 4 + 1) - 64))
                nc.sync.dma_start(QS[0:32, h, :].bitcast(F32), SRCQ[r:r + HD, o, :, :].bitcast(F32))\
                    .then_inc(stack_ready[h], 16)
                nc.sync.dma_start(QS[32:64, h, :].bitcast(F32), SRCQ[r:r + HD, o, :, :].bitcast(F32))\
                    .then_inc(stack_ready[h], 16)
                nc.sync.dma_start(KS[0:32, h, :].bitcast(F32), SRCK[r:r + HD, o, 0:2, :].bitcast(F32))\
                    .then_inc(stack_ready[h], 16)
                nc.sync.dma_start(KS[32:64, h, :].bitcast(F32), SRCK[r:r + HD, o, 1:3, :].bitcast(F32))\
                    .then_inc(stack_ready[h], 16)

            def negmax(q, turn):
                alone(sp, misc_free, turn + 1)
                for part, row in ((0, MAX_HI), (1, MAX_LO)):
                    nc.sync.dma_start(QS[row:row + 1, 4 * q:4 * q + 4, :].bitcast(F32),
                                      NEGMX[:, q, part, :].bitcast(F32)).then_inc(negmax_ready[q], 16)

            def frame(b, kind):
                turns = numbered(b, kind)
                for s in range(16):
                    for t, what, _, i in turns[s]:
                        if what == "MX":
                            negmax(i, t)
                    if kind != "tail" and s < 10:
                        stack(b, 6 + s)
                    if kind in ("first", "middle") and s >= 10:
                        stack(b + 1, s - 10)

            for h in range(6):
                stack(0, h)
            frame(0, "first")
            with sp.Fori(1, B - 1) as b:
                frame(b, "middle")
            frame(B - 1, "last")
            frame(B, "tail")

            sp.wait_ge(ffn["w1_lo"], W_CHUNKS)
            sp.dma_start(WRAW[:, :], w2_0).then_inc(s_w2raw, 16)
            sp.wait_ge(pv_done, 16 * B)
            sp.dma_start(B2_0, b2_0.partition_broadcast(P)).then_inc(s_s5raw, 16)
            sp.dma_start(B2_1, b2_1.partition_broadcast(P)).then_inc(s_s5raw, 16)
            for dst, src in ((B_ST, b_st), (B_SW, b_sw), (C_ST, c_st), (C_SW, c_sw)):
                sp.dma_start(dst, src).then_inc(s_s5raw, 16)
            sp.dma_start(RAW1, w1_1).then_inc(s_raw1, 16)
            sp.dma_start(RAW2, w2_1).then_inc(s_raw1, 16)
            ov = out.rearrange("b (t p) d -> p (b t) d", p=P)
            for b in range(B):
                sp.wait_ge(ffn["down_free"], 2 * (B + b + 1))
                sp.dma_start(ov[:, b * TT:(b + 1) * TT, :], X[:, b * TT:(b + 1) * TT, :]).then_inc(s_out, 16)
            sp.wait_ge(s_out, 16 * B)

        @block.gpsimd
        def _(pool):
            g = nc.gpsimd
            g.memset(IDENT[:, :], 0.0).then_inc(pool_chain, 1)
            g.memset(MINUS_HALF[:, :], -0.5)
            pool.wait_ge(pool_chain, 1)
            g.affine_select(out=IDENT[:, :], in_=IDENT[:, :], compare_op=ALU.not_equal, fill=1.0, base=0,
                            pattern=[[-1, P]], channel_multiplier=1).then_inc(ident_ready, 1)
            pool.wait_ge(ident_ready, 1)
            g.memset(ROWS[0:1, :], 0.0).then_inc(const_ready, 1)
            pool.wait_ge(const_ready, 1)
            g.memset(ROWS[32:33, :], 1.0).then_inc(const_ready, 1)
            pool.wait_ge(const_ready, 2)

            chain = [1]

            def link(op):
                chain[0] += 1
                op.then_inc(pool_chain, 1)
                pool.wait_ge(pool_chain, chain[0])

            def over_b(name):
                return vecs_of(name).unsqueeze(2).to_broadcast([P, KT, B])

            def mt(t):
                return MT[:, t:t + KT, :]

            ln_rstd_pool(pool, LN_ATT)
            pool.wait_ge(mt_ready, 1)
            pool.wait_ge(s_small, 32)

            def affine(ln, scale, shift, w, bias):
                link(g.tensor_scalar(ONE_S[:, :, :], mt(scale), 1.0, None, ALU.add))
                link(g.tensor_tensor(AB[:, ln, 0, :, :], ONE_S[:, :, :], over_b(w), ALU.mult))
                link(g.tensor_tensor(AB[:, ln, 1, :, :], ONE_S[:, :, :], over_b(bias), ALU.mult))
                return g.tensor_tensor(AB[:, ln, 1, :, :], AB[:, ln, 1, :, :], mt(shift), ALU.add)

            affine(0, M_SCALE0, M_SHIFT0, "ln1_w", "ln1_b").then_inc(ab_ready, 1)
            g.memset(VA[:, :, :, :, HD:2 * HD].rearrange("p o t h d -> p (o t h) d"), 1.0).then_inc(const_ready, 1)

            def dup_turn(t, o):
                alone(pool, misc_free, t + 1)
                g.tensor_copy(SRCK[:, o, 2, :], SRCK[:, o, 0, :].bitcast(F32)).then_inc(src_dup, 1)

            def va_fill(o):
                for tt in range(TT):
                    op = g.tensor_copy(VA[:, o, tt, :, 0:HD],
                                       VS[:, tt, o * P:(o + 1) * P].rearrange("p (h d) -> p h d", h=8))
                op.then_inc(va_ready, 1)

            cols = {}

            def col(name):
                cols.setdefault(name, len(cols))
                assert len(cols) <= MAG_COL
                return SC[:, cols[name]:cols[name] + 1]

            def ts(dst, src, s1, op0, s2=None, op1=ALU.bypass):
                link(g.tensor_scalar(dst, src, s1, s2, op0, op1) if s2 is not None
                     else g.tensor_scalar(dst, src, s1, None, op0))

            def tt_(dst, a, b_, op):
                link(g.tensor_tensor(dst, a, b_, op))

            ROUND = 1.5 * 2.0 ** 23

            def nearest(dst, src, factor, offset=0.0):
                ts(dst, src, factor, ALU.mult, offset, ALU.add)
                ts(dst, dst, ROUND, ALU.add)
                ts(dst, dst, ROUND, ALU.subtract)

            def horner(dst, r, coefficients):
                ts(dst, r, coefficients[0], ALU.mult, coefficients[1], ALU.add)
                for c in coefficients[2:]:
                    ts(dst, dst, r, ALU.mult, c, ALU.add)

            def exp_(dst, src):
                n, r, t = col("n"), col("r"), col("t")
                nearest(n, src, 1.0 / math.log(2.0))
                ts(n, n, -126.0, ALU.max, 127.0, ALU.min)
                ts(t, n, -0.693359375, ALU.mult)
                tt_(r, src, t, ALU.add)
                ts(t, n, 2.12194440e-4, ALU.mult)
                tt_(r, r, t, ALU.add)
                horner(t, r, [1.0 / math.factorial(k) for k in range(8, -1, -1)])
                ts(col("bits").bitcast(I32), n, 127.0, ALU.add, 2.0 ** 23, ALU.mult)
                tt_(dst, t, col("bits"), ALU.mult)

            def lambda_bar():
                lre, lim = vec("lam_re", 0), vec("lam_im", 0)
                dt, mag, th = col("dt"), col("mag"), col("th")
                exp_(dt, vec("log_step", 0))
                tt_(th, lre, dt, ALU.mult)
                exp_(mag, th)
                tt_(th, lim, dt, ALU.mult)
                n, r, t, r2, si, co = col("n"), col("r"), col("t"), col("r2"), col("si"), col("co")
                nearest(n, th, 2.0 / math.pi)
                ts(t, n, -1.5703125, ALU.mult)
                tt_(r, th, t, ALU.add)
                ts(t, n, -4.837512969970703125e-4, ALU.mult)
                tt_(r, r, t, ALU.add)
                ts(t, n, -7.54978995489188216e-8, ALU.mult)
                tt_(r, r, t, ALU.add)
                tt_(r2, r, r, ALU.mult)
                horner(si, r2, [(-1.0) ** k / math.factorial(2 * k + 1) for k in range(5, -1, -1)])
                tt_(si, si, r, ALU.mult)
                horner(co, r2, [(-1.0) ** k / math.factorial(2 * k) for k in range(6, -1, -1)])
                m, is1, is3, odd = col("m"), col("is1"), col("is3"), col("odd")
                nearest(m, n, 0.25, -0.375)
                ts(m, m, -4.0, ALU.mult)
                tt_(m, m, n, ALU.add)
                ts(is1, m, 1.0, ALU.is_equal)
                ts(is3, m, 3.0, ALU.is_equal)
                tt_(odd, is1, is3, ALU.add)
                even, sg_s, sg_c = col("even"), col("sg_s"), col("sg_c")
                ts(even, odd, -1.0, ALU.mult, 1.0, ALU.add)
                ts(sg_s, m, 2.0, ALU.is_ge, -2.0, ALU.mult)
                ts(sg_s, sg_s, 1.0, ALU.add)
                ts(sg_c, m, 2.0, ALU.is_equal)
                tt_(sg_c, sg_c, is1, ALU.add)
                ts(sg_c, sg_c, -2.0, ALU.mult, 1.0, ALU.add)
                sin, cos = col("sin"), col("cos")
                tt_(sin, si, even, ALU.mult)
                tt_(t, co, odd, ALU.mult)
                tt_(sin, sin, t, ALU.add)
                tt_(sin, sin, sg_s, ALU.mult)
                tt_(cos, co, even, ALU.mult)
                tt_(t, si, odd, ALU.mult)
                tt_(cos, cos, t, ALU.add)
                tt_(cos, cos, sg_c, ALU.mult)

            def state_tables():
                lre, lim = vec("lam_re", 0), vec("lam_im", 0)
                mag, cos, sin, r2, t = col("mag"), col("cos"), col("sin"), col("r2"), col("t")
                lb_re, lb_im, cr, ci = col("lb_re"), col("lb_im"), col("cr"), col("ci")
                tt_(lb_re, mag, cos, ALU.mult)
                ts(lb_re, lb_re, 1.0, ALU.subtract)
                tt_(lb_im, mag, sin, ALU.mult)
                tt_(cr, lb_re, lre, ALU.mult)
                tt_(t, lb_im, lim, ALU.mult)
                tt_(cr, cr, t, ALU.add)
                tt_(ci, lb_im, lre, ALU.mult)
                tt_(t, lb_re, lim, ALU.mult)
                tt_(ci, ci, t, ALU.subtract)
                tt_(r2, lre, lre, ALU.mult)
                tt_(t, lim, lim, ALU.mult)
                tt_(r2, r2, t, ALU.add)
                link(g.memset(t, -1.0))
                tt_(r2, r2, t, ALU.pow)
                tt_(cr, cr, r2, ALU.mult)
                tt_(ci, ci, r2, ALU.mult)
                sgn, nci, scr, s2 = col("sgn"), col("nci"), col("scr"), col("s2")
                link(g.memset(sgn[0:NS, :], 1.0))
                link(g.memset(sgn[NS:P, :], -1.0))
                tt_(nci, sgn, ci, ALU.mult)
                ts(nci, nci, -1.0, ALU.mult)
                tt_(scr, sgn, cr, ALU.mult)
                ts(s2, sgn, 2.0, ALU.mult)
                link(g.memset(TAB_C[:, 0:1], 1.0))
                link(g.memset(TAB_S[:, 0:1], 0.0))
                wc, ws = col("wc"), col("ws")
                link(g.tensor_copy(wc, cos))
                link(g.tensor_copy(ws, sin))
                n_ = 1
                while n_ < S:
                    lo, hi = slice(0, n_), slice(n_, 2 * n_)
                    ts(TAB_C[:, hi], TAB_C[:, lo], wc, ALU.mult)
                    ts(PART[:, lo], TAB_S[:, lo], ws, ALU.mult)
                    tt_(TAB_C[:, hi], TAB_C[:, hi], PART[:, lo], ALU.subtract)
                    ts(TAB_S[:, hi], TAB_S[:, lo], wc, ALU.mult)
                    ts(PART[:, lo], TAB_C[:, lo], ws, ALU.mult)
                    tt_(TAB_S[:, hi], TAB_S[:, hi], PART[:, lo], ALU.add)
                    if 2 * n_ < S:
                        tt_(t, ws, ws, ALU.mult)
                        tt_(r2, wc, ws, ALU.mult)
                        tt_(wc, wc, wc, ALU.mult)
                        tt_(wc, wc, t, ALU.subtract)
                        ts(ws, r2, 2.0, ALU.mult)
                    n_ *= 2
                g.tensor_copy(SC[:, MAG_COL:MAG_COL + 1], mag).then_inc(s5_tables, 1)

            def state_inputs():
                cr, ci, nci, scr, s2 = col("cr"), col("ci"), col("nci"), col("scr"), col("s2")
                pool.wait_ge(s_s5raw, 16 * 6)
                ts(BB[:, 0, :], B_ST, cr, ALU.mult)
                ts(PART[:, :], B_SW, nci, ALU.mult)
                tt_(BB[:, 0, :], BB[:, 0, :], PART[:, :], ALU.add)
                ts(BB[:, 1, :], B_ST, ci, ALU.mult)
                ts(PART[:, :], B_SW, scr, ALU.mult)
                g.tensor_tensor(BB[:, 1, :], BB[:, 1, :], PART[:, :], ALU.add).then_inc(s5_inputs, 1)
                ts(WC[:, 0, :], C_ST, s2, ALU.mult)
                ts(WC[:, 1, :], C_SW, -2.0, ALU.mult)

            def frame(b, kind):
                turns = numbered(b, kind)
                for s in range(16):
                    if kind in ("first", "middle") and s == 0:
                        ln_rstd_pool(pool, LN_ATT + 1 + b)
                    for t, what, bb, i in turns[s]:
                        if what == "K":
                            dup_turn(t, i)
                        if what == "V" and i == 1 and kind == "first" and s == 1:
                            alone(pool, misc_free, t + 1)
                            pool.wait_ge(const_ready, 3)
                            va_fill(0)
                            va_fill(1)
                    if kind != "first" and kind != "tail" and s == 1:
                        alone(pool, pv_done, b * 16 - 8)
                        va_fill(0)
                    if kind != "first" and kind != "tail" and s == 7:
                        alone(pool, pv_done, b * 16)
                        va_fill(1)
                    if kind == "first" and s == 7:
                        lambda_bar()
                    if kind == "last" and s == 7:
                        state_tables()
                    if kind == "middle" or kind == "last" or kind == "first":
                        if s == 3:
                            alone(pool, ln_xhat, b + 1)
                            g.tensor_tensor(x_batch(b), x_batch(b), BO[:, :].unsqueeze(1).to_broadcast([P, TT, D]),
                                            ALU.add).then_inc(x_bias, 1)

            dup_turn(3, 0)
            pool.wait_ge(s_rows, 80)
            pool.wait_ge(mt_ready, 4)
            link(affine(1, M_SCALE1, M_SHIFT1, "ln2_w", "ln2_b"))
            g.tensor_scalar(AB[:, 2, 0, :, :], mt(M_SCALE2), 1.0, None, ALU.add)
            g.tensor_copy(AB[:, 2, 1, :, :], mt(M_SHIFT2))
            g.tensor_tensor(DG[:, :, :], mt(M_GATE_A), over_b("d_diag"), ALU.mult)
            link(g.tensor_scalar(ONE_S[:, :, :], mt(M_SCALEF), 1.0, None, ALU.add))
            link(g.tensor_scalar(AB[:, 3, 0, :, :], mt(M_SCALEC), 1.0, None, ALU.add))
            link(g.tensor_tensor(AB[:, 3, 0, :, :], AB[:, 3, 0, :, :], ONE_S[:, :, :], ALU.mult))
            link(g.tensor_tensor(AB[:, 3, 1, :, :], mt(M_SHIFTC), ONE_S[:, :, :], ALU.mult))
            g.tensor_tensor(AB[:, 3, 1, :, :], AB[:, 3, 1, :, :], mt(M_SHIFTF), ALU.add).then_inc(ab_ready, 1)

            frame(0, "first")
            with pool.Fori(1, B - 1) as b:
                frame(b, "middle")
            frame(B - 1, "last")

            ln_rstd_pool(pool, LN_FFN)

            def gated_weights(j):
                for i in range(2):
                    g.tensor_tensor(WGF[:, i, :], WC[:, i, :],
                                    GATE_A[:, bass.ds(j, 1), :].rearrange("p a n -> p (a n)"),
                                    ALU.mult).then_inc(s5["wgf"], 1)
                for k in range(KT):
                    g.tensor_tensor(DGF[:, k, :], IDENT[:, :], DG[:, k, bass.ds(j, 1)].to_broadcast([P, P]),
                                    ALU.mult).then_inc(s5["wgf"], 1)

            def output_bias(f, layer):
                b = ffn_batch(f, layer)
                bias = B2_0
                if layer == 1:
                    g.tensor_tensor(GB2, GATE_F[:, bass.ds(b, 1), :].rearrange("p a n -> p (a n)"), B2_1,
                                    ALU.mult).then_inc(gb2_ready, 1)
                    pool.wait_ge(gb2_ready, b + 1)
                    bias = GB2
                g.tensor_tensor(x_batch(b), x_batch(b), bias.unsqueeze(1).to_broadcast([P, TT, D]),
                                ALU.add).then_inc(x_bias, 1)

            def ffn_frame(f, layer, with_s5, with_next, next_s5):
                if with_s5:
                    ln_rstd_pool(pool, norm_s5(f))
                    gated_weights(f - 1)
                else:
                    alone(pool, ln_xhat, f + (LN_FFN + 1 + B * layer))
                if isinstance(f, int) and f == 0:
                    pool.wait_ge(s_s5raw, 16 * 6)
                output_bias(f, layer)
                if with_next:
                    ln_rstd_pool(pool, norm_next(f, with_s5))
                if isinstance(f, int) and f == 0:
                    pool.wait_ge(misc_free, ALL_TURNS)
                    state_inputs()
                if with_s5:
                    alone(pool, s5["t2"], f)
                    g.tensor_tensor(ROT, T1, T2, ALU.add).then_inc(s5["rot"], 1)

            ffn_frames(pool, ffn_frame)

        @block.scalar
        def _(act):
            a = nc.scalar
            act.wait_ge(s_wq, 16)
            a.activation(WQ[:, 0:1536], WRAW[:, 0:1536], ACT.Copy).then_inc(wq_hi, 1)

            def mrow_out_copies(chunks):
                for c in chunks:
                    j = c // 2
                    op = a.activation(MROW[32 * j:32 * j + B, c % 2, :], bank[c % 2][32 * j:32 * j + B, 0:384], ACT.Copy)
                op.then_inc(mrow_out, 1)

            act.wait_ge(mrow_mm, 1)
            mrow_out_copies((0, 1))

            def turn(t, what, b, i):
                if what == "LT":
                    act.wait_ge(misc_full, t + 1)
                    if positive(b):
                        act.wait_ge(xn_ready, 2 * b + (i - 1))
                    a.activation(XNF[:, i, :], MISC, ACT.Identity, bias=ab(0, 1, i, b), scale=ab(0, 0, i, b))\
                        .then_inc(misc_free, 1)
                if what in ("Q", "K"):
                    act.wait_ge(misc_full, t + 1)
                    if positive(b) and what == "Q":
                        act.wait_ge(s1_full, 32 * b + (16 * i + 10 - 32))
                        for h in range(8 * i + 5, 8 * i + 8):
                            act.wait_ge(stack_ready[h], 64 * b)
                    src, bias = (SRCQ, "bq") if what == "Q" else (SRCK, "bk")
                    a.activation(src[:, i, 0, :], MISC, ACT.Identity, bias=vec(bias, i)).then_inc(src_hi, 1)
                if what == "MX":
                    act.wait_ge(misc_full, t + 1)
                    if positive(b):
                        act.wait_ge(negmax_ready[i], 32 * b)
                    a.activation(NEGMX[:, i, 0, :], MISC[0:16, 0:P], ACT.Copy, scale=-1.0).then_inc(mx_hi, 1)
                if what == "OB":
                    act.wait_ge(misc_full, t + 1)
                    a.activation(OF[:, i, :], MISC, ACT.Copy).then_inc(misc_free, 1)

            act.wait_ge(ab_ready, 1)
            turn(0, "LT", 0, 0)
            turn(1, "LT", 0, 1)
            turn(2, "Q", 0, 0)
            turn(3, "K", 0, 0)
            act.wait_ge(mrow_mm, 2)
            mrow_out_copies(range(2, 8))

            def exps(b, s, js):
                g = 16 * b + (s - LAG)
                kt = (s - LAG) % 4
                for j in js:
                    act.wait_ge(s2_full, 4 * g + (j + 1))
                    if j == 0 and not (isinstance(g, int) and g < 4):
                        act.wait_ge(pv_done, g - 3)
                    a.activation(PTV[:, kt, j, :], bank[4 + j % 2], ACT.Exp, scale=SCALE).then_inc(exp_done, 1)

            def xnf_out(f, layer):
                ln, b = (1, 3)[layer], ffn_batch(f, layer)
                for k in range(KT):
                    act.wait_ge(ffn["t_full"], 2 * f + (k + 1))
                    act.wait_ge(xn_ready, 2 * f + (2 * B + k - 1))
                    a.activation(XNF[:, k, :], bank[T_BANK + k], ACT.Identity, bias=ab(ln, 1, k, b),
                                 scale=ab(ln, 0, k, b)).then_inc(ffn["xnf"], 1)

            def frame(b, kind):
                turns = numbered(b, kind)
                for s in range(16 if kind != "tail" else LAG + 1):
                    has_p2 = (kind != "first" or s >= LAG) and (kind != "tail" or s < LAG)
                    if has_p2:
                        exps(b, s, (0, 1))
                    for one in turns[s][0:1]:
                        turn(*one)
                    if has_p2:
                        exps(b, s, (2, 3))
                    for one in turns[s][1:]:
                        turn(*one)
                    done = s - LAG - 1
                    if (kind != "first" or done >= 0) and (kind != "tail" or done < 0) and done % 4 == 3:
                        q = (done // 4) % 4
                        act.wait_ge(pv_done, 16 * b + (done + 1))
                        a.activation(OR[:, q % 2, :], PV, ACT.Copy).then_inc(pv_evac, 1)
                    if kind == "tail" and s == LAG:
                        xnf_out(0, 0)

            frame(0, "first")
            with act.Fori(1, B - 1) as b:
                frame(b, "middle")
            frame(B - 1, "last")
            frame(B, "tail")

            TAIL = numbered(B, "tail")

            def tail_hook(ft):
                for one in TAIL[LAG + 1 + ft] if ft < 5 else []:
                    turn(*one)

            def ffn_frame(f, layer, with_s5, with_next, next_s5):
                n = ffn
                j = f - 1
                new_layer = isinstance(f, int) and f == B - 1
                for ft in range(FT):
                    act.wait_ge(n["up_full"], FT * f + (ft + 1))
                    if positive(f) or ft >= 2:
                        act.wait_ge(n["h_lo"], FT * f + (ft - 1))
                    func, b1 = ((ACT.Gelu, "b1_0"), (ACT.Gelu_apprx_tanh, "b1_1"))[layer]
                    a.activation(HF[:, ft % 2, :], bank[UP_BANK + ft % 2], func, bias=vec(b1, ft))
                    if positive(f):
                        if ft < FT - 1:
                            act.wait_ge(n["down_ft"], (FT - 1) * f + (ft + 2 - FT))
                        else:
                            act.wait_ge(n["down_full"], 2 * f)
                    a.activation(HH[:, ft, :], bank[UP_BANK + ft % 2], func, bias=vec(b1, ft)).then_inc(n["h_hi"], 1)
                    if isinstance(f, int) and f == 0:
                        tail_hook(ft)
                    if with_s5 and ft == 2:
                        for k in range(KT):
                            act.wait_ge(s5["t_full"], 2 * j + (k + 1))
                            a.activation(XNF2[:, k, :], bank[T_BANK + k], ACT.Identity, bias=ab(2, 1, k, j),
                                         scale=ab(2, 0, k, j)).then_inc(s5["xnf"], 1)
                    if with_s5 and ft == 3:
                        act.wait_ge(s5["wgf"], 4 * j + 4)
                        a.activation(WG[:, 0, :, :], WGF[:, :, :], ACT.Copy).then_inc(s5["wg_hi"], 1)
                        a.activation(DGP[:, 0, :, :], DGF[:, :, :], ACT.Copy).then_inc(s5["wg_hi"], 1)
                    if with_s5 and ft == 5:
                        for m in range(2):
                            act.wait_ge(s5["cyf"], 2 * j + (m + 1))
                            a.activation(CYP[:, m, 0, :], CYF[:, m, :], ACT.Copy).then_inc(s5["cy_hi"], 1)
                    if with_next and ft == (7 if with_s5 else 5):
                        xnf_out(f + 1, 1 if new_layer else layer)
                if new_layer:
                    act.wait_ge(s_raw1, 32)
                    act.wait_ge(n["up_full"], FT * B)
                    for c in range(W_CHUNKS):
                        at = slice(c * WN * P, (c + 1) * WN * P)
                        a.activation(W1P[:, 0, :, at], RAW1.rearrange("p (k n) -> p k n", k=KT)[:, :, at], ACT.Copy)\
                            .then_inc(n["w1_hi"], 1)
                if new_layer:
                    act.wait_ge(n["down_full"], 2 * B)
                    for c in range(W_CHUNKS):
                        at = slice(c * WN, (c + 1) * WN)
                        a.activation(W2P[:, 0, at, :], RAW2.rearrange("p (f n) -> p f n", f=FT)[:, at, :], ACT.Copy)\
                            .then_inc(n["w2_hi"], 1)
                if isinstance(f, int) and f == 0:
                    act.wait_ge(s5["bb_t"], 1)
                    a.activation(BBT[:, :, :], MISC.rearrange("p (m n) -> p m n", m=4), ACT.Copy)\
                        .then_inc(s5["bbt"], 1)
                    act.wait_ge(s5["bbt"], 1)
                    a.activation(WB[:, 0, :, :], BBT[:, :, :], ACT.Copy).then_inc(s5["wb_hi"], 1)

            ffn_frames(act, ffn_frame)

        @block.vector
        def _(dve):
            v = nc.vector
            dve.wait_ge(s_x[0], 16)
            ln_stats_dve(dve, LN_ATT, 0)
            dve.wait_ge(wq_hi, 1)
            v.tensor_tensor(WQ[:, 1536:3072], WRAW[:, 0:1536], WQ[:, 0:1536].bitcast(F32), ALU.subtract)\
                .then_inc(wq_lo, 1)
            ln_xhat_dve(dve, LN_ATT, 0)

            def mt_out(j):
                t0, t1 = 6 * j, 6 * j + 6
                dve.wait_ge(mt_mm, j + 1)
                v.tensor_tensor(MT[:, t0:t1, :], bank[2 + j][:, t0 * B:t1 * B].rearrange("p (t b) -> p t b", b=B),
                                VEC_SB[:, VEC["bmod"][0] + t0:VEC["bmod"][0] + t1].unsqueeze(2)
                                .to_broadcast([P, t1 - t0, B]), ALU.add).then_inc(mt_ready, 1)

            dve.wait_ge(s_small, 32)
            mt_out(0)

            def turn(t, what, b, i):
                if what == "LT":
                    dve.wait_ge(misc_free, t + 1)
                    xn_split_dve(dve, b, i, XNF, xn_part, xn_hi, xn_ready)
                    return
                dve.wait_ge(misc_full, t + 1)
                if what in ("Q", "K"):
                    src, bias, second = (SRCQ, "bq", 0) if what == "Q" else (SRCK, "bk", 1)
                    dve.wait_ge(src_hi, 4 * b + (2 * i + second + 1))
                    v.scalar_tensor_tensor(src[:, i, 1, :], MISC, vec(bias, i), src[:, i, 0, :].bitcast(F32),
                                           ALU.add, ALU.subtract).then_inc(misc_free, 1)
                if what == "V":
                    if positive(b):
                        dve.wait_ge(va_ready, 2 * b)
                    v.tensor_tensor(VS[:, 2 * i:2 * i + 2, :], MISC.rearrange("p (a n) -> p a n", a=2),
                                    BV[:, :].unsqueeze(1).to_broadcast([P, 2, D]), ALU.add).then_inc(misc_free, 1)
                if what == "MX":
                    dve.wait_ge(mx_hi, QUADS * b + (i + 1))
                    v.scalar_tensor_tensor(NEGMX[:, i, 1, :], MISC[0:16, 0:P], -1.0,
                                           NEGMX[:, i, 0, :].bitcast(F32), ALU.mult, ALU.subtract)\
                        .then_inc(misc_free, 1)
                if what == "OT":
                    o = MISC.rearrange("p (t j c) -> p t j c", t=TT, j=4)
                    v.reciprocal(RC[:, :].rearrange("p (t j) -> p t j", t=TT), o[:, :, :, HD]).then_inc(rc_ready, 1)
                    dve.wait_ge(rc_ready, QUADS * b + (i + 1))
                    v.tensor_tensor(OTK[:, :, 64 * i:64 * i + 64].rearrange("p t (j d) -> p t j d", j=4),
                                    o[:, :, :, 0:HD],
                                    RC[:, :].rearrange("p (t j) -> p t j", t=TT).unsqueeze(3)
                                    .to_broadcast([P, TT, 4, HD]), ALU.mult).then_inc(misc_free, 1)
                if what == "WO":
                    dve.wait_ge(x_bias, b + 1)
                    v.tensor_tensor(x_pair(b, i), x_pair(b, i), MISC.rearrange("p (a n) -> p a n", a=2), ALU.add)\
                        .then_inc(misc_free, 1)

            turn(0, "LT", 0, 0)
            turn(1, "LT", 0, 1)
            turn(2, "Q", 0, 0)
            turn(3, "K", 0, 0)
            for j in range(1, 4):
                mt_out(j)
            dve.wait_ge(s_rows, 80)
            for gi, gate in enumerate((GATE_A, GATE_F)):
                for bp in range(2):
                    dve.wait_ge(gate_mm, 2 * gi + bp + 1)
                    v.tensor_tensor(gate[:, 2 * bp:2 * bp + 2, :],
                                    bank[(2 * gi + bp)].rearrange("p (a n) -> p a n", a=2),
                                    BG[:, gi, :].unsqueeze(1).to_broadcast([P, 2, D]), ALU.add).then_inc(gate_ready, 1)

            def row_max(b, s, half):
                n = 32 * b + (2 * s + half)
                dve.wait_ge(s1_full, n + 1)
                v.reduce_max(MX[:, (s // 4) % 2, s % 4, 2 * half:2 * half + 2], PS1[:, 2 * half:2 * half + 2, :],
                             AX_X).then_inc(s1_free, 1)

            def copy_hi(to, raw):
                return v.tensor_copy(to, raw)

            def lo_of(to, raw, hi):
                return v.tensor_tensor(to, raw, hi.bitcast(F32), ALU.subtract)

            def w1_lo(layer, raw, with_hi):
                for c in range(W_CHUNKS):
                    at, k_n = slice(c * WN * P, (c + 1) * WN * P), raw.rearrange("p (k n) -> p k n", k=KT)
                    if with_hi:
                        copy_hi(W1P[:, 0, :, at], k_n[:, :, at]).then_inc(ffn["w1_hi"], 1)
                    dve.wait_ge(ffn["w1_hi"], W_CHUNKS * layer + c + 1)
                    lo_of(W1P[:, 1, :, at], k_n[:, :, at], W1P[:, 0, :, at]).then_inc(ffn["w1_lo"], 1)

            def w2_lo(layer, raw, with_hi):
                for c in range(W_CHUNKS):
                    at, f_n = slice(c * WN, (c + 1) * WN), raw.rearrange("p (f n) -> p f n", f=FT)
                    if with_hi:
                        copy_hi(W2P[:, 0, at, :], f_n[:, at, :]).then_inc(ffn["w2_hi"], 1)
                    dve.wait_ge(ffn["w2_hi"], W_CHUNKS * layer + c + 1)
                    lo_of(W2P[:, 1, at, :], f_n[:, at, :], W2P[:, 0, at, :]).then_inc(ffn["w2_lo"], 1)

            def xn_split(f):
                for k in range(KT):
                    dve.wait_ge(ffn["xnf"], 2 * f + (k + 1))
                    xn_split_dve(dve, f + B, k, XNF, xn_part, xn_hi, xn_ready)

            def frame(b, kind):
                turns = numbered(b, kind)
                for s in range(16 if kind != "tail" else LAG + 1):
                    if kind != "tail":
                        row_max(b, s, 0)
                    for one in turns[s][0:1]:
                        turn(*one)
                    if kind != "tail":
                        row_max(b, s, 1)
                    for one in turns[s][1:]:
                        turn(*one)
                    if kind in ("first", "middle") and s == 0:
                        if kind == "first":
                            dve.wait_ge(s_x[1], 16)
                            dve.wait_ge(s_x[2], 16)
                            dve.wait_ge(s_x[3], 16)
                        ln_stats_dve(dve, b + (LN_ATT + 1), b + 1)
                    if kind in ("first", "middle") and s == 1:
                        ln_xhat_dve(dve, b + (LN_ATT + 1), b + 1)
                    if kind == "tail" and s == 0:
                        dve.wait_ge(misc_free, turn_base(B))
                        ln_stats_dve(dve, LN_FFN, 0)
                        dve.wait_ge(s_w1raw, 16)
                        dve.wait_ge(exp_done, 64 * (B - 1) + 32)
                        w1_lo(0, WRAW[:, :], True)
                        ln_xhat_dve(dve, LN_FFN, 0)

            frame(0, "first")
            with dve.Fori(1, B - 1) as b:
                frame(b, "middle")
            frame(B - 1, "last")
            frame(B, "tail")
            dve.wait_ge(s_w2raw, 16)
            w2_lo(0, WRAW[:, :], True)
            xn_split(0)

            TAIL = numbered(B, "tail")
            mag = SC[:, MAG_COL:MAG_COL + 1]

            def tail_hook(ft):
                for one in TAIL[LAG + 1 + ft] if ft < 5 else []:
                    turn(*one)
                if ft == 5:
                    dve.wait_ge(misc_free, ALL_TURNS)

            def s5_step(f, ft):
                j = f - 1
                if ft == 0:
                    dve.wait_ge(ffn["t_full"], 2 * f + 2)
                    ln_xhat_dve(dve, norm_s5(f), j)
                if ft == 2:
                    for k in range(KT):
                        dve.wait_ge(s5["xnf"], 2 * j + (k + 1))
                        xn_split_dve(dve, j, k, XNF2, xn2_part, s5["xn_hi"], s5["xn_ready"])
                if ft == 4:
                    dve.wait_ge(s5["bu_full"], 2 * j + 1)
                    v.tensor_tensor(T1, bank[S5_BANK], TAB_C, ALU.mult).then_inc(s5["t1"], 1)
                    dve.wait_ge(s5["bu_full"], 2 * j + 2)
                    v.tensor_tensor(T2, bank[S5_BANK + 1], TAB_S, ALU.mult).then_inc(s5["t2"], 1)
                    dve.wait_ge(s5["wg_hi"], 2 * j + 2)
                    lo_of(WG[:, 1, :, :], WGF[:, :, :], WG[:, 0, :, :]).then_inc(s5["wg_lo"], 1)
                    lo_of(DGP[:, 1, :, :], DGF[:, :, :], DGP[:, 0, :, :]).then_inc(s5["wg_lo"], 1)
                if ft == 5:
                    dve.wait_ge(s5["rot"], j + 1)
                    v.tensor_tensor_scan(STATE, mag.to_broadcast([P, S]), ROT, 0.0, ALU.mult, ALU.add)\
                        .then_inc(s5["scan"], 1)
                    dve.wait_ge(s5["scan"], j + 1)
                    v.tensor_tensor(CYF[:, 0, :], STATE, TAB_C, ALU.mult).then_inc(s5["cyf"], 1)
                    v.tensor_tensor(CYF[:, 1, :], STATE, TAB_S, ALU.mult).then_inc(s5["cyf"], 1)
                if ft == 6:
                    for m in range(2):
                        dve.wait_ge(s5["cy_hi"], 2 * j + (m + 1))
                        lo_of(CYP[:, m, 1, :], CYF[:, m, :], CYP[:, m, 0, :]).then_inc(s5["cy_lo"], 1)

            def residual(f, layer):
                b = ffn_batch(f, layer)
                dve.wait_ge(x_bias, f + (B + 1))
                for p in range(2):
                    dve.wait_ge(ffn["down_full"], 2 * f + (p + 1))
                    product = bank[DOWN_BANK + p].rearrange("p (a n) -> p a n", a=2)
                    if layer == 1:
                        v.tensor_tensor(TMP[:, p, :, :], product, GATE_F[:, bass.ds(b, 1), :].to_broadcast([P, 2, D]),
                                        ALU.mult).then_inc(ffn["gated"], 1)
                        dve.wait_ge(ffn["gated"], 2 * b + (p + 1))
                        product = TMP[:, p, :, :]
                    v.tensor_tensor(x_pair(b, p), x_pair(b, p), product, ALU.add).then_inc(ffn["down_free"], 1)

            def ffn_frame(f, layer, with_s5, with_next, next_s5):
                for ft in range(FT):
                    dve.wait_ge(ffn["h_hi"], FT * f + (ft + 1))
                    lo_of(HL[:, ft, :], HF[:, ft % 2, :], HH[:, ft, :]).then_inc(ffn["h_lo"], 1)
                    if isinstance(f, int) and f == 0:
                        tail_hook(ft)
                    if with_s5:
                        s5_step(f, ft)
                    if with_next and ft == 1:
                        next_layer = 1 if layer == 1 or (isinstance(f, int) and f == B - 1) else 0
                        if next_layer == 1:
                            alone(dve, s5["out_free"], 2 * f + 2 * (2 - B))
                        ln_stats_dve(dve, norm_next(f, with_s5), ffn_batch(f + 1, next_layer))
                    if with_next and ft == 3:
                        if with_s5:
                            dve.wait_ge(s5["t_full"], 2 * f)
                        else:
                            dve.wait_ge(ffn["t_full"], 2 * f + 2)
                        ln_xhat_dve(dve, norm_next(f, with_s5), ffn_batch(f + 1, next_layer))
                if with_next:
                    xn_split(f + 1)
                new_layer = isinstance(f, int) and f == B - 1
                if new_layer:
                    w1_lo(1, RAW1, False)
                residual(f, layer)
                if next_s5:
                    alone(dve, ffn["down_free"], 2 * f + 2)
                    ln_stats_dve(dve, norm_s5(f + 1), f)
                if with_s5:
                    j = f - 1
                    for p in range(2):
                        dve.wait_ge(s5["out_full"], 2 * j + (p + 1))
                        v.tensor_tensor(x_pair(j, p), x_pair(j, p),
                                        bank[S5_BANK + p].rearrange("p (a n) -> p a n", a=2), ALU.add)\
                            .then_inc(s5["out_free"], 1)
                if new_layer:
                    w2_lo(1, RAW2, False)
                if isinstance(f, int) and f == 0:
                    dve.wait_ge(s5["wb_hi"], 1)
                    lo_of(WB[:, 1, :, :], BBT[:, :, :], WB[:, 0, :, :]).then_inc(s5["wb_lo"], 1)
                    dve.wait_ge(s5_tables, 1)

            ffn_frames(dve, ffn_frame)

        @block.tensor
        def _(pe):
            def mm(out_, lhsT, rhs, start, stop):
                return nc.tensor.matmul(out_, lhsT, rhs, start=start, stop=stop, skip_group_check=True)

            PARTS = ((0, 0), (0, 1), (1, 0))

            def parts(out_, pairs, start=True, stop=True):
                n = 0
                for left, right in pairs:
                    for p, q in PARTS:
                        op = mm(out_, left(p), right(q), start and n == 0, stop and n == 3 * len(pairs) - 1)
                        n += 1
                return op

            pe.wait_ge(ident_ready, 1)

            def mrow(chunks):
                for k in range(KT):
                    for c in chunks:
                        j = c // 2
                        op = mm(bank[c % 2][32 * j:32 * j + B, 0:384], COND[:, k, :], WMOD[:, k, 384 * c:384 * (c + 1)],
                                k == 0, k == KT - 1)
                op.then_inc(mrow_mm, 1)

            def mt_transpose(j):
                for t in range(6 * j, 6 * j + 6):
                    c = t // 3
                    rows = slice(32 * j, 32 * j + B)
                    op = nc.tensor.transpose(bank[2 + j][:, t * B:(t + 1) * B],
                                             MROW[rows, c % 2, P * (t % 3):P * (t % 3 + 1)], IDENT[rows, rows])
                op.then_inc(mt_mm, 1)

            pe.wait_ge(s_small, 32)
            pe.wait_ge(s_wmod_a, 16)
            mrow((0, 1))
            pe.wait_ge(mrow_out, 1)
            mt_transpose(0)

            def turn(t, what, b, i):
                if not (isinstance(t, int) and t == 0):
                    pe.wait_ge(misc_free, t)
                if what == "LT":
                    op = ln_transpose_pe(pe, b + LN_ATT, i, MISC)
                if what in ("Q", "K"):
                    pe.wait_ge(xn_ready, 2 * b + 2)
                    c0 = (0 if what == "Q" else D) + P * i
                    op = parts(MISC, [(lambda p, k=k: WQV[:, p, k, c0:c0 + P], lambda q, k=k: XN[:, q, k, :])
                                      for k in range(KT)])
                if what == "V":
                    for one in range(2):
                        at = (2 * i + one) * P
                        op = parts(MISC[:, D * one:D * (one + 1)],
                                   [(lambda p, k=k, at=at: XN[:, p, k, at:at + P], lambda q, k=k: WQV[:, q, k, 2 * D:3 * D])
                                    for k in range(KT)])
                if what == "MX":
                    pe.wait_ge(s1_free, 32 * b + 8 * (i + 1))
                    op = nc.tensor.transpose(MISC[0:16, 0:P], MX[:, i % 2, :, :].rearrange("p j t -> p (j t)"),
                                             IDENT[:, :])
                if what == "OT":
                    pe.wait_ge(pv_evac, QUADS * b + (i + 1))
                    for qt in range(TT):
                        op = nc.tensor.transpose(MISC[:, qt * P:(qt + 1) * P], OR[:, i % 2, qt * P:(qt + 1) * P],
                                                 IDENT[:, :])
                if what == "OB":
                    for qt in range(TT):
                        op = nc.tensor.transpose(MISC[:, qt * P:(qt + 1) * P], OTK[:, qt, i * P:(i + 1) * P],
                                                 IDENT[:, :])
                if what == "WO":
                    for one in range(2):
                        at = (2 * i + one) * P
                        for k in range(KT):
                            op = mm(MISC[:, D * one:D * (one + 1)], OF[:, k, at:at + P], WO[:, k, :],
                                    k == 0, k == KT - 1)
                op.then_inc(misc_full, 1)

            turn(0, "LT", 0, 0)
            turn(1, "LT", 0, 1)
            pe.wait_ge(wq_lo, 1)
            turn(2, "Q", 0, 0)
            turn(3, "K", 0, 0)
            pe.wait_ge(s_wmod_b, 16)
            mrow(range(2, 8))
            pe.wait_ge(mrow_out, 2)
            for j in range(1, 4):
                mt_transpose(j)
            pe.wait_ge(mt_ready, 4)
            for gi, tile in enumerate((M_GATE_A, M_GATE_F)):
                for bp in range(2):
                    for one in range(2):
                        for k in range(KT):
                            op = mm(bank[2 * gi + bp][:, D * one:D * (one + 1)],
                                    COND[:, k, 2 * bp + one:2 * bp + one + 1].to_broadcast([P, P]),
                                    WMOD[:, k, tile * P:tile * P + D], k == 0, k == KT - 1)
                    op.then_inc(gate_mm, 1)
            pe.wait_ge(gate_ready, 4)
            pe.wait_ge(s_const_rows, 64)
            pe.wait_ge(s_rows, 80)

            def scores_for_max(b, s, half):
                n = 32 * b + (2 * s + half)
                if half == 0:
                    pe.wait_ge(stack_ready[s], 64 * b + 64)
                if positive(b) or 2 * s + half >= 2:
                    pe.wait_ge(s1_free, n - 1)
                for one in range(2):
                    qt = 2 * half + one
                    op = mm(bank[qt], QS[0:P1_ROWS, s, qt * P:(qt + 1) * P], KS[0:P1_ROWS, s, :], True, True)
                op.then_inc(s1_full, 1)

            def scores_less_max(b, s, j):
                g = 16 * b + (s - LAG)
                q, kt = ((s - LAG) // 4) % 4, (s - LAG) % 4
                h = 4 * q + j
                if kt == 0 and j == 0:
                    pe.wait_ge(negmax_ready[q], 32 * b + (32 if s >= LAG else 0))
                if not (isinstance(g, int) and g == 0 and j < 2):
                    pe.wait_ge(exp_done, 4 * g + (j - 1))
                mm(bank[4 + j % 2], KS[0:P2_ROWS, h, kt * P:(kt + 1) * P], QS[0:P2_ROWS, h, :], True, True)\
                    .then_inc(s2_full, 1)

            def values(b, s):
                g = 16 * b + (s - LAG - 1)
                q, kt = ((s - LAG - 1) // 4) % 4, (s - LAG - 1) % 4
                o = q // 2
                if kt == 0:
                    if not (isinstance(g, int) and g == 0):
                        pe.wait_ge(pv_evac, QUADS * b + ((s - LAG - 1) // 4))
                    pe.wait_ge(va_ready, 2 * b + (o + 1 if s > LAG else o - 1))
                pe.wait_ge(exp_done, 4 * g + 4)
                for j in range(4):
                    op = mm(PV[32 * j:32 * (j + 1), :], VA[:, o, kt, 4 * (q % 2) + j, :], PTV[:, kt, j, :],
                            kt == 0, kt == TT - 1)
                op.then_inc(pv_done, 1)

            def transpose_norm(n, full):
                for k in range(KT):
                    ln_transpose_pe(pe, n, k, bank[T_BANK + k]).then_inc(full, 1)

            def frame(b, kind):
                turns = numbered(b, kind)
                for s in range(16 if kind != "tail" else LAG + 1):
                    has_p1 = kind != "tail"
                    has_p2 = (kind != "first" or s >= LAG) and (kind != "tail" or s < LAG)
                    has_pv = (kind != "first" or s > LAG) and (kind != "tail" or s <= LAG)
                    if has_p2:
                        scores_less_max(b, s, 0)
                    if has_p1:
                        scores_for_max(b, s, 0)
                    if has_p2:
                        scores_less_max(b, s, 1)
                    for one in turns[s][0:1]:
                        turn(*one)
                    if has_p2:
                        scores_less_max(b, s, 2)
                    if has_p1:
                        scores_for_max(b, s, 1)
                    if has_p2:
                        scores_less_max(b, s, 3)
                    if has_pv:
                        values(b, s)
                    for one in turns[s][1:]:
                        turn(*one)
                    if kind == "tail" and s == 4:
                        pe.wait_ge(s1_free, 2 * H * B)
                        transpose_norm(LN_FFN, ffn["t_full"])

            frame(0, "first")
            with pe.Fori(1, B - 1) as b:
                frame(b, "middle")
            frame(B - 1, "last")
            frame(B, "tail")

            TAIL = numbered(B, "tail")
            pe.wait_ge(exp_done, 4 * H * B)

            def up(f, layer, ft):
                if isinstance(f, int) and f % B == 0 and ft % WN == 0:
                    pe.wait_ge(ffn["w1_lo"], W_CHUNKS * layer + ft // WN + 1)
                if positive(f) or ft >= 2:
                    pe.wait_ge(ffn["h_hi"], FT * f + (ft - 1))
                parts(bank[UP_BANK + ft % 2], [(lambda p, k=k: W1P[:, p, k, ft * P:(ft + 1) * P],
                                                lambda q, k=k: XN[:, q, k, :]) for k in range(KT)])\
                    .then_inc(ffn["up_full"], 1)

            def down(f, layer, ft):
                if isinstance(f, int) and f % B == 0 and ft % WN == 0:
                    pe.wait_ge(ffn["w2_lo"], W_CHUNKS * layer + ft // WN + 1)
                pe.wait_ge(ffn["h_lo"], FT * f + (ft + 1))
                for tt in range(TT):
                    p, one = tt // 2, tt % 2
                    if ft == 0 and one == 0 and positive(f):
                        pe.wait_ge(ffn["down_free"], 2 * f + (p - 1))
                    op = parts(bank[DOWN_BANK + p][:, D * one:D * (one + 1)],
                               [(lambda q: (HH, HL)[q][:, ft, tt * P:(tt + 1) * P], lambda q: W2P[:, q, ft, :])],
                               start=ft == 0 and one == 0, stop=ft == FT - 1)
                    if ft == FT - 1 and one == 1:
                        op.then_inc(ffn["down_full"], 1)
                if ft < FT - 1:
                    op.then_inc(ffn["down_ft"], 1)

            def s5_inputs_pe(j):
                pe.wait_ge(s5["wb_lo"], 1)
                pe.wait_ge(s5["xn_ready"], 2 * j + 2)
                for m in range(2):
                    parts(bank[S5_BANK + m], [(lambda p, k=k: WB[:, p, 2 * m + k, :], lambda q, k=k: XN2[:, k, q, :])
                                              for k in range(KT)]).then_inc(s5["bu_full"], 1)

            def s5_outputs_pe(j):
                pe.wait_ge(s5["wg_lo"], 2 * j + 2)
                pe.wait_ge(s5["cy_lo"], 2 * j + 2)
                for tt in range(TT):
                    at, into = slice(tt * P, (tt + 1) * P), bank[S5_BANK + tt // 2]
                    c0 = D * (tt % 2)
                    parts(into[:, c0:c0 + D], [(lambda p, m=m: CYP[:, m, p, at], lambda q, m=m: WG[:, q, m, :])
                                               for m in range(2)], stop=False)
                    for k in range(KT):
                        op = parts(into[:, c0 + k * P:c0 + (k + 1) * P],
                                   [(lambda p: XN2[:, k, p, at], lambda q: DGP[:, q, k, :])],
                                   start=False, stop=k == KT - 1)
                    if tt % 2 == 1:
                        op.then_inc(s5["out_full"], 1)

            def ffn_frame(f, layer, with_s5, with_next, next_s5):
                pe.wait_ge(xn_ready, 2 * f + (2 * B + 2))
                for ft in range(FT):
                    up(f, layer, ft)
                    if with_s5 and ft == 4:
                        s5_inputs_pe(f - 1)
                    if ft >= 2:
                        down(f, layer, ft - 2)
                    if isinstance(f, int) and f == 0:
                        for one in TAIL[LAG + 1 + ft] if ft < 5 else []:
                            turn(*one)
                    if with_s5 and ft == 2:
                        transpose_norm(norm_s5(f), s5["t_full"])
                    if with_next and ft == 5:
                        transpose_norm(norm_next(f, with_s5), ffn["t_full"])
                down(f, layer, FT - 2)
                down(f, layer, FT - 1)
                if with_s5:
                    s5_outputs_pe(f - 1)
                if isinstance(f, int) and f == 0:
                    pe.wait_ge(s5_inputs, 1)
                    for m in range(2):
                        for k in range(KT):
                            op = nc.tensor.transpose(MISC[:, (2 * m + k) * P:(2 * m + k + 1) * P],
                                                     BB[:, m, k * P:(k + 1) * P], IDENT[:, :])
                    op.then_inc(s5["bb_t"], 1)

            ffn_frames(pe, ffn_frame)


_ORDER = ["x", "vecs", "cond", "wmod", "bgate", "wqkv", "bv", "wo", "bo", "w1_0", "w2_0", "b2_0",
          "b_st", "b_sw", "c_st", "c_sw", "w1_1", "w2_1", "b2_1"]


def kernel(**inputs):
    import numpy as np
    import concourse.bacc as bacc
    from concourse.bass_utils import run_bass_kernel_spmd

    a = {k: np.asarray(v) for k, v in inputs.items()}
    L0, L1 = "L0_cond_", "L1_cond_"

    def feature_tiles(m):
        return np.ascontiguousarray(m.reshape(m.shape[0] // P, P, m.shape[1]).transpose(1, 0, 2))

    def columns(v):
        return v.reshape(-1, P).T

    def twice(v):
        return np.concatenate([v, v])

    bmod = np.concatenate([a[L0 + "bt_attn"], a[L0 + "bt_ffn"], a[L1 + "bm"], a[L1 + "bc"]])
    vectors = {"ln1_w": a[L0 + "ln1_w"], "ln1_b": a[L0 + "ln1_b"], "ln2_w": a[L0 + "ln2_w"], "ln2_b": a[L0 + "ln2_b"],
               "bq": a[L0 + "bq"], "bk": a[L0 + "bk"], "bmod": bmod, "b1_0": a[L0 + "b1"], "b1_1": a[L1 + "b1"],
               "d_diag": a[L1 + "D_diag"], "lam_re": twice(a[L1 + "Lam_re"]), "lam_im": twice(a[L1 + "Lam_im"]),
               "log_step": twice(a[L1 + "log_step"])}
    laid = {
        "x": a["x"],
        "vecs": np.concatenate([columns(vectors[name]) for name, _ in VEC_SIZES], axis=1),
        "cond": feature_tiles(a["cond_1024"].T),
        "wmod": feature_tiles(np.concatenate([a[L0 + "wt_attn"], a[L0 + "wt_ffn"], a[L1 + "Wm"], a[L1 + "Wc"]], axis=1)),
        "bgate": np.stack([a[L1 + "bm"][2 * D:3 * D], a[L1 + "bm"][5 * D:6 * D]]),
        "wqkv": feature_tiles(np.concatenate([a[L0 + "wq"], a[L0 + "wk"], a[L0 + "wv"]], axis=1)).reshape(P, -1),
        "bv": a[L0 + "bv"],
        "wo": feature_tiles(a[L0 + "wo"]),
        "bo": a[L0 + "bo"],
        "w1_0": feature_tiles(a[L0 + "w1"]).reshape(P, -1),
        "w2_0": feature_tiles(a[L0 + "w2"]).reshape(P, -1),
        "b2_0": a[L0 + "b2"],
        "b_st": np.concatenate([a[L1 + "B_re"], a[L1 + "B_im"]]),
        "b_sw": np.concatenate([a[L1 + "B_im"], a[L1 + "B_re"]]),
        "c_st": np.concatenate([a[L1 + "C_re"].T, a[L1 + "C_im"].T]),
        "c_sw": np.concatenate([a[L1 + "C_im"].T, a[L1 + "C_re"].T]),
        "w1_1": feature_tiles(a[L1 + "W1"]).reshape(P, -1),
        "w2_1": feature_tiles(a[L1 + "W2"]).reshape(P, -1),
        "b2_1": a[L1 + "b2"],
    }
    nc = bacc.Bacc("TRN2", target_bir_lowering=False, num_devices=1, dynamic_dma_scratch_size=4096)
    arrays, args = {}, []
    for name in _ORDER:
        arrays["in_" + name] = np.ascontiguousarray(laid[name])
        args.append(nc.dram_tensor("in_" + name, laid[name].shape, F32, kind="ExternalInput").ap())
    out = nc.dram_tensor("out_y", (B, S, D), F32, kind="ExternalOutput").ap()
    cond_seq_kernel(nc, *args, out)
    r = run_bass_kernel_spmd(nc, [arrays], core_ids=[0])
    return r.results[0]["out_y"]
```

```python
import math
from contextlib import ExitStack

import concourse.bass as bass
from concourse import mybir

F32 = mybir.dt.float32
F32R = mybir.dt.float32r
I32 = mybir.dt.int32
ALU = mybir.AluOpType
ACT = mybir.ActivationFunctionType
AX_X = mybir.AxisListType.X

P = 128
B, S, D = 4, 512, 256
H, HD = 16, 16
F = 1024
NS = 64
KT = D // P
TT = S // P
FT = F // P
EPS = 1e-5
QUADS = H // 4
SCALE = 1.0 / math.sqrt(HD)
ZERO_ROW, MAX_HI, MAX_LO = 64, 65, 66
P1_ROWS, P2_ROWS = 65, 67
LAG = 6
NMOD = 24

M_SHIFT0, M_SCALE0, M_SHIFT1, M_SCALE1 = 0, 2, 4, 6
M_SHIFT2, M_SCALE2, M_GATE_A, M_SHIFTF, M_SCALEF, M_GATE_F = 8, 10, 12, 14, 16, 18
M_SCALEC, M_SHIFTC = 20, 22

VEC_SIZES = [("ln1_w", 2), ("ln1_b", 2), ("ln2_w", 2), ("ln2_b", 2), ("bq", 2), ("bk", 2), ("bmod", NMOD),
             ("b1_0", FT), ("b1_1", FT), ("d_diag", 2), ("lam_re", 1), ("lam_im", 1), ("log_step", 1)]
VEC = {}
for _name, _n in VEC_SIZES:
    VEC[_name] = sum(VEC[k][1] for k in VEC), _n
NVEC = sum(n for _, n in VEC_SIZES)


MAG_COL = 63


def turns_of(kind):
    first, last, tail = kind == "first", kind == "last", kind == "tail"
    steps = {s: [] for s in range(16)}
    if first:
        steps[0] += [("V", 0, 0)]
        steps[1] += [("V", 0, 1), ("Q", 0, 1)]
        steps[2] += [("K", 0, 1)]
    else:
        steps[0] += [("MX", -1, 3)]
    if not (last or tail):
        steps[2] += [("LT", 1, 0)]
        steps[3] += [("LT", 1, 1)]
    if not first:
        steps[3] += [("OT", -1, 2)]
    if not tail:
        steps[4] += [("MX", 0, 0)]
    if not (last or tail):
        steps[5] += [("Q", 1, 0)]
        steps[6] += [("K", 1, 0)]
    if not first:
        steps[7] += [("OT", -1, 3)]
        steps[8] += [("OB", -1, 0)]
        steps[9] += [("OB", -1, 1)]
        steps[10] += [("WO", -1, 0)]
        steps[11] += [("WO", -1, 1)]
    if not tail:
        steps[8] += [("MX", 0, 1)]
        steps[11] += [("OT", 0, 0)]
        steps[12] += [("MX", 0, 2)]
        steps[15] += [("OT", 0, 1)]
    if not (last or tail):
        steps[9] += [("V", 1, 0)]
        steps[10] += [("V", 1, 1)]
        steps[13] += [("Q", 1, 1)]
        steps[14] += [("K", 1, 1)]
    return steps


def n_turns(kind):
    return sum(len(v) for v in turns_of(kind).values())


PRO_TURNS = 4
FIRST_TURNS, MID_TURNS, LAST_TURNS, TAIL_TURNS = (n_turns(k) for k in ("first", "middle", "last", "tail"))


def turn_base(b):
    if isinstance(b, int) and b == 0:
        return PRO_TURNS
    if isinstance(b, int) and b == B:
        return PRO_TURNS + FIRST_TURNS + (B - 2) * MID_TURNS + LAST_TURNS
    return b * MID_TURNS + (PRO_TURNS + FIRST_TURNS - MID_TURNS)


ALL_TURNS = turn_base(B) + TAIL_TURNS


def numbered(b, kind):
    out, n = {}, turn_base(b)
    for s, turns in turns_of(kind).items():
        out[s] = []
        for what, off, i in turns:
            out[s].append((n, what, b + off, i))
            n = n + 1
    return out


def positive(b):
    return not (isinstance(b, int) and b <= 0)


def cond_seq_kernel(nc, x, vecs, cond, wmod, bgate, wqkv, bv, wo, bo, w1_0, w2_0, b2_0,
                    b_st, b_sw, c_st, c_sw, w1_1, w2_1, b2_1, out):
    ctx = ExitStack()
    with ctx:
        def sb(name, shape, dt=F32):
            return ctx.enter_context(nc.sbuf_tensor(name, shape, dt))

        def sem(name):
            return ctx.enter_context(nc.semaphore(name))

        X = sb("X", [P, B * TT, D])
        STK = sb("STK", [P, 2 * H * S], F32R)
        PT = sb("PT", [P, TT * 4 * S])
        SRCQ = sb("SRCQ", [P, 2, 2, S], F32R)
        SRCK = sb("SRCK", [P, 2, 3, S], F32R)
        WQ = sb("WQ", [P, 3072], F32R)
        WRAW = sb("WRAW", [P, 2048])
        XNF = sb("XNF", [P, KT, S])
        XNF2 = sb("XNF2", [P, KT, S])
        XN = sb("XN", [P, 2, KT, S], F32R)
        XH = sb("XH", [P, TT, D])
        AO = sb("AO", [P, 6144])
        WO = sb("WO", [P, KT, D])
        VEC_SB = sb("VEC_SB", [P, NVEC])
        COND = sb("COND", [P, KT, B])
        IDENT = sb("IDENT", [P, P])
        BV = sb("BV", [P, D])
        BO = sb("BO", [P, D])
        GATE_A = sb("GATE_A", [P, B, D])
        GATE_F = sb("GATE_F", [P, B, D])
        MT = sb("MT", [P, NMOD, B])
        ONE_S = sb("ONE_S", [P, KT, B])
        AB = sb("AB", [P, 4, 2, KT, B])
        DG = sb("DG", [P, KT, B])
        STAT = sb("STAT", [P, TT, 6])
        MV = sb("MV", [P, TT, 2])
        VE = sb("VE", [P, TT])
        RSTD = sb("RSTD", [P, TT])
        MINUS_HALF = sb("MINUS_HALF", [P, TT])
        MX = sb("MX", [P, 2, 4, TT])
        NEGMX = sb("NEGMX", [16, QUADS, 2, P], F32R)
        RC = sb("RC", [P, 16])
        PART = sb("PART", [P, D])
        SC = sb("SC", [P, MAG_COL + 1])

        QS = STK[0:P2_ROWS, 0:H * S].rearrange("p (h t) -> p h t", h=H)
        KS = STK[0:P2_ROWS, H * S:2 * H * S].rearrange("p (h t) -> p h t", h=H)
        PTV = PT[:, :].rearrange("p (k j t) -> p k j t", k=TT, j=4)
        WMOD = PT[:, 0:2 * NMOD * P].rearrange("p (k n) -> p k n", k=KT)
        WQV = WQ[:, :].rearrange("p (s k n) -> p s k n", s=2, k=KT)
        VS = AO[:, 0:1024].rearrange("p (t n) -> p t n", t=TT)
        VA = AO[:, 1024:3072].rearrange("p (o t h d) -> p o t h d", o=2, t=TT, h=8)
        OR = AO[:, 3072:4096].rearrange("p (s t) -> p s t", s=2)
        OTK = AO[:, 4096:5120].rearrange("p (t n) -> p t n", t=TT)
        OF = AO[:, 5120:6144].rearrange("p (k t) -> p k t", k=KT)
        MROW = AO[:, 4096:5120].rearrange("p (h n) -> p h n", h=2)
        BG = AO[:, 3072:3584].rearrange("p (g n) -> p g n", g=2)
        ROWS = AO[:, 3584:4096]
        W1P = STK[:, 0:4096].rearrange("p (s k n) -> p s k n", s=2, k=KT)
        HH = STK[:, 4096:8192].rearrange("p (f t) -> p f t", f=FT)
        W2P = STK[:, 8192:12288].rearrange("p (s f n) -> p s f n", s=2, f=FT)
        HL = STK[:, 12288:16384].rearrange("p (f t) -> p f t", f=FT)
        T1, T2, ROT, STATE = (PT[:, S * i:S * (i + 1)] for i in range(4))
        HF = PT[:, 2048:3072].rearrange("p (s t) -> p s t", s=2)
        CYF = PT[:, 3072:4096].rearrange("p (m t) -> p m t", m=2)
        TMP = PT[:, 3072:4096].rearrange("p (a t n) -> p a t n", a=2, t=2)
        RAW1 = PT[:, 4096:6144]
        RAW2 = PT[:, 6144:8192]
        CYP, XN2 = SRCK, SRCQ
        TAB_C, TAB_S = AO[:, 0:512], AO[:, 512:1024]
        B_ST, B_SW, C_ST, C_SW = (AO[:, 1024 + 256 * i:1280 + 256 * i] for i in range(4))
        B2_0, B2_1, GB2 = (AO[:, 2048 + 256 * i:2304 + 256 * i] for i in range(3))
        BB = AO[:, 3072:3584].rearrange("p (m n) -> p m n", m=2)
        WC = AO[:, 3584:4096].rearrange("p (m n) -> p m n", m=2)
        WGF = AO[:, 4096:4608].rearrange("p (m n) -> p m n", m=2)
        DGF = AO[:, 4608:4864].rearrange("p (k n) -> p k n", k=KT)
        BBT = AO[:, 5120:5632].rearrange("p (m n) -> p m n", m=4)
        WB = WQ[:, 0:1024].rearrange("p (s m n) -> p s m n", s=2, m=4)
        WG = WQ[:, 1024:2048].rearrange("p (s m n) -> p s m n", s=2, m=2)
        DGP = WQ[:, 2048:2560].rearrange("p (s k n) -> p s k n", s=2, k=KT)

        PS = [ctx.enter_context(nc.psum_tensor(f"bank{i}", [P, 512], F32)) for i in range(4, 8)]
        PS1 = ctx.enter_context(nc.psum_tensor("banks0_3", [P, 4, 512], F32))
        bank = [PS1[:, i, :] for i in range(4)] + [p[:, :] for p in PS]
        PV, MISC = bank[6], bank[7]
        T_BANK, UP_BANK, DOWN_BANK, S5_BANK = 0, 2, 4, 6

        def turn_bank(t):
            return {1: bank[6], 2: bank[5]}.get(t, MISC) if isinstance(t, int) else MISC

        def vec(name, i):
            at = VEC[name][0] + i
            return VEC_SB[:, at:at + 1]

        def vecs_of(name):
            at, n = VEC[name]
            return VEC_SB[:, at:at + n]

        def x_tile(b, tt):
            return X[:, bass.ds(b * TT + tt, 1), :].rearrange("p a n -> p (a n)")

        def x_pair(b, p):
            return X[:, bass.ds(b * TT + 2 * p, 2), :]

        def x_batch(b):
            return X[:, bass.ds(b * TT, TT), :]

        def ab(ln, which, k, b):
            return AB[:, ln, which, k, bass.ds(b, 1)]

        s_x = [sem(f"x_loaded{b}") for b in range(B)]
        s_small = sem("small_loaded")
        s_wq = sem("wqkv_loaded")
        s_wmod_a = sem("wmod_attn_loaded")
        s_wmod_b = sem("wmod_rest_loaded")
        s_rows = sem("rows_loaded")
        s_const_rows = sem("constant_rows_placed")
        s_w1raw = sem("w1_raw_loaded")
        s_w2raw = sem("w2_raw_loaded")
        s_raw1 = sem("block1_raw_loaded")
        s_s5raw = sem("s5_raw_loaded")
        s_out = sem("out_stored")
        ident_ready = sem("ident_ready")
        const_ready = sem("const_ready")
        wq_hi, wq_lo = sem("wq_hi"), sem("wq_lo")
        mrow_mm, mrow_out, mt_mm, mt_ready = sem("mrow_mm"), sem("mrow_out"), sem("mt_mm"), sem("mt_ready")
        gate_mm, gate_out, gate_ready = sem("gate_mm"), sem("gate_out"), sem("gate_ready")
        ab_ready = sem("ab_ready")
        pool_chain = sem("pool_chain")
        ln_stats, ln_mv, ln_ve = sem("ln_stats"), sem("ln_mv"), sem("ln_ve")
        ln_rstd, ln_xhat = sem("ln_rstd"), sem("ln_xhat")
        xn_hi, xn_ready = sem("xn_hi"), sem("xn_ready")
        misc_full, misc_free = sem("misc_full"), sem("misc_free")
        src_hi, src_dup = sem("src_hi"), sem("src_dup")
        mx_hi = sem("mx_hi")
        stack_ready = [sem(f"stack_ready{h}") for h in range(H)]
        negmax_ready = [sem(f"negmax_ready{q}") for q in range(QUADS)]
        s1_full, s1_free = sem("s1_full"), sem("s1_free")
        s2_full, exp_done = sem("s2_full"), sem("exp_done")
        pv_done, pv_evac = sem("pv_done"), sem("pv_evac")
        va_ready = sem("va_ready")
        rc_ready = sem("rc_ready")
        x_bias = sem("x_bias")
        ffn = {n: sem(f"{n}_ffn") for n in
               ("t_full", "xnf", "up_full", "h_hi", "h_lo", "down_ft", "down_full", "down_free",
                "w1_hi", "w1_lo", "w2_hi", "w2_lo", "gated")}
        gb2_ready = sem("gb2_ready")
        waits_carried = sem("waits_carried")
        s5_tables, s5_inputs = sem("s5_tables"), sem("s5_inputs")
        s5 = {n: sem(f"{n}_s5") for n in
              ("t_full", "xnf", "xn_hi", "xn_ready", "bu_full", "t1", "t2", "rot", "scan", "cyf", "cy_hi", "cy_lo",
               "wgf", "wg_hi", "wg_lo", "out_full", "out_free", "bb_t", "bbt", "wb_hi", "wb_lo")}

        MT_FIRST = 4
        CHUNKS = (NMOD - MT_FIRST) * P // 512
        MT_PARTS = [(0, MT_FIRST, bank[3])] + [(MT_FIRST + 8 * j, min(MT_FIRST + 8 * j + 8, NMOD), bank[4 + j])
                                               for j in range((CHUNKS + 1) // 2)]
        GATES = [(gate, gi, tile, 2 * bp, bank[k]) for gate, gi, tile, bp, k in
                 ((GATE_A, 0, M_GATE_A, 0, 6), (GATE_A, 0, M_GATE_A, 1, 4), (GATE_F, 1, M_GATE_F, 0, 5),
                  (GATE_F, 1, M_GATE_F, 1, 6))]

        block = ctx.enter_context(nc.Block())

        LN_ATT, LN_FFN = 0, B
        LAYERS = 2
        FRAMES = LAYERS * B
        W_CHUNKS = 2
        WN = FT // W_CHUNKS

        def ffn_batch(f, layer):
            return f - B * layer

        def norm_next(f, with_s5):
            if isinstance(f, int) and f == 0:
                return LN_FFN + 1
            return 2 * f + (LN_FFN + 1) if with_s5 else f + (LN_FFN + B + 1)

        def norm_s5(f):
            return 2 * f + LN_FFN

        def ffn_frames(engine, frame):
            frame(0, 0, False, True, True)
            with engine.Fori(1, B - 1) as f:
                frame(f, 0, True, True, True)
            frame(B - 1, 0, True, True, True)
            frame(B, 1, True, True, False)
            with engine.Fori(B + 1, FRAMES - 1) as f:
                frame(f, 1, False, True, False)
            frame(FRAMES - 1, 1, False, False, False)

        def ln_stats_dve(dve, n, b):
            for tt in range(TT):
                op = nc.vector.bn_stats(STAT[:, tt, :], x_tile(b, tt))
            op.then_inc(ln_stats, 1)
            alone(dve, ln_stats, n + 1)
            for tt in range(TT):
                op = nc.vector.bn_aggr(MV[:, tt, :], STAT[:, tt, :])
            op.then_inc(ln_mv, 1)

        def ln_rstd_pool(pool, n):
            alone(pool, ln_mv, n + 1)
            nc.gpsimd.tensor_scalar(VE[:, :], MV[:, :, 1], EPS, None, ALU.add).then_inc(ln_ve, 1)
            pool.wait_ge(ln_ve, n + 1)
            nc.gpsimd.tensor_tensor(RSTD[:, :], VE[:, :], MINUS_HALF[:, :], ALU.pow).then_inc(ln_rstd, 1)

        def ln_xhat_dve(dve, n, b):
            dve.wait_ge(ln_rstd, n + 1)
            for tt in range(TT):
                op = nc.vector.tensor_scalar(XH[:, tt, :], x_tile(b, tt), MV[:, tt, 0:1], RSTD[:, tt:tt + 1],
                                             ALU.subtract, ALU.mult)
            op.then_inc(ln_xhat, 1)

        def ln_transpose_pe(pe, n, k, into):
            pe.wait_ge(ln_xhat, n + 1)
            for tt in range(TT):
                op = nc.tensor.transpose(into[:, tt * P:(tt + 1) * P], XH[:, tt, k * P:(k + 1) * P], IDENT[:, :])
            return op

        def xn_split_dve(dve, m, k, full, parts_, hi, ready):
            nc.vector.tensor_copy(parts_(0, k), full[:, k, :]).then_inc(hi, 1)
            dve.wait_ge(hi, 2 * m + (k + 1))
            nc.vector.tensor_tensor(parts_(1, k), full[:, k, :], parts_(0, k).bitcast(F32),
                                    ALU.subtract).then_inc(ready, 1)

        def xn_part(p, k):
            return XN[:, p, k, :]

        def xn2_part(p, k):
            return XN2[:, k, p, :]

        def alone(engine, semaphore, value):
            engine.wait_ge(semaphore, value)
            if not isinstance(value, int):
                engine.sem_inc(waits_carried, 1)

        @block.sync
        def _(sp):
            xv = x.rearrange("b (t p) d -> p (b t) d", p=P)
            sp.dma_start(X[:, 0:TT, :], xv[:, 0:TT, :]).then_inc(s_x[0], 16)
            sp.dma_start(VEC_SB[:, :], vecs).then_inc(s_small, 16)
            sp.dma_start(COND[:, :, :], cond).then_inc(s_small, 16)
            sp.dma_start(WMOD[:, :, 0:MT_FIRST * P], wmod[:, :, 0:MT_FIRST * P]).then_inc(s_wmod_a, 16)
            sp.dma_start(WRAW[:, 0:1536], wqkv).then_inc(s_wq, 16)
            sp.wait_ge(const_ready, 2)
            for stacks, row, constant in ((QS, ZERO_ROW, 0), (KS, ZERO_ROW, 0), (KS, MAX_HI, 32), (KS, MAX_LO, 32)):
                sp.dma_start(stacks[row:row + 1, :, :].bitcast(F32),
                             ROWS[constant:constant + 1, :].unsqueeze(1).to_broadcast([1, H, S]))\
                    .then_inc(s_const_rows, 16)
            sp.dma_start(WMOD[:, :, MT_FIRST * P:NMOD * P], wmod[:, :, MT_FIRST * P:NMOD * P]).then_inc(s_wmod_b, 16)
            sp.dma_start(BV[:, :], bv.partition_broadcast(P)).then_inc(s_rows, 16)
            sp.dma_start(BO[:, :], bo.partition_broadcast(P)).then_inc(s_rows, 16)
            sp.dma_start(BG[:, 0, :], bgate[0, :].partition_broadcast(P)).then_inc(s_rows, 16)
            sp.dma_start(BG[:, 1, :], bgate[1, :].partition_broadcast(P)).then_inc(s_rows, 16)
            sp.dma_start(WO[:, :, :], wo).then_inc(s_rows, 16)
            for b in range(1, B):
                sp.dma_start(X[:, b * TT:(b + 1) * TT, :], xv[:, b * TT:(b + 1) * TT, :]).then_inc(s_x[b], 16)

            def stack(b, h):
                o, r = h // 8, HD * (h % 8)
                alone(sp, src_dup, b * 2 + (o + 1))
                if positive(b):
                    alone(sp, exp_done, b * 64 + (16 * (h // 4 + 1) - 64))
                nc.sync.dma_start(QS[0:32, h, :].bitcast(F32), SRCQ[r:r + HD, o, :, :].bitcast(F32))\
                    .then_inc(stack_ready[h], 16)
                nc.sync.dma_start(QS[32:64, h, :].bitcast(F32), SRCQ[r:r + HD, o, :, :].bitcast(F32))\
                    .then_inc(stack_ready[h], 16)
                nc.sync.dma_start(KS[0:32, h, :].bitcast(F32), SRCK[r:r + HD, o, 0:2, :].bitcast(F32))\
                    .then_inc(stack_ready[h], 16)
                nc.sync.dma_start(KS[32:64, h, :].bitcast(F32), SRCK[r:r + HD, o, 1:3, :].bitcast(F32))\
                    .then_inc(stack_ready[h], 16)

            def negmax(q, turn):
                alone(sp, misc_free, turn + 1)
                for part, row in ((0, MAX_HI), (1, MAX_LO)):
                    nc.sync.dma_start(QS[row:row + 1, 4 * q:4 * q + 4, :].bitcast(F32),
                                      NEGMX[:, q, part, :].bitcast(F32)).then_inc(negmax_ready[q], 16)

            def frame(b, kind):
                turns = numbered(b, kind)
                for s in range(16):
                    for t, what, _, i in turns[s]:
                        if what == "MX":
                            negmax(i, t)
                    if kind != "tail" and s < 10:
                        stack(b, 6 + s)
                    if kind in ("first", "middle") and s >= 10:
                        stack(b + 1, s - 10)

            def q_stack(h):
                for row in (0, 32):
                    sp.dma_start(QS[row:row + 32, h, :].bitcast(F32), SRCQ[HD * h:HD * h + HD, 0, :, :].bitcast(F32))\
                        .then_inc(stack_ready[h], 16)

            def k_stack(h):
                for row, part in ((0, 0), (32, 1)):
                    sp.dma_start(KS[row:row + 32, h, :].bitcast(F32),
                                 SRCK[HD * h:HD * h + HD, 0, part:part + 2, :].bitcast(F32))\
                        .then_inc(stack_ready[h], 16)

            sp.wait_ge(misc_free, 3)
            for h in range(3):
                q_stack(h)
            sp.wait_ge(misc_free, 4)
            sp.wait_ge(src_dup, 1)
            for h in range(3):
                k_stack(h)
            for h in range(3, 6):
                q_stack(h)
                k_stack(h)
            frame(0, "first")
            sp.wait_ge(wq_hi, 1)
            sp.wait_ge(wq_lo, 1)
            sp.dma_start(WRAW[:, :], w1_0).then_inc(s_w1raw, 16)
            with sp.Fori(1, B - 1) as b:
                frame(b, "middle")
            frame(B - 1, "last")
            frame(B, "tail")

            sp.wait_ge(ffn["w1_lo"], W_CHUNKS)
            sp.dma_start(WRAW[:, :], w2_0).then_inc(s_w2raw, 16)
            sp.wait_ge(pv_done, 16 * B)
            sp.dma_start(B2_0, b2_0.partition_broadcast(P)).then_inc(s_s5raw, 16)
            sp.dma_start(B2_1, b2_1.partition_broadcast(P)).then_inc(s_s5raw, 16)
            for dst, src in ((B_ST, b_st), (B_SW, b_sw), (C_ST, c_st), (C_SW, c_sw)):
                sp.dma_start(dst, src).then_inc(s_s5raw, 16)
            sp.dma_start(RAW1, w1_1).then_inc(s_raw1, 16)
            sp.dma_start(RAW2, w2_1).then_inc(s_raw1, 16)
            ov = out.rearrange("b (t p) d -> p (b t) d", p=P)
            for b in range(B):
                for p in range(2):
                    sp.wait_ge(ffn["down_free"], 2 * (B + b) + p + 1)
                    at = slice(b * TT + 2 * p, b * TT + 2 * p + 2)
                    sp.dma_start(ov[:, at, :], X[:, at, :]).then_inc(s_out, 16)
            sp.wait_ge(s_out, 16 * 2 * B)

        @block.gpsimd
        def _(pool):
            g = nc.gpsimd
            g.memset(IDENT[:, :], 0.0).then_inc(pool_chain, 1)
            g.memset(MINUS_HALF[:, :], -0.5)
            pool.wait_ge(pool_chain, 1)
            g.affine_select(out=IDENT[:, :], in_=IDENT[:, :], compare_op=ALU.not_equal, fill=1.0, base=0,
                            pattern=[[-1, P]], channel_multiplier=1).then_inc(ident_ready, 1)
            pool.wait_ge(ident_ready, 1)
            g.memset(ROWS[0:1, :], 0.0).then_inc(const_ready, 1)
            pool.wait_ge(const_ready, 1)
            g.memset(ROWS[32:33, :], 1.0).then_inc(const_ready, 1)
            pool.wait_ge(const_ready, 2)

            chain = [1]

            def link(op):
                chain[0] += 1
                op.then_inc(pool_chain, 1)
                pool.wait_ge(pool_chain, chain[0])

            def over_b(name):
                return vecs_of(name).unsqueeze(2).to_broadcast([P, KT, B])

            def mt(t):
                return MT[:, t:t + KT, :]

            ln_rstd_pool(pool, LN_ATT)
            pool.wait_ge(mt_ready, 1)
            pool.wait_ge(s_small, 32)

            def affine(ln, scale, shift, w, bias):
                link(g.tensor_scalar(ONE_S[:, :, :], mt(scale), 1.0, None, ALU.add))
                link(g.tensor_tensor(AB[:, ln, 0, :, :], ONE_S[:, :, :], over_b(w), ALU.mult))
                link(g.tensor_tensor(AB[:, ln, 1, :, :], ONE_S[:, :, :], over_b(bias), ALU.mult))
                return g.tensor_tensor(AB[:, ln, 1, :, :], AB[:, ln, 1, :, :], mt(shift), ALU.add)

            affine(0, M_SCALE0, M_SHIFT0, "ln1_w", "ln1_b").then_inc(ab_ready, 1)
            g.memset(VA[:, :, :, :, HD:2 * HD].rearrange("p o t h d -> p (o t h) d"), 1.0).then_inc(const_ready, 1)

            def dup_turn(t, o):
                alone(pool, misc_free, t + 1)
                g.tensor_copy(SRCK[:, o, 2, :], SRCK[:, o, 0, :].bitcast(F32)).then_inc(src_dup, 1)

            def va_fill(o):
                for tt in range(TT):
                    op = g.tensor_copy(VA[:, o, tt, :, 0:HD],
                                       VS[:, tt, o * P:(o + 1) * P].rearrange("p (h d) -> p h d", h=8))
                op.then_inc(va_ready, 1)

            cols = {}

            def col(name):
                cols.setdefault(name, len(cols))
                assert len(cols) <= MAG_COL
                return SC[:, cols[name]:cols[name] + 1]

            def ts(dst, src, s1, op0, s2=None, op1=ALU.bypass):
                link(g.tensor_scalar(dst, src, s1, s2, op0, op1) if s2 is not None
                     else g.tensor_scalar(dst, src, s1, None, op0))

            def tt_(dst, a, b_, op):
                link(g.tensor_tensor(dst, a, b_, op))

            ROUND = 1.5 * 2.0 ** 23

            def nearest(dst, src, factor, offset=0.0):
                ts(dst, src, factor, ALU.mult, offset, ALU.add)
                ts(dst, dst, ROUND, ALU.add)
                ts(dst, dst, ROUND, ALU.subtract)

            def horner(dst, r, coefficients):
                ts(dst, r, coefficients[0], ALU.mult, coefficients[1], ALU.add)
                for c in coefficients[2:]:
                    ts(dst, dst, r, ALU.mult, c, ALU.add)

            def exp_(dst, src):
                n, r, t = col("n"), col("r"), col("t")
                nearest(n, src, 1.0 / math.log(2.0))
                ts(n, n, -126.0, ALU.max, 127.0, ALU.min)
                ts(t, n, -0.693359375, ALU.mult)
                tt_(r, src, t, ALU.add)
                ts(t, n, 2.12194440e-4, ALU.mult)
                tt_(r, r, t, ALU.add)
                horner(t, r, [1.0 / math.factorial(k) for k in range(8, -1, -1)])
                ts(col("bits").bitcast(I32), n, 127.0, ALU.add, 2.0 ** 23, ALU.mult)
                tt_(dst, t, col("bits"), ALU.mult)

            def lambda_bar():
                lre, lim = vec("lam_re", 0), vec("lam_im", 0)
                dt, mag, th = col("dt"), col("mag"), col("th")
                exp_(dt, vec("log_step", 0))
                tt_(th, lre, dt, ALU.mult)
                exp_(mag, th)
                tt_(th, lim, dt, ALU.mult)
                n, r, t, r2, si, co = col("n"), col("r"), col("t"), col("r2"), col("si"), col("co")
                nearest(n, th, 2.0 / math.pi)
                ts(t, n, -1.5703125, ALU.mult)
                tt_(r, th, t, ALU.add)
                ts(t, n, -4.837512969970703125e-4, ALU.mult)
                tt_(r, r, t, ALU.add)
                ts(t, n, -7.54978995489188216e-8, ALU.mult)
                tt_(r, r, t, ALU.add)
                tt_(r2, r, r, ALU.mult)
                horner(si, r2, [(-1.0) ** k / math.factorial(2 * k + 1) for k in range(5, -1, -1)])
                tt_(si, si, r, ALU.mult)
                horner(co, r2, [(-1.0) ** k / math.factorial(2 * k) for k in range(6, -1, -1)])
                m, is1, is3, odd = col("m"), col("is1"), col("is3"), col("odd")
                nearest(m, n, 0.25, -0.375)
                ts(m, m, -4.0, ALU.mult)
                tt_(m, m, n, ALU.add)
                ts(is1, m, 1.0, ALU.is_equal)
                ts(is3, m, 3.0, ALU.is_equal)
                tt_(odd, is1, is3, ALU.add)
                even, sg_s, sg_c = col("even"), col("sg_s"), col("sg_c")
                ts(even, odd, -1.0, ALU.mult, 1.0, ALU.add)
                ts(sg_s, m, 2.0, ALU.is_ge, -2.0, ALU.mult)
                ts(sg_s, sg_s, 1.0, ALU.add)
                ts(sg_c, m, 2.0, ALU.is_equal)
                tt_(sg_c, sg_c, is1, ALU.add)
                ts(sg_c, sg_c, -2.0, ALU.mult, 1.0, ALU.add)
                sin, cos = col("sin"), col("cos")
                tt_(sin, si, even, ALU.mult)
                tt_(t, co, odd, ALU.mult)
                tt_(sin, sin, t, ALU.add)
                tt_(sin, sin, sg_s, ALU.mult)
                tt_(cos, co, even, ALU.mult)
                tt_(t, si, odd, ALU.mult)
                tt_(cos, cos, t, ALU.add)
                tt_(cos, cos, sg_c, ALU.mult)

            def coefficients():
                lre, lim = vec("lam_re", 0), vec("lam_im", 0)
                mag, cos, sin, r2, t = col("mag"), col("cos"), col("sin"), col("r2"), col("t")
                lb_re, lb_im, cr, ci = col("lb_re"), col("lb_im"), col("cr"), col("ci")
                tt_(lb_re, mag, cos, ALU.mult)
                ts(lb_re, lb_re, 1.0, ALU.subtract)
                tt_(lb_im, mag, sin, ALU.mult)
                tt_(cr, lb_re, lre, ALU.mult)
                tt_(t, lb_im, lim, ALU.mult)
                tt_(cr, cr, t, ALU.add)
                tt_(ci, lb_im, lre, ALU.mult)
                tt_(t, lb_re, lim, ALU.mult)
                tt_(ci, ci, t, ALU.subtract)
                tt_(r2, lre, lre, ALU.mult)
                tt_(t, lim, lim, ALU.mult)
                tt_(r2, r2, t, ALU.add)
                link(g.memset(t, -1.0))
                tt_(r2, r2, t, ALU.pow)
                tt_(cr, cr, r2, ALU.mult)
                tt_(ci, ci, r2, ALU.mult)
                sgn, nci, scr, s2 = col("sgn"), col("nci"), col("scr"), col("s2")
                link(g.memset(sgn[0:NS, :], 1.0))
                link(g.memset(sgn[NS:P, :], -1.0))
                tt_(nci, sgn, ci, ALU.mult)
                ts(nci, nci, -1.0, ALU.mult)
                tt_(scr, sgn, cr, ALU.mult)
                ts(s2, sgn, 2.0, ALU.mult)
                link(g.tensor_copy(col("cos1"), cos))
                link(g.tensor_copy(col("sin1"), sin))
                n_ = 1
                while 2 * n_ < S:
                    wc, ws, wc2, ws2 = col(f"cos{n_}"), col(f"sin{n_}"), col(f"cos{2 * n_}"), col(f"sin{2 * n_}")
                    tt_(t, ws, ws, ALU.mult)
                    tt_(r2, wc, ws, ALU.mult)
                    tt_(wc2, wc, wc, ALU.mult)
                    tt_(wc2, wc2, t, ALU.subtract)
                    ts(ws2, r2, 2.0, ALU.mult)
                    n_ *= 2
                link(g.tensor_copy(SC[:, MAG_COL:MAG_COL + 1], mag))

            def state_tables():
                pool.wait_ge(va_ready, 2 * B)
                link(g.memset(TAB_C[:, 0:1], 1.0))
                link(g.memset(TAB_S[:, 0:1], 0.0))
                n_ = 1
                while n_ < S:
                    lo, hi = slice(0, n_), slice(n_, 2 * n_)
                    wc, ws = col(f"cos{n_}"), col(f"sin{n_}")
                    ts(TAB_C[:, hi], TAB_C[:, lo], wc, ALU.mult)
                    ts(PART[:, lo], TAB_S[:, lo], ws, ALU.mult)
                    tt_(TAB_C[:, hi], TAB_C[:, hi], PART[:, lo], ALU.subtract)
                    ts(TAB_S[:, hi], TAB_S[:, lo], wc, ALU.mult)
                    ts(PART[:, lo], TAB_C[:, lo], ws, ALU.mult)
                    op = g.tensor_tensor(TAB_S[:, hi], TAB_S[:, hi], PART[:, lo], ALU.add)
                    n_ *= 2
                    if n_ < S:
                        link(op)
                op.then_inc(s5_tables, 1)

            def state_inputs():
                cr, ci, nci, scr, s2 = col("cr"), col("ci"), col("nci"), col("scr"), col("s2")
                pool.wait_ge(s_s5raw, 16 * 6)
                ts(BB[:, 0, :], B_ST, cr, ALU.mult)
                ts(PART[:, :], B_SW, nci, ALU.mult)
                tt_(BB[:, 0, :], BB[:, 0, :], PART[:, :], ALU.add)
                ts(BB[:, 1, :], B_ST, ci, ALU.mult)
                ts(PART[:, :], B_SW, scr, ALU.mult)
                g.tensor_tensor(BB[:, 1, :], BB[:, 1, :], PART[:, :], ALU.add).then_inc(s5_inputs, 1)
                ts(WC[:, 0, :], C_ST, s2, ALU.mult)
                ts(WC[:, 1, :], C_SW, -2.0, ALU.mult)

            def other_affines():
                pool.wait_ge(mt_ready, len(MT_PARTS))
                link(affine(1, M_SCALE1, M_SHIFT1, "ln2_w", "ln2_b"))
                g.tensor_scalar(AB[:, 2, 0, :, :], mt(M_SCALE2), 1.0, None, ALU.add)
                g.tensor_copy(AB[:, 2, 1, :, :], mt(M_SHIFT2))
                g.tensor_tensor(DG[:, :, :], mt(M_GATE_A), over_b("d_diag"), ALU.mult)
                link(g.tensor_scalar(ONE_S[:, :, :], mt(M_SCALEF), 1.0, None, ALU.add))
                link(g.tensor_scalar(AB[:, 3, 0, :, :], mt(M_SCALEC), 1.0, None, ALU.add))
                link(g.tensor_tensor(AB[:, 3, 0, :, :], AB[:, 3, 0, :, :], ONE_S[:, :, :], ALU.mult))
                link(g.tensor_tensor(AB[:, 3, 1, :, :], mt(M_SHIFTC), ONE_S[:, :, :], ALU.mult))
                g.tensor_tensor(AB[:, 3, 1, :, :], AB[:, 3, 1, :, :], mt(M_SHIFTF), ALU.add).then_inc(ab_ready, 1)

            def gate_bias(i):
                gate, gi, _, b, _ = GATES[i]
                pool.wait_ge(s_rows, 80)
                pool.wait_ge(gate_out, i + 1)
                g.tensor_tensor(gate[:, b:b + 2, :], gate[:, b:b + 2, :], BG[:, gi, :].unsqueeze(1)
                                .to_broadcast([P, 2, D]), ALU.add).then_inc(gate_ready, 1)

            def frame(b, kind):
                turns = numbered(b, kind)
                for s in range(16):
                    if kind in ("first", "middle") and s == 0:
                        ln_rstd_pool(pool, LN_ATT + 1 + b)
                    for t, what, bb, i in turns[s]:
                        if what == "K":
                            dup_turn(t, i)
                        if what == "V" and i == 1 and kind == "first" and s == 1:
                            pool.wait_ge(misc_free, t + 1)
                            pool.wait_ge(const_ready, 3)
                            va_fill(0)
                            va_fill(1)
                    if kind != "first" and s == 1:
                        alone(pool, pv_done, b * 16 - 8)
                        va_fill(0)
                    if kind != "first" and s == 7:
                        alone(pool, pv_done, b * 16)
                        va_fill(1)
                    if kind == "first" and s == 3:
                        other_affines()
                    if kind == "first" and 4 <= s < 4 + len(GATES):
                        gate_bias(s - 4)
                    if kind == "first" and s == 8:
                        lambda_bar()
                    if kind == "last" and s == 7:
                        state_tables()
                    if s == 3:
                        alone(pool, ln_xhat, b + 1)
                        g.tensor_tensor(x_batch(b), x_batch(b), BO[:, :].unsqueeze(1).to_broadcast([P, TT, D]),
                                        ALU.add).then_inc(x_bias, 1)
                    if kind == "last" and s == 3:
                        coefficients()

            frame(0, "first")
            with pool.Fori(1, B - 1) as b:
                frame(b, "middle")
            frame(B - 1, "last")

            ln_rstd_pool(pool, LN_FFN)

            def gated_weights(j):
                for i in range(2):
                    g.tensor_tensor(WGF[:, i, :], WC[:, i, :],
                                    GATE_A[:, bass.ds(j, 1), :].rearrange("p a n -> p (a n)"),
                                    ALU.mult).then_inc(s5["wgf"], 1)
                for k in range(KT):
                    g.tensor_tensor(DGF[:, k, :], IDENT[:, :], DG[:, k, bass.ds(j, 1)].to_broadcast([P, P]),
                                    ALU.mult).then_inc(s5["wgf"], 1)

            def output_bias(f, layer):
                b = ffn_batch(f, layer)
                bias = B2_0
                if layer == 1:
                    g.tensor_tensor(GB2, GATE_F[:, bass.ds(b, 1), :].rearrange("p a n -> p (a n)"), B2_1,
                                    ALU.mult).then_inc(gb2_ready, 1)
                    pool.wait_ge(gb2_ready, b + 1)
                    bias = GB2
                g.tensor_tensor(x_batch(b), x_batch(b), bias.unsqueeze(1).to_broadcast([P, TT, D]),
                                ALU.add).then_inc(x_bias, 1)

            def ffn_frame(f, layer, with_s5, with_next, next_s5):
                if with_s5:
                    ln_rstd_pool(pool, norm_s5(f))
                    gated_weights(f - 1)
                else:
                    alone(pool, ln_xhat, f + (LN_FFN + 1 + B * layer))
                if isinstance(f, int) and f == 0:
                    pool.wait_ge(s_s5raw, 16 * 6)
                output_bias(f, layer)
                if with_next:
                    ln_rstd_pool(pool, norm_next(f, with_s5))
                if isinstance(f, int) and f == 0:
                    pool.wait_ge(misc_free, ALL_TURNS)
                    state_inputs()
                if with_s5:
                    alone(pool, s5["t2"], f)
                    g.tensor_tensor(ROT, T1, T2, ALU.add).then_inc(s5["rot"], 1)

            ffn_frames(pool, ffn_frame)

        @block.scalar
        def _(act):
            a = nc.scalar
            act.wait_ge(s_wq, 16)
            a.activation(WQ[:, 0:1536], WRAW[:, 0:1536], ACT.Copy).then_inc(wq_hi, 1)

            def turn(t, what, b, i):
                at_bank = turn_bank(t)
                if what == "LT":
                    act.wait_ge(misc_full, t + 1)
                    if positive(b):
                        act.wait_ge(xn_ready, 2 * b + (i - 1))
                    a.activation(XNF[:, i, :], at_bank, ACT.Identity, bias=ab(0, 1, i, b), scale=ab(0, 0, i, b))\
                        .then_inc(misc_free, 1)
                if what in ("Q", "K"):
                    act.wait_ge(misc_full, t + 1)
                    if positive(b) and what == "Q":
                        act.wait_ge(s1_full, 32 * b + (16 * i + 10 - 32))
                        for h in range(8 * i + 5, 8 * i + 8):
                            act.wait_ge(stack_ready[h], 64 * b)
                    src, bias = (SRCQ, "bq") if what == "Q" else (SRCK, "bk")
                    a.activation(src[:, i, 0, :], at_bank, ACT.Identity, bias=vec(bias, i)).then_inc(src_hi, 1)
                if what == "MX":
                    act.wait_ge(misc_full, t + 1)
                    if positive(b):
                        act.wait_ge(negmax_ready[i], 32 * b)
                    a.activation(NEGMX[:, i, 0, :], at_bank[0:16, 0:P], ACT.Copy, scale=-1.0).then_inc(mx_hi, 1)
                if what == "OB":
                    act.wait_ge(misc_full, t + 1)
                    a.activation(OF[:, i, :], at_bank, ACT.Copy).then_inc(misc_free, 1)

            act.wait_ge(ab_ready, 1)
            turn(0, "LT", 0, 0)
            turn(1, "LT", 0, 1)
            turn(2, "Q", 0, 0)
            turn(3, "K", 0, 0)
            act.wait_ge(src_hi, 2)
            a.activation(SRCK[:, 0, 2, :], SRCK[:, 0, 0, :].bitcast(F32), ACT.Copy).then_inc(src_dup, 1)
            act.wait_ge(mrow_mm, 1)
            for c in range(CHUNKS):
                at = slice(32 * (c // 2), 32 * (c // 2) + B)
                op = a.activation(MROW[at, c % 2, :], bank[4 + c % 2][at, :], ACT.Copy)
            op.then_inc(mrow_out, 1)

            def exps(b, s, js):
                g = 16 * b + (s - LAG)
                kt = (s - LAG) % 4
                for j in js:
                    act.wait_ge(s2_full, 4 * g + (j + 1))
                    if j == 0 and not (isinstance(g, int) and g < 4):
                        act.wait_ge(pv_done, g - 3)
                    a.activation(PTV[:, kt, j, :], bank[4 + j % 2], ACT.Exp, scale=SCALE).then_inc(exp_done, 1)

            def xnf_out(f, layer):
                ln, b = (1, 3)[layer], ffn_batch(f, layer)
                for k in range(KT):
                    act.wait_ge(ffn["t_full"], 2 * f + (k + 1))
                    act.wait_ge(xn_ready, 2 * f + (2 * B + k - 1))
                    a.activation(XNF[:, k, :], bank[T_BANK + k], ACT.Identity, bias=ab(ln, 1, k, b),
                                 scale=ab(ln, 0, k, b)).then_inc(ffn["xnf"], 1)

            def frame(b, kind):
                turns = numbered(b, kind)
                for s in range(16 if kind != "tail" else LAG + 1):
                    has_p2 = (kind != "first" or s >= LAG) and (kind != "tail" or s < LAG)
                    if has_p2:
                        exps(b, s, (0, 1))
                    for one in turns[s][0:1]:
                        turn(*one)
                    if has_p2:
                        exps(b, s, (2, 3))
                    for one in turns[s][1:]:
                        turn(*one)
                    if kind == "first" and 1 <= s <= len(GATES):
                        gate, _, _, b_, from_bank = GATES[s - 1]
                        act.wait_ge(gate_mm, s)
                        a.activation(gate[:, b_:b_ + 2, :], from_bank.rearrange("p (a n) -> p a n", a=2), ACT.Copy)\
                            .then_inc(gate_out, 1)
                    done = s - LAG - 1
                    if (kind != "first" or done >= 0) and (kind != "tail" or done < 0) and done % 4 == 3:
                        q = (done // 4) % 4
                        act.wait_ge(pv_done, 16 * b + (done + 1))
                        if kind == "first":
                            act.wait_ge(gate_ready, len(GATES))
                        a.activation(OR[:, q % 2, :], PV, ACT.Copy).then_inc(pv_evac, 1)
                    if kind == "tail" and s == 3:
                        xnf_out(0, 0)

            frame(0, "first")
            with act.Fori(1, B - 1) as b:
                frame(b, "middle")
            frame(B - 1, "last")
            frame(B, "tail")

            TAIL = numbered(B, "tail")

            def tail_hook(ft):
                for one in TAIL[LAG + 1 + ft] if ft < 5 else []:
                    turn(*one)

            def ffn_frame(f, layer, with_s5, with_next, next_s5):
                n = ffn
                j = f - 1
                new_layer = isinstance(f, int) and f == B - 1
                for ft in range(FT):
                    act.wait_ge(n["up_full"], FT * f + (ft + 1))
                    if positive(f) or ft >= 2:
                        act.wait_ge(n["h_lo"], FT * f + (ft - 1))
                    func, b1 = ((ACT.Gelu, "b1_0"), (ACT.Gelu_apprx_tanh, "b1_1"))[layer]
                    a.activation(HF[:, ft % 2, :], bank[UP_BANK + ft % 2], func, bias=vec(b1, ft))
                    if positive(f):
                        if ft < FT - 1:
                            act.wait_ge(n["down_ft"], (FT - 1) * f + (ft + 2 - FT))
                        else:
                            act.wait_ge(n["down_full"], 2 * f)
                    a.activation(HH[:, ft, :], bank[UP_BANK + ft % 2], func, bias=vec(b1, ft)).then_inc(n["h_hi"], 1)
                    if isinstance(f, int) and f == 0:
                        tail_hook(ft)
                    if with_s5 and ft == 2:
                        for k in range(KT):
                            act.wait_ge(s5["t_full"], 2 * j + (k + 1))
                            a.activation(XNF2[:, k, :], bank[T_BANK + k], ACT.Identity, bias=ab(2, 1, k, j),
                                         scale=ab(2, 0, k, j)).then_inc(s5["xnf"], 1)
                    if with_s5 and ft == 3:
                        act.wait_ge(s5["wgf"], 4 * j + 4)
                        a.activation(WG[:, 0, :, :], WGF[:, :, :], ACT.Copy).then_inc(s5["wg_hi"], 1)
                        a.activation(DGP[:, 0, :, :], DGF[:, :, :], ACT.Copy).then_inc(s5["wg_hi"], 1)
                    if with_s5 and ft == 5:
                        for m in range(2):
                            act.wait_ge(s5["cyf"], 2 * j + (m + 1))
                            a.activation(CYP[:, m, 0, :], CYF[:, m, :], ACT.Copy).then_inc(s5["cy_hi"], 1)
                    if with_next and ft == (7 if with_s5 else 5):
                        xnf_out(f + 1, 1 if new_layer else layer)
                if new_layer:
                    act.wait_ge(s_raw1, 32)
                    act.wait_ge(n["up_full"], FT * B)
                    for c in range(W_CHUNKS):
                        at = slice(c * WN * P, (c + 1) * WN * P)
                        a.activation(W1P[:, 0, :, at], RAW1.rearrange("p (k n) -> p k n", k=KT)[:, :, at], ACT.Copy)\
                            .then_inc(n["w1_hi"], 1)
                if new_layer:
                    act.wait_ge(n["down_full"], 2 * B)
                    for c in range(W_CHUNKS):
                        at = slice(c * WN, (c + 1) * WN)
                        a.activation(W2P[:, 0, at, :], RAW2.rearrange("p (f n) -> p f n", f=FT)[:, at, :], ACT.Copy)\
                            .then_inc(n["w2_hi"], 1)
                if isinstance(f, int) and f == 0:
                    act.wait_ge(s5["bb_t"], 1)
                    a.activation(BBT[:, :, :], MISC.rearrange("p (m n) -> p m n", m=4), ACT.Copy)\
                        .then_inc(s5["bbt"], 1)
                    act.wait_ge(s5["bbt"], 1)
                    a.activation(WB[:, 0, :, :], BBT[:, :, :], ACT.Copy).then_inc(s5["wb_hi"], 1)

            ffn_frames(act, ffn_frame)

        @block.vector
        def _(dve):
            v = nc.vector
            dve.wait_ge(s_x[0], 16)
            ln_stats_dve(dve, LN_ATT, 0)

            def mt_out(j):
                t0, t1, from_bank = MT_PARTS[j]
                dve.wait_ge(mt_mm, j + 1)
                v.tensor_tensor(MT[:, t0:t1, :], from_bank[:, t0 * B:t1 * B].rearrange("p (t b) -> p t b", b=B),
                                VEC_SB[:, VEC["bmod"][0] + t0:VEC["bmod"][0] + t1].unsqueeze(2)
                                .to_broadcast([P, t1 - t0, B]), ALU.add).then_inc(mt_ready, 1)

            ln_xhat_dve(dve, LN_ATT, 0)
            dve.wait_ge(s_small, 32)
            mt_out(0)
            dve.wait_ge(wq_hi, 1)
            v.tensor_tensor(WQ[:, 1536:3072], WRAW[:, 0:1536], WQ[:, 0:1536].bitcast(F32), ALU.subtract)\
                .then_inc(wq_lo, 1)

            def turn(t, what, b, i):
                at_bank = turn_bank(t)
                if what == "LT":
                    dve.wait_ge(misc_free, t + 1)
                    xn_split_dve(dve, b, i, XNF, xn_part, xn_hi, xn_ready)
                    return
                dve.wait_ge(misc_full, t + 1)
                if what in ("Q", "K"):
                    src, bias, second = (SRCQ, "bq", 0) if what == "Q" else (SRCK, "bk", 1)
                    dve.wait_ge(src_hi, 4 * b + (2 * i + second + 1))
                    v.scalar_tensor_tensor(src[:, i, 1, :], at_bank, vec(bias, i), src[:, i, 0, :].bitcast(F32),
                                           ALU.add, ALU.subtract).then_inc(misc_free, 1)
                if what == "V":
                    if positive(b):
                        dve.wait_ge(va_ready, 2 * b)
                    v.tensor_tensor(VS[:, 2 * i:2 * i + 2, :], at_bank.rearrange("p (a n) -> p a n", a=2),
                                    BV[:, :].unsqueeze(1).to_broadcast([P, 2, D]), ALU.add).then_inc(misc_free, 1)
                if what == "MX":
                    dve.wait_ge(mx_hi, QUADS * b + (i + 1))
                    v.scalar_tensor_tensor(NEGMX[:, i, 1, :], at_bank[0:16, 0:P], -1.0,
                                           NEGMX[:, i, 0, :].bitcast(F32), ALU.mult, ALU.subtract)\
                        .then_inc(misc_free, 1)
                if what == "OT":
                    o = at_bank.rearrange("p (t j c) -> p t j c", t=TT, j=4)
                    v.reciprocal(RC[:, :].rearrange("p (t j) -> p t j", t=TT), o[:, :, :, HD]).then_inc(rc_ready, 1)
                    dve.wait_ge(rc_ready, QUADS * b + (i + 1))
                    v.tensor_tensor(OTK[:, :, 64 * i:64 * i + 64].rearrange("p t (j d) -> p t j d", j=4),
                                    o[:, :, :, 0:HD],
                                    RC[:, :].rearrange("p (t j) -> p t j", t=TT).unsqueeze(3)
                                    .to_broadcast([P, TT, 4, HD]), ALU.mult).then_inc(misc_free, 1)
                if what == "WO":
                    dve.wait_ge(x_bias, b + 1)
                    v.tensor_tensor(x_pair(b, i), x_pair(b, i), at_bank.rearrange("p (a n) -> p a n", a=2), ALU.add)\
                        .then_inc(misc_free, 1)

            turn(0, "LT", 0, 0)
            turn(1, "LT", 0, 1)
            turn(2, "Q", 0, 0)
            turn(3, "K", 0, 0)
            dve.wait_ge(s_rows, 80)

            def row_max(b, s, half):
                n = 32 * b + (2 * s + half)
                dve.wait_ge(s1_full, n + 1)
                v.reduce_max(MX[:, (s // 4) % 2, s % 4, 2 * half:2 * half + 2], PS1[:, 2 * half:2 * half + 2, :],
                             AX_X).then_inc(s1_free, 1)

            def copy_hi(to, raw):
                return v.tensor_copy(to, raw)

            def lo_of(to, raw, hi):
                return v.tensor_tensor(to, raw, hi.bitcast(F32), ALU.subtract)

            def w1_lo(layer, raw, with_hi):
                for c in range(W_CHUNKS):
                    at, k_n = slice(c * WN * P, (c + 1) * WN * P), raw.rearrange("p (k n) -> p k n", k=KT)
                    if with_hi:
                        copy_hi(W1P[:, 0, :, at], k_n[:, :, at]).then_inc(ffn["w1_hi"], 1)
                    dve.wait_ge(ffn["w1_hi"], W_CHUNKS * layer + c + 1)
                    lo_of(W1P[:, 1, :, at], k_n[:, :, at], W1P[:, 0, :, at]).then_inc(ffn["w1_lo"], 1)

            def w2_lo(layer, raw, with_hi):
                for c in range(W_CHUNKS):
                    at, f_n = slice(c * WN, (c + 1) * WN), raw.rearrange("p (f n) -> p f n", f=FT)
                    if with_hi:
                        copy_hi(W2P[:, 0, at, :], f_n[:, at, :]).then_inc(ffn["w2_hi"], 1)
                    dve.wait_ge(ffn["w2_hi"], W_CHUNKS * layer + c + 1)
                    lo_of(W2P[:, 1, at, :], f_n[:, at, :], W2P[:, 0, at, :]).then_inc(ffn["w2_lo"], 1)

            def xn_split(f):
                for k in range(KT):
                    dve.wait_ge(ffn["xnf"], 2 * f + (k + 1))
                    xn_split_dve(dve, f + B, k, XNF, xn_part, xn_hi, xn_ready)

            def frame(b, kind):
                turns = numbered(b, kind)
                for s in range(16 if kind != "tail" else LAG + 1):
                    if kind != "tail":
                        row_max(b, s, 0)
                    for one in turns[s][0:1]:
                        turn(*one)
                    if kind in ("first", "middle") and s == 1:
                        ln_xhat_dve(dve, b + (LN_ATT + 1), b + 1)
                    if kind != "tail":
                        row_max(b, s, 1)
                    for one in turns[s][1:]:
                        turn(*one)
                    if kind == "first" and s == 0:
                        for j in range(1, len(MT_PARTS)):
                            mt_out(j)
                    if kind in ("first", "middle") and s == 0:
                        if kind == "first":
                            dve.wait_ge(s_x[1], 16)
                            dve.wait_ge(s_x[2], 16)
                            dve.wait_ge(s_x[3], 16)
                        ln_stats_dve(dve, b + (LN_ATT + 1), b + 1)
                    if kind == "tail" and s == 0:
                        dve.wait_ge(misc_free, turn_base(B))
                        ln_stats_dve(dve, LN_FFN, 0)
                        dve.wait_ge(s_w1raw, 16)
                        dve.wait_ge(exp_done, 64 * (B - 1) + 32)
                        w1_lo(0, WRAW[:, :], True)
                        ln_xhat_dve(dve, LN_FFN, 0)
                    if kind == "tail" and s == 3:
                        xn_split(0)

            frame(0, "first")
            with dve.Fori(1, B - 1) as b:
                frame(b, "middle")
            frame(B - 1, "last")
            frame(B, "tail")
            dve.wait_ge(s_w2raw, 16)
            w2_lo(0, WRAW[:, :], True)

            TAIL = numbered(B, "tail")
            mag = SC[:, MAG_COL:MAG_COL + 1]

            def tail_hook(ft):
                for one in TAIL[LAG + 1 + ft] if ft < 5 else []:
                    turn(*one)
                if ft == 5:
                    dve.wait_ge(misc_free, ALL_TURNS)

            def s5_step(f, ft):
                j = f - 1
                if ft == 0:
                    dve.wait_ge(ffn["t_full"], 2 * f + 2)
                    ln_xhat_dve(dve, norm_s5(f), j)
                if ft == 2:
                    for k in range(KT):
                        dve.wait_ge(s5["xnf"], 2 * j + (k + 1))
                        xn_split_dve(dve, j, k, XNF2, xn2_part, s5["xn_hi"], s5["xn_ready"])
                if ft == 4:
                    dve.wait_ge(s5["bu_full"], 2 * j + 1)
                    v.tensor_tensor(T1, bank[S5_BANK], TAB_C, ALU.mult).then_inc(s5["t1"], 1)
                    dve.wait_ge(s5["bu_full"], 2 * j + 2)
                    v.tensor_tensor(T2, bank[S5_BANK + 1], TAB_S, ALU.mult).then_inc(s5["t2"], 1)
                    dve.wait_ge(s5["wg_hi"], 2 * j + 2)
                    lo_of(WG[:, 1, :, :], WGF[:, :, :], WG[:, 0, :, :]).then_inc(s5["wg_lo"], 1)
                    lo_of(DGP[:, 1, :, :], DGF[:, :, :], DGP[:, 0, :, :]).then_inc(s5["wg_lo"], 1)
                if ft == 5:
                    dve.wait_ge(s5["rot"], j + 1)
                    v.tensor_tensor_scan(STATE, mag.to_broadcast([P, S]), ROT, 0.0, ALU.mult, ALU.add)\
                        .then_inc(s5["scan"], 1)
                    dve.wait_ge(s5["scan"], j + 1)
                    v.tensor_tensor(CYF[:, 0, :], STATE, TAB_C, ALU.mult).then_inc(s5["cyf"], 1)
                    v.tensor_tensor(CYF[:, 1, :], STATE, TAB_S, ALU.mult).then_inc(s5["cyf"], 1)
                if ft == 6:
                    for m in range(2):
                        dve.wait_ge(s5["cy_hi"], 2 * j + (m + 1))
                        lo_of(CYP[:, m, 1, :], CYF[:, m, :], CYP[:, m, 0, :]).then_inc(s5["cy_lo"], 1)

            def residual(f, layer):
                b = ffn_batch(f, layer)
                dve.wait_ge(x_bias, f + (B + 1))
                for p in range(2):
                    dve.wait_ge(ffn["down_full"], 2 * f + (p + 1))
                    product = bank[DOWN_BANK + p].rearrange("p (a n) -> p a n", a=2)
                    if layer == 1:
                        v.tensor_tensor(TMP[:, p, :, :], product, GATE_F[:, bass.ds(b, 1), :].to_broadcast([P, 2, D]),
                                        ALU.mult).then_inc(ffn["gated"], 1)
                        dve.wait_ge(ffn["gated"], 2 * b + (p + 1))
                        product = TMP[:, p, :, :]
                    v.tensor_tensor(x_pair(b, p), x_pair(b, p), product, ALU.add).then_inc(ffn["down_free"], 1)

            def ffn_frame(f, layer, with_s5, with_next, next_s5):
                for ft in range(FT):
                    if isinstance(f, int) and f == 0 and ft == 0:
                        tail_hook(0)
                    dve.wait_ge(ffn["h_hi"], FT * f + (ft + 1))
                    lo_of(HL[:, ft, :], HF[:, ft % 2, :], HH[:, ft, :]).then_inc(ffn["h_lo"], 1)
                    if isinstance(f, int) and f == 0 and ft > 0:
                        tail_hook(ft)
                    if with_s5:
                        s5_step(f, ft)
                    if with_next and ft == 1:
                        next_layer = 1 if layer == 1 or (isinstance(f, int) and f == B - 1) else 0
                        if next_layer == 1:
                            alone(dve, s5["out_free"], 2 * f + 2 * (2 - B))
                        ln_stats_dve(dve, norm_next(f, with_s5), ffn_batch(f + 1, next_layer))
                    if with_next and ft == 3:
                        if with_s5:
                            dve.wait_ge(s5["t_full"], 2 * f)
                        else:
                            dve.wait_ge(ffn["t_full"], 2 * f + 2)
                        ln_xhat_dve(dve, norm_next(f, with_s5), ffn_batch(f + 1, next_layer))
                if with_next:
                    xn_split(f + 1)
                new_layer = isinstance(f, int) and f == B - 1
                if new_layer:
                    w1_lo(1, RAW1, False)
                residual(f, layer)
                if next_s5:
                    alone(dve, ffn["down_free"], 2 * f + 2)
                    ln_stats_dve(dve, norm_s5(f + 1), f)
                if with_s5:
                    j = f - 1
                    for p in range(2):
                        dve.wait_ge(s5["out_full"], 2 * j + (p + 1))
                        v.tensor_tensor(x_pair(j, p), x_pair(j, p),
                                        bank[S5_BANK + p].rearrange("p (a n) -> p a n", a=2), ALU.add)\
                            .then_inc(s5["out_free"], 1)
                if new_layer:
                    w2_lo(1, RAW2, False)
                if isinstance(f, int) and f == 0:
                    dve.wait_ge(s5["wb_hi"], 1)
                    lo_of(WB[:, 1, :, :], BBT[:, :, :], WB[:, 0, :, :]).then_inc(s5["wb_lo"], 1)
                    dve.wait_ge(s5_tables, 1)

            ffn_frames(dve, ffn_frame)

        @block.tensor
        def _(pe):
            def mm(out_, lhsT, rhs, start, stop):
                return nc.tensor.matmul(out_, lhsT, rhs, start=start, stop=stop, skip_group_check=True)

            PARTS = ((0, 0), (0, 1), (1, 0))

            def parts(out_, pairs, start=True, stop=True):
                n = 0
                for left, right in pairs:
                    for p, q in PARTS:
                        op = mm(out_, left(p), right(q), start and n == 0, stop and n == 3 * len(pairs) - 1)
                        n += 1
                return op

            def mt_products():
                t0, t1, into = MT_PARTS[0]
                for t in range(t0, t1):
                    for k in range(KT):
                        op = mm(into[:, t * B:(t + 1) * B], WMOD[:, k, t * P:(t + 1) * P], COND[:, k, :],
                                k == 0, k == KT - 1)
                op.then_inc(mt_mm, 1)

            def mrow_products():
                for k in range(KT):
                    for c in range(CHUNKS):
                        at = MT_FIRST * P + 512 * c
                        op = mm(bank[4 + c % 2][32 * (c // 2):32 * (c // 2) + B, :], COND[:, k, :],
                                WMOD[:, k, at:at + 512], k == 0, k == KT - 1)
                op.then_inc(mrow_mm, 1)

            def mt_transposes(j):
                t0, t1, into = MT_PARTS[j]
                rows = slice(32 * (j - 1), 32 * (j - 1) + B)
                for t in range(t0, t1):
                    c = (t - MT_FIRST) // 4
                    op = nc.tensor.transpose(into[:, t * B:(t + 1) * B],
                                             MROW[rows, c % 2, P * (t % 4):P * (t % 4 + 1)], IDENT[rows, rows])
                op.then_inc(mt_mm, 1)

            pe.wait_ge(s_small, 32)
            pe.wait_ge(s_wmod_a, 16)
            mt_products()
            pe.wait_ge(ident_ready, 1)

            def turn(t, what, b, i):
                at_bank = turn_bank(t)
                if isinstance(t, int) and t == 3:
                    pe.wait_ge(misc_free, 1)
                elif not (isinstance(t, int) and t < 3):
                    pe.wait_ge(misc_free, t)
                if what == "LT":
                    op = ln_transpose_pe(pe, b + LN_ATT, i, at_bank)
                if what in ("Q", "K"):
                    pe.wait_ge(xn_ready, 2 * b + 2)
                    c0 = (0 if what == "Q" else D) + P * i
                    op = parts(at_bank, [(lambda p, k=k: WQV[:, p, k, c0:c0 + P], lambda q, k=k: XN[:, q, k, :])
                                      for k in range(KT)])
                if what == "V":
                    for one in range(2):
                        at = (2 * i + one) * P
                        op = parts(at_bank[:, D * one:D * (one + 1)],
                                   [(lambda p, k=k, at=at: XN[:, p, k, at:at + P],
                                     lambda q, k=k: WQV[:, q, k, 2 * D:3 * D]) for k in range(KT)])
                if what == "MX":
                    pe.wait_ge(s1_free, 32 * b + 8 * (i + 1))
                    op = nc.tensor.transpose(at_bank[0:16, 0:P], MX[:, i % 2, :, :].rearrange("p j t -> p (j t)"),
                                             IDENT[:, :])
                if what == "OT":
                    pe.wait_ge(pv_evac, QUADS * b + (i + 1))
                    for qt in range(TT):
                        op = nc.tensor.transpose(at_bank[:, qt * P:(qt + 1) * P], OR[:, i % 2, qt * P:(qt + 1) * P],
                                                 IDENT[:, :])
                if what == "OB":
                    for qt in range(TT):
                        op = nc.tensor.transpose(at_bank[:, qt * P:(qt + 1) * P], OTK[:, qt, i * P:(i + 1) * P],
                                                 IDENT[:, :])
                if what == "WO":
                    pe.wait_ge(s_rows, 80)
                    for one in range(2):
                        at = (2 * i + one) * P
                        for k in range(KT):
                            op = mm(at_bank[:, D * one:D * (one + 1)], OF[:, k, at:at + P], WO[:, k, :],
                                    k == 0, k == KT - 1)
                op.then_inc(misc_full, 1)

            turn(0, "LT", 0, 0)
            turn(1, "LT", 0, 1)
            pe.wait_ge(wq_lo, 1)
            turn(2, "Q", 0, 0)
            turn(3, "K", 0, 0)
            pe.wait_ge(misc_free, 3)
            pe.wait_ge(s_wmod_b, 16)
            mrow_products()

            def gate_product(i):
                _, _, tile, b, into = GATES[i]
                if i == 3:
                    pe.wait_ge(gate_out, 1)
                for one in range(2):
                    for k in range(KT):
                        op = mm(into[:, D * one:D * (one + 1)],
                                COND[:, k, b + one:b + one + 1].to_broadcast([P, P]),
                                WMOD[:, k, tile * P:tile * P + D], k == 0, k == KT - 1)
                op.then_inc(gate_mm, 1)


            def scores_for_max(b, s, half):
                n = 32 * b + (2 * s + half)
                if half == 0:
                    pe.wait_ge(stack_ready[s], 64 * b + 64)
                if positive(b) or 2 * s + half >= 2:
                    pe.wait_ge(s1_free, n - 1)
                for one in range(2):
                    qt = 2 * half + one
                    op = mm(bank[qt], QS[0:P1_ROWS, s, qt * P:(qt + 1) * P], KS[0:P1_ROWS, s, :], True, True)
                op.then_inc(s1_full, 1)

            def scores_less_max(b, s, j):
                g = 16 * b + (s - LAG)
                q, kt = ((s - LAG) // 4) % 4, (s - LAG) % 4
                h = 4 * q + j
                if kt == 0 and j == 0:
                    pe.wait_ge(negmax_ready[q], 32 * b + (32 if s >= LAG else 0))
                if not (isinstance(g, int) and g == 0 and j < 2):
                    pe.wait_ge(exp_done, 4 * g + (j - 1))
                mm(bank[4 + j % 2], KS[0:P2_ROWS, h, kt * P:(kt + 1) * P], QS[0:P2_ROWS, h, :], True, True)\
                    .then_inc(s2_full, 1)

            def values(b, s):
                g = 16 * b + (s - LAG - 1)
                q, kt = ((s - LAG - 1) // 4) % 4, (s - LAG - 1) % 4
                o = q // 2
                if kt == 0:
                    if not (isinstance(g, int) and g == 0):
                        pe.wait_ge(pv_evac, QUADS * b + ((s - LAG - 1) // 4))
                    pe.wait_ge(va_ready, 2 * b + (o + 1 if s > LAG else o - 1))
                pe.wait_ge(exp_done, 4 * g + 4)
                for j in range(4):
                    op = mm(PV[32 * j:32 * (j + 1), :], VA[:, o, kt, 4 * (q % 2) + j, :], PTV[:, kt, j, :],
                            kt == 0, kt == TT - 1)
                op.then_inc(pv_done, 1)

            def up(f, layer, ft):
                if isinstance(f, int) and f == 0 and ft == 0:
                    pe.wait_ge(xn_ready, 2 * B + 2)
                if isinstance(f, int) and f % B == 0 and ft % WN == 0:
                    pe.wait_ge(ffn["w1_lo"], W_CHUNKS * layer + ft // WN + 1)
                if positive(f) or ft >= 2:
                    pe.wait_ge(ffn["h_hi"], FT * f + (ft - 1))
                parts(bank[UP_BANK + ft % 2], [(lambda p, k=k: W1P[:, p, k, ft * P:(ft + 1) * P],
                                                lambda q, k=k: XN[:, q, k, :]) for k in range(KT)])\
                    .then_inc(ffn["up_full"], 1)

            def transpose_norm(n, full):
                for k in range(KT):
                    ln_transpose_pe(pe, n, k, bank[T_BANK + k]).then_inc(full, 1)

            def frame(b, kind):
                turns = numbered(b, kind)
                for s in range(16 if kind != "tail" else LAG + 1):
                    has_p1 = kind != "tail"
                    has_p2 = (kind != "first" or s >= LAG) and (kind != "tail" or s < LAG)
                    has_pv = (kind != "first" or s > LAG) and (kind != "tail" or s <= LAG)
                    turn_first = kind == "first" and s == 0
                    if turn_first:
                        turn(*turns[s][0])
                        pe.wait_ge(s_const_rows, 64)
                    if has_p2:
                        scores_less_max(b, s, 0)
                    if has_p1:
                        scores_for_max(b, s, 0)
                    if has_p2:
                        scores_less_max(b, s, 1)
                    for one in turns[s][0:1] if not turn_first else []:
                        turn(*one)
                    if has_p2:
                        scores_less_max(b, s, 2)
                    if has_p1:
                        scores_for_max(b, s, 1)
                    if has_p2:
                        scores_less_max(b, s, 3)
                    if kind == "first" and s == 0:
                        pe.wait_ge(mrow_out, 1)
                        for j in range(1, len(MT_PARTS)):
                            mt_transposes(j)
                    if kind == "first" and 1 <= s <= len(GATES):
                        if s == 1:
                            pe.wait_ge(mt_ready, len(MT_PARTS))
                        gate_product(s - 1)
                    if kind == "tail" and s >= LAG - 1:
                        up(0, 0, s - (LAG - 1))
                    if has_pv:
                        values(b, s)
                    for one in turns[s][1:]:
                        turn(*one)
                    if kind == "tail" and s == 2:
                        pe.wait_ge(s1_free, 2 * H * B)
                        transpose_norm(LN_FFN, ffn["t_full"])

            frame(0, "first")
            with pe.Fori(1, B - 1) as b:
                frame(b, "middle")
            frame(B - 1, "last")
            frame(B, "tail")

            TAIL = numbered(B, "tail")
            pe.wait_ge(exp_done, 4 * H * B)

            def down(f, layer, ft):
                if isinstance(f, int) and f % B == 0 and ft % WN == 0:
                    pe.wait_ge(ffn["w2_lo"], W_CHUNKS * layer + ft // WN + 1)
                pe.wait_ge(ffn["h_lo"], FT * f + (ft + 1))
                for tt in range(TT):
                    p, one = tt // 2, tt % 2
                    if ft == 0 and one == 0 and positive(f):
                        pe.wait_ge(ffn["down_free"], 2 * f + (p - 1))
                    op = parts(bank[DOWN_BANK + p][:, D * one:D * (one + 1)],
                               [(lambda q: (HH, HL)[q][:, ft, tt * P:(tt + 1) * P], lambda q: W2P[:, q, ft, :])],
                               start=ft == 0 and one == 0, stop=ft == FT - 1)
                    if ft == FT - 1 and one == 1:
                        op.then_inc(ffn["down_full"], 1)
                if ft < FT - 1:
                    op.then_inc(ffn["down_ft"], 1)

            def s5_inputs_pe(j):
                pe.wait_ge(s5["wb_lo"], 1)
                pe.wait_ge(s5["xn_ready"], 2 * j + 2)
                for m in range(2):
                    parts(bank[S5_BANK + m], [(lambda p, k=k: WB[:, p, 2 * m + k, :], lambda q, k=k: XN2[:, k, q, :])
                                              for k in range(KT)]).then_inc(s5["bu_full"], 1)

            def s5_outputs_pe(j):
                pe.wait_ge(s5["wg_lo"], 2 * j + 2)
                pe.wait_ge(s5["cy_lo"], 2 * j + 2)
                for tt in range(TT):
                    at, into = slice(tt * P, (tt + 1) * P), bank[S5_BANK + tt // 2]
                    c0 = D * (tt % 2)
                    parts(into[:, c0:c0 + D], [(lambda p, m=m: CYP[:, m, p, at], lambda q, m=m: WG[:, q, m, :])
                                               for m in range(2)], stop=False)
                    for k in range(KT):
                        op = parts(into[:, c0 + k * P:c0 + (k + 1) * P],
                                   [(lambda p: XN2[:, k, p, at], lambda q: DGP[:, q, k, :])],
                                   start=False, stop=k == KT - 1)
                    if tt % 2 == 1:
                        op.then_inc(s5["out_full"], 1)

            def ffn_frame(f, layer, with_s5, with_next, next_s5):
                if positive(f):
                    pe.wait_ge(xn_ready, 2 * f + (2 * B + 2))
                for ft in range(FT):
                    if positive(f) or ft >= 2:
                        up(f, layer, ft)
                    if with_s5 and ft == 4:
                        s5_inputs_pe(f - 1)
                    if ft >= 2:
                        down(f, layer, ft - 2)
                    if isinstance(f, int) and f == 0:
                        for one in TAIL[LAG + 1 + ft] if ft < 5 else []:
                            turn(*one)
                    if with_s5 and ft == 2:
                        transpose_norm(norm_s5(f), s5["t_full"])
                    if with_next and ft == 5:
                        transpose_norm(norm_next(f, with_s5), ffn["t_full"])
                down(f, layer, FT - 2)
                down(f, layer, FT - 1)
                if with_s5:
                    s5_outputs_pe(f - 1)
                if isinstance(f, int) and f == 0:
                    pe.wait_ge(s5_inputs, 1)
                    for m in range(2):
                        for k in range(KT):
                            op = nc.tensor.transpose(MISC[:, (2 * m + k) * P:(2 * m + k + 1) * P],
                                                     BB[:, m, k * P:(k + 1) * P], IDENT[:, :])
                    op.then_inc(s5["bb_t"], 1)

            ffn_frames(pe, ffn_frame)


_ORDER = ["x", "vecs", "cond", "wmod", "bgate", "wqkv", "bv", "wo", "bo", "w1_0", "w2_0", "b2_0",
          "b_st", "b_sw", "c_st", "c_sw", "w1_1", "w2_1", "b2_1"]


def kernel(**inputs):
    import numpy as np
    import concourse.bacc as bacc
    from concourse.bass_utils import run_bass_kernel_spmd

    a = {k: np.asarray(v) for k, v in inputs.items()}
    L0, L1 = "L0_cond_", "L1_cond_"

    def feature_tiles(m):
        return np.ascontiguousarray(m.reshape(m.shape[0] // P, P, m.shape[1]).transpose(1, 0, 2))

    def columns(v):
        return v.reshape(-1, P).T

    def twice(v):
        return np.concatenate([v, v])

    bmod = np.concatenate([a[L0 + "bt_attn"], a[L0 + "bt_ffn"], a[L1 + "bm"], a[L1 + "bc"]])
    vectors = {"ln1_w": a[L0 + "ln1_w"], "ln1_b": a[L0 + "ln1_b"], "ln2_w": a[L0 + "ln2_w"], "ln2_b": a[L0 + "ln2_b"],
               "bq": a[L0 + "bq"], "bk": a[L0 + "bk"], "bmod": bmod, "b1_0": a[L0 + "b1"], "b1_1": a[L1 + "b1"],
               "d_diag": a[L1 + "D_diag"], "lam_re": twice(a[L1 + "Lam_re"]), "lam_im": twice(a[L1 + "Lam_im"]),
               "log_step": twice(a[L1 + "log_step"])}
    laid = {
        "x": a["x"],
        "vecs": np.concatenate([columns(vectors[name]) for name, _ in VEC_SIZES], axis=1),
        "cond": feature_tiles(a["cond_1024"].T),
        "wmod": feature_tiles(np.concatenate([a[L0 + "wt_attn"], a[L0 + "wt_ffn"], a[L1 + "Wm"], a[L1 + "Wc"]],
                                             axis=1)),
        "bgate": np.stack([a[L1 + "bm"][2 * D:3 * D], a[L1 + "bm"][5 * D:6 * D]]),
        "wqkv": feature_tiles(np.concatenate([a[L0 + "wq"], a[L0 + "wk"], a[L0 + "wv"]], axis=1)).reshape(P, -1),
        "bv": a[L0 + "bv"],
        "wo": feature_tiles(a[L0 + "wo"]),
        "bo": a[L0 + "bo"],
        "w1_0": feature_tiles(a[L0 + "w1"]).reshape(P, -1),
        "w2_0": feature_tiles(a[L0 + "w2"]).reshape(P, -1),
        "b2_0": a[L0 + "b2"],
        "b_st": np.concatenate([a[L1 + "B_re"], a[L1 + "B_im"]]),
        "b_sw": np.concatenate([a[L1 + "B_im"], a[L1 + "B_re"]]),
        "c_st": np.concatenate([a[L1 + "C_re"].T, a[L1 + "C_im"].T]),
        "c_sw": np.concatenate([a[L1 + "C_im"].T, a[L1 + "C_re"].T]),
        "w1_1": feature_tiles(a[L1 + "W1"]).reshape(P, -1),
        "w2_1": feature_tiles(a[L1 + "W2"]).reshape(P, -1),
        "b2_1": a[L1 + "b2"],
    }
    nc = bacc.Bacc("TRN2", target_bir_lowering=False, num_devices=1, dynamic_dma_scratch_size=4096)
    arrays, args = {}, []
    for name in _ORDER:
        arrays["in_" + name] = np.ascontiguousarray(laid[name])
        args.append(nc.dram_tensor("in_" + name, laid[name].shape, F32, kind="ExternalInput").ap())
    out = nc.dram_tensor("out_y", (B, S, D), F32, kind="ExternalOutput").ap()
    cond_seq_kernel(nc, *args, out)
    r = run_bass_kernel_spmd(nc, [arrays], core_ids=[0])
    return r.results[0]["out_y"]
```
